# Optimizing a Trainium2 kernel written in Bass

```python
import numpy as np
import jax
import jax.numpy as jnp

def _softmax(x, axis=-1):
    return jax.nn.softmax(x, axis=axis)

def _gelu(x):
    return jax.nn.gelu(x, approximate=True)

def _silu(x):
    return jax.nn.silu(x)

def _sigmoid(x):
    return jax.nn.sigmoid(x)

def _layernorm(x, axis=-1, eps=1e-05):
    m = jnp.mean(x, axis=axis, keepdims=True)
    v = jnp.var(x, axis=axis, keepdims=True)
    return (x - m) / jnp.sqrt(v + eps)

def _scatter_add(tgt, idx, src, axis=0):
    return tgt.at[idx].add(src)

def _segment_sum(src, seg, n):
    return jax.ops.segment_sum(src, seg, n)
kernel_name = 'mk_flamingo_gated_d2_seqx_r4_02cdb5'

def setup_inputs(seed: int=0):
    np.random.seed(seed)
    _w = jnp.asarray

    def _rec_inputs():
        import jax
        import jax.numpy as jnp
        _rk = jax.random.key(seed)
        x = -0.0002928 + 1 * jax.random.normal(jax.random.fold_in(_rk, 1), (16, 256, 256), jnp.float32)
        _lenS = 256 - jax.random.randint(jax.random.fold_in(_rk, 7), (16,), 0, max(1, 256 // 4) + 1, jnp.int32)
        _lenS2 = 256 - jax.random.randint(jax.random.fold_in(_rk, 8), (16,), 0, max(1, 256 // 4) + 1, jnp.int32)
        _ctx_1024P = jax.random.normal(jax.random.fold_in(_rk, 11), (16, 16, 256), jnp.float32)
        _ctx_1024c = jax.random.dirichlet(jax.random.fold_in(_rk, 511), 0.3 * jnp.ones((16,), jnp.float32), (16, 256))
        _ctx_1024t = jnp.einsum('bsk,bkd->bsd', _ctx_1024c, _ctx_1024P)
        _ctx_1024t = _ctx_1024t * jax.lax.rsqrt(jnp.mean(jnp.square(_ctx_1024t)) + 1e-12) * 0.953939
        ctx_1024 = -1.39393e-06 + 0.999914 * (_ctx_1024t + 0.3 * jax.random.normal(jax.random.fold_in(_rk, 611), (16, 256, 256), jnp.float32))
        _validS = jnp.arange(256)[None, :] < _lenS[:, None]
        _validS2 = jnp.arange(256)[None, :] < _lenS2[:, None]
        _causal = jnp.tril(jnp.ones((256, 256), dtype=bool))
        mask_B_ik0 = jnp.where(jnp.ones((16,), dtype=bool), 69, 391).astype(jnp.int32)
        _g = jax.random.normal(jax.random.fold_in(_rk, 9001), (2, 2), jnp.float32)
        _g = jnp.sign(_g) * jnp.maximum(jnp.abs(_g), 1.0) + (_g == 0) * 1.0
        g_xattn = _g[0]
        g_ffn = _g[1]
        return (x, ctx_1024, mask_B_ik0, g_xattn, g_ffn)
    x, ctx_1024, mask_B_ik0, g_xattn, g_ffn = _rec_inputs()

    def _L0_xattn_setup():
        import jax, jax.numpy as jnp
        import numpy as np
        EMBED_PHI = 256
        EMBED_F = 256
        HIDDEN_F = 256
        N_HEADS = 16
        B, S = (2, 512)
        key = jax.random.key(seed)
        ks = jax.random.split(key, 9)
        sphi = 1.0 / np.sqrt(EMBED_PHI)
        sf = 1.0 / np.sqrt(EMBED_F)
        sh = 1.0 / np.sqrt(HIDDEN_F)
        return {'q': jax.random.normal(ks[0], (B, S, EMBED_PHI), jnp.float32), 'k': jax.random.normal(ks[1], (B, S, EMBED_PHI), jnp.float32), 'v': jax.random.normal(ks[2], (B, S, EMBED_F), jnp.float32), 'Wq': jax.random.normal(ks[3], (HIDDEN_F, EMBED_PHI), jnp.float32) * sphi, 'Wk': jax.random.normal(ks[4], (HIDDEN_F, EMBED_PHI), jnp.float32) * sphi, 'Wv': jax.random.normal(ks[5], (HIDDEN_F, EMBED_F), jnp.float32) * sf, 'bv': jax.random.normal(ks[6], (HIDDEN_F,), jnp.float32) * sf, 'Wo': jax.random.normal(ks[7], (EMBED_F, HIDDEN_F), jnp.float32) * sh, 'bo': jax.random.normal(ks[8], (EMBED_F,), jnp.float32) * sh}
    _L0_xattn_all = _L0_xattn_setup()
    _L0_xattn_in = {k: v for k, v in _L0_xattn_all.items() if k in ('Wq', 'Wk', 'Wv', 'bv', 'Wo', 'bo')}
    del _L0_xattn_all

    def _L0_ffn_setup():
        import jax, jax.numpy as jnp
        import numpy as np
        D_MODEL = 256
        HIDDEN = 256
        NUM_EXPERTS = 8
        TOP_K = 2
        key = jax.random.key(seed)
        ks = jax.random.split(key, 10)
        s = 0.02
        return {'x': jax.random.normal(ks[0], (2, 512, D_MODEL), dtype=jnp.float32), 'gate_w': jax.random.normal(ks[1], (NUM_EXPERTS, D_MODEL), dtype=jnp.float32) * s, 'up_w': jax.random.normal(ks[2], (NUM_EXPERTS, D_MODEL, HIDDEN), dtype=jnp.float32) * s, 'up_b': jnp.zeros((NUM_EXPERTS, HIDDEN), dtype=jnp.float32), 'down_w': jax.random.normal(ks[3], (NUM_EXPERTS, HIDDEN, D_MODEL), dtype=jnp.float32) * s, 'down_b': jnp.zeros((NUM_EXPERTS, D_MODEL), dtype=jnp.float32), 'sh_up_w': jax.random.normal(ks[4], (D_MODEL, HIDDEN), dtype=jnp.float32) * s, 'sh_up_b': jnp.zeros((HIDDEN,), dtype=jnp.float32), 'sh_down_w': jax.random.normal(ks[5], (HIDDEN, D_MODEL), dtype=jnp.float32) * s, 'sh_down_b': jnp.zeros((D_MODEL,), dtype=jnp.float32)}
    _L0_ffn_all = _L0_ffn_setup()
    _L0_ffn_in = {k: v for k, v in _L0_ffn_all.items() if k in ('gate_w', 'up_w', 'up_b', 'down_w', 'down_b', 'sh_up_w', 'sh_up_b', 'sh_down_w', 'sh_down_b')}
    del _L0_ffn_all

    def _L1_xattn_setup():
        import jax, jax.numpy as jnp
        import numpy as np
        NEG = -1000000.0
        key = jax.random.key(seed)
        ks = jax.random.split(key, 8)
        B, S, D = (2, 512, 256)
        query = jax.random.normal(ks[0], (B, S, D), jnp.float32)
        key_t = jax.random.normal(ks[1], (B, S, D), jnp.float32)
        value = jax.random.normal(ks[2], (B, S, D), jnp.float32)
        valid_len = jax.random.randint(ks[3], (B,), 1, S + 1, jnp.int32)
        s = 1.0 / np.sqrt(D)
        W_q = jax.random.normal(ks[4], (D, D), jnp.float32) * s
        W_k = jax.random.normal(ks[5], (D, D), jnp.float32) * s
        W_v = jax.random.normal(ks[6], (D, D), jnp.float32) * s
        W_o = jax.random.normal(ks[7], (D, D), jnp.float32) * s
        return {'query': query, 'key': key_t, 'value': value, 'valid_len': valid_len, 'W_q': W_q, 'W_k': W_k, 'W_v': W_v, 'W_o': W_o}
    _L1_xattn_all = _L1_xattn_setup()
    _L1_xattn_in = {k: v for k, v in _L1_xattn_all.items() if k in ('W_q', 'W_k', 'W_v', 'W_o')}
    del _L1_xattn_all

    def _L1_ffn_setup():
        import jax, jax.numpy as jnp
        import numpy as np
        EPS = 1e-12

        def _l2norm(v):
            n = jnp.sqrt(jnp.sum(v * v, axis=-1, keepdims=True))
            return v / jnp.maximum(n, EPS)
        key = jax.random.key(seed)
        ks = jax.random.split(key, 6)
        B, S, D, F, E = (2, 512, 256, 1024, 8)
        std = 0.02
        return {'x': jax.random.normal(ks[0], (B, S, D), jnp.float32), 'Wp': jax.random.normal(ks[1], (D, D), jnp.float32) * (1.0 / np.sqrt(D)), 'sim_matrix': jax.random.normal(ks[2], (E, D), jnp.float32) * std, 'temperature': jnp.asarray(1.0, jnp.float32), 'W1': jax.random.normal(ks[3], (E, D, F), jnp.float32) * (1.0 / np.sqrt(D)), 'b1': jnp.zeros((E, F), jnp.float32), 'W2': jax.random.normal(ks[4], (E, F, D), jnp.float32) * (1.0 / np.sqrt(F)), 'b2': jnp.zeros((E, D), jnp.float32)}
    _L1_ffn_all = _L1_ffn_setup()
    _L1_ffn_in = {k: v for k, v in _L1_ffn_all.items() if k in ('Wp', 'sim_matrix', 'temperature', 'W1', 'b1', 'W2', 'b2')}
    del _L1_ffn_all
    return {'x': x, 'ctx_1024': ctx_1024, 'mask_B_ik0': mask_B_ik0, 'g_xattn': g_xattn, 'g_ffn': g_ffn, 'L0_xattn_Wq': _L0_xattn_in['Wq'], 'L0_xattn_Wk': _L0_xattn_in['Wk'], 'L0_xattn_Wv': _L0_xattn_in['Wv'], 'L0_xattn_bv': _L0_xattn_in['bv'], 'L0_xattn_Wo': _L0_xattn_in['Wo'], 'L0_xattn_bo': _L0_xattn_in['bo'], 'L0_ffn_gate_w': _L0_ffn_in['gate_w'], 'L0_ffn_up_w': _L0_ffn_in['up_w'], 'L0_ffn_up_b': _L0_ffn_in['up_b'], 'L0_ffn_down_w': _L0_ffn_in['down_w'], 'L0_ffn_down_b': _L0_ffn_in['down_b'], 'L0_ffn_sh_up_w': _L0_ffn_in['sh_up_w'], 'L0_ffn_sh_up_b': _L0_ffn_in['sh_up_b'], 'L0_ffn_sh_down_w': _L0_ffn_in['sh_down_w'], 'L0_ffn_sh_down_b': _L0_ffn_in['sh_down_b'], 'L1_xattn_W_q': _L1_xattn_in['W_q'], 'L1_xattn_W_k': _L1_xattn_in['W_k'], 'L1_xattn_W_v': _L1_xattn_in['W_v'], 'L1_xattn_W_o': _L1_xattn_in['W_o'], 'L1_ffn_Wp': _L1_ffn_in['Wp'], 'L1_ffn_sim_matrix': _L1_ffn_in['sim_matrix'], 'L1_ffn_temperature': _L1_ffn_in['temperature'], 'L1_ffn_W1': _L1_ffn_in['W1'], 'L1_ffn_b1': _L1_ffn_in['b1'], 'L1_ffn_W2': _L1_ffn_in['W2'], 'L1_ffn_b2': _L1_ffn_in['b2']}

def reference(x, ctx_1024, mask_B_ik0, g_xattn, g_ffn, L0_xattn_Wq, L0_xattn_Wk, L0_xattn_Wv, L0_xattn_bv, L0_xattn_Wo, L0_xattn_bo, L0_ffn_gate_w, L0_ffn_up_w, L0_ffn_up_b, L0_ffn_down_w, L0_ffn_down_b, L0_ffn_sh_up_w, L0_ffn_sh_up_b, L0_ffn_sh_down_w, L0_ffn_sh_down_b, L1_xattn_W_q, L1_xattn_W_k, L1_xattn_W_v, L1_xattn_W_o, L1_ffn_Wp, L1_ffn_sim_matrix, L1_ffn_temperature, L1_ffn_W1, L1_ffn_b1, L1_ffn_W2, L1_ffn_b2):
    import jax
    import jax.numpy as jnp

    def _L0_xattn_ref(q, k, v, Wq, Wk, Wv, bv, Wo, bo):
        import jax, jax.numpy as jnp
        import numpy as np
        EMBED_PHI = 256
        EMBED_F = 256
        HIDDEN_F = 256
        N_HEADS = 16
        B, S = (2, 512)
        Bq, Sq, _ = q.shape
        hd = HIDDEN_F // N_HEADS
        scale = 1.0 / np.sqrt(hd)
        qh = (q @ Wq.T).reshape(Bq, Sq, N_HEADS, hd).transpose(0, 2, 1, 3)
        kh = (k @ Wk.T).reshape(Bq, Sq, N_HEADS, hd).transpose(0, 2, 1, 3)
        vh = (v @ Wv.T + bv).reshape(Bq, Sq, N_HEADS, hd).transpose(0, 2, 1, 3)
        scores = jnp.einsum('bhsd,bhtd->bhst', qh, kh) * scale
        mask = jnp.triu(jnp.ones((Sq, Sq), dtype=bool), k=0).at[0, 0].set(False)
        scores = jnp.where(mask, -jnp.inf, scores)
        probs = jax.nn.softmax(scores, axis=-1)
        out = jnp.einsum('bhst,bhtd->bhsd', probs, vh)
        out = out.transpose(0, 2, 1, 3).reshape(Bq, Sq, HIDDEN_F)
        return out @ Wo.T + bo

    def _L0_ffn_ref(x, gate_w, up_w, up_b, down_w, down_b, sh_up_w, sh_up_b, sh_down_w, sh_down_b):
        import jax, jax.numpy as jnp
        import numpy as np
        D_MODEL = 256
        HIDDEN = 256
        NUM_EXPERTS = 8
        TOP_K = 2
        b, s, d = x.shape
        xf = x.reshape(-1, d)
        shared = jax.nn.silu(x @ sh_up_w + sh_up_b) @ sh_down_w + sh_down_b
        logits = xf @ gate_w.T
        scores = jax.nn.softmax(logits, axis=-1)
        topk_w, topk_i = jax.lax.top_k(scores, TOP_K)
        topk_w = topk_w / (topk_w.sum(axis=-1, keepdims=True) + 1e-20)
        comb = (jax.nn.one_hot(topk_i, NUM_EXPERTS, dtype=xf.dtype) * topk_w[..., None]).sum(axis=1)
        h = jnp.einsum('nd,edh->neh', xf, up_w) + up_b
        h = jax.nn.silu(h)
        ye = jnp.einsum('neh,ehd->ned', h, down_w) + down_b
        y = jnp.einsum('ned,ne->nd', ye, comb).reshape(b, s, d)
        return y + shared

    def _L1_xattn_ref(query, key, value, valid_len, W_q, W_k, W_v, W_o):
        import jax, jax.numpy as jnp
        import numpy as np
        NEG = -1000000.0
        B, S, D = query.shape
        H = 16
        hd = D // H

        def split_heads(x, W):
            return (x @ W.T).reshape(B, S, H, hd)
        q = split_heads(query, W_q)
        k = split_heads(key, W_k)
        v = split_heads(value, W_v)
        scores = jnp.einsum('bqhd,bkhd->bhqk', q, k) / np.sqrt(hd)
        kmask = jnp.arange(S)[None, None, None, :] < valid_len[:, None, None, None]
        scores = jnp.where(kmask, scores, NEG)
        attn = jax.nn.softmax(scores, axis=-1)
        out = jnp.einsum('bhqk,bkhd->bqhd', attn, v).reshape(B, S, D)
        return out @ W_o.T

    def _L1_ffn_ref(x, Wp, sim_matrix, temperature, W1, b1, W2, b2):
        import jax, jax.numpy as jnp
        import numpy as np
        EPS = 1e-12

        def _l2norm(v):
            n = jnp.sqrt(jnp.sum(v * v, axis=-1, keepdims=True))
            return v / jnp.maximum(n, EPS)
        E = sim_matrix.shape[0]
        top_k = 2
        proj = jnp.einsum('bsd,ed->bse', x, Wp)
        pn = _l2norm(proj)
        sn = _l2norm(sim_matrix)
        gate_scores = jnp.einsum('bsd,ed->bse', pn, sn) / temperature
        top_v, top_i = jax.lax.top_k(gate_scores, top_k)
        gate_probs = jax.nn.softmax(top_v, axis=-1)
        comb = jnp.sum(jax.nn.one_hot(top_i, E, dtype=x.dtype) * gate_probs[..., None], axis=-2)
        h = jax.nn.gelu(jnp.einsum('bsd,edf->ebsf', x, W1) + b1[:, None, None, :], approximate=False)
        eo = jnp.einsum('ebsf,efd->ebsd', h, W2) + b2[:, None, None, :]
        out = jnp.einsum('ebsd,bse->bsd', eo, comb)
        return out
    x = x + jnp.tanh(g_xattn[0]) * _L0_xattn_ref(_layernorm(x, axis=-1), ctx_1024, ctx_1024, L0_xattn_Wq, L0_xattn_Wk, L0_xattn_Wv, L0_xattn_bv, L0_xattn_Wo, L0_xattn_bo)
    x = x + jnp.tanh(g_ffn[0]) * _L0_ffn_ref(_layernorm(x, axis=-1), L0_ffn_gate_w, L0_ffn_up_w, L0_ffn_up_b, L0_ffn_down_w, L0_ffn_down_b, L0_ffn_sh_up_w, L0_ffn_sh_up_b, L0_ffn_sh_down_w, L0_ffn_sh_down_b)
    x = x + jnp.tanh(g_xattn[1]) * _L1_xattn_ref(_layernorm(x, axis=-1), ctx_1024, ctx_1024, mask_B_ik0, L1_xattn_W_q, L1_xattn_W_k, L1_xattn_W_v, L1_xattn_W_o)
    x = x + jnp.tanh(g_ffn[1]) * _L1_ffn_ref(_layernorm(x, axis=-1), L1_ffn_Wp, L1_ffn_sim_matrix, L1_ffn_temperature, L1_ffn_W1, L1_ffn_b1, L1_ffn_W2, L1_ffn_b2)
    return x

_drawn_inputs = setup_inputs


def setup_inputs(seed=0):
    import zlib

    import numpy as np

    out = dict(_drawn_inputs(seed))
    spreads = {'g_ffn': (-1.0, 0.6),
     'L0_ffn_up_b': (0.0, 0.1),
     'L0_ffn_down_b': (0.0, 0.1),
     'L0_ffn_sh_up_b': (0.0, 0.1),
     'L0_ffn_sh_down_b': (0.0, 0.1),
     'L1_ffn_b1': (0.0, 0.1),
     'L1_ffn_b2': (0.0, 0.1)}
    factors = {}
    for name, (base, spread) in spreads.items():
        noise = np.random.default_rng([zlib.crc32(name.encode()), seed]).standard_normal(out[name].shape)
        drawn = base * np.exp(spread * noise) if base else spread * noise
        out[name] = jnp.asarray(drawn.astype(out[name].dtype))
    for name, factor in factors.items():
        out[name] = (out[name] * factor).astype(out[name].dtype)
    return out
```

```python
from contextlib import ExitStack

import concourse.bass as bass
from concourse import mybir

P = 128
F32 = mybir.dt.float32
BF16 = mybir.dt.bfloat16
I32 = mybir.dt.int32
U32 = mybir.dt.uint32
ALU = mybir.AluOpType
ACT = mybir.ActivationFunctionType
AX_X = mybir.AxisListType.X

LN_EPS = 1e-5
CAUSAL_FILL = -1e30
NEG_HI, NEG_LO = -999424.0, -576.0


class Step:

    def __init__(self, pair, off, count):
        self.pair, self.off, self.count = pair, off, count

    def at(self, d):
        return self.pair * 2 + (self.off + d)

    def half(self, d):
        return self.pair + (self.off + d) // 2

    def par(self, d):
        return (self.off + d) % 2

    def has(self, d):
        return not isinstance(self.pair, int) or 0 <= self.at(d) < self.count

    def upto(self, d):
        n = self.at(d) + 1
        return min(n, self.count) if isinstance(n, int) else n


def pipeline(eng, step, count, first, last, head, tail):
    for i in range(first, first + head):
        step(Step(0, i, count))
    lo, hi = first + head, last + 1 - tail
    assert lo % 2 == 0 and (hi - lo) % 2 == 0
    with eng.Fori(lo // 2, hi // 2) as pair:
        step(Step(pair, 0, count))
        step(Step(pair, 1, count))
    for i in range(hi, last + 1):
        step(Step(0, i, count))


def need(eng, sem, value, base=0):
    if isinstance(value, int) and value <= 0:
        return
    eng.wait_ge(sem, value + base)


def wait_apart(eng, sem, value, met, met_value):
    if not isinstance(value, int):
        value = eng.snap(value)
    eng.wait_ge(met, met_value)
    eng.wait_ge(sem, value)


class Resident:

    def __init__(self, nc, ctx, tokens, width):
        def sb(name, shape, dt):
            return ctx.enter_context(nc.sbuf_tensor(name, shape, dt))

        self.x = sb("x_rows", [P, tokens // P, width], F32)
        self.ident = sb("ident", [P, P], F32)
        self.ident16 = sb("ident16", [P, P], BF16)
        self.rows_sent = [[ctx.enter_context(nc.semaphore(f"rows_sent{layer}{n}")) for n in range(2)] for layer in range(2)]
        self.pads_sent = [ctx.enter_context(nc.semaphore(f"pads_sent{layer}")) for layer in range(2)]
        self.y_sent = [ctx.enter_context(nc.semaphore(f"y_sent{layer}")) for layer in range(2)]
        self.tanh_gates = sb("tanh_gates", [P, 4], F32)


def clear_semaphores(nc, ctx_sems):
    with nc.Block() as block:
        @block.gpsimd
        def _(pool):
            for s in ctx_sems:
                pool.sem_clear(s)


def setup_phase(nc, keep, g_xattn, g_ffn):
    with ExitStack() as ctx:
        gates = ctx.enter_context(nc.sbuf_tensor("gates", [P, 4], F32))
        gates_loaded = ctx.enter_context(nc.semaphore("gates_loaded"))
        idents_cleared = ctx.enter_context(nc.semaphore("idents_cleared"))
        block = ctx.enter_context(nc.Block())

        @block.sync
        def _(sp):
            for n, g in enumerate((g_xattn, g_ffn)):
                row = g.rearrange("(a n) -> a n", a=1)
                sp.dma_start(gates[:, 2 * n:2 * n + 2], row.to_broadcast((P, 2))).then_inc(gates_loaded, 16)

        @block.scalar
        def _(act):
            act.wait_ge(gates_loaded, 32)
            nc.scalar.activation(keep.tanh_gates[:], gates[:], ACT.Tanh)

        @block.gpsimd
        def _(pool):
            nc.gpsimd.memset(keep.ident[:], 0.0).then_inc(idents_cleared, 1)
            nc.gpsimd.memset(keep.ident16[:], 0.0).then_inc(idents_cleared, 1)
            pool.wait_ge(idents_cleared, 2)
            for ident in (keep.ident, keep.ident16):
                nc.gpsimd.affine_select(out=ident[:], in_=ident[:], compare_op=ALU.not_equal, fill=1.0,
                                        base=0, pattern=[[-1, P]], channel_multiplier=1)

    clear_semaphores(nc, [gates_loaded, idents_cleared])


def attention_phase(nc, keep, layer, x_in, ctx_in, lens, weights, biases, scratch):
    B, S, D = ctx_in.shape
    H, HD = 16, D // 16
    KC, TC = D // P, S // P
    causal = layer == 0
    scale = HD ** -0.5
    Q_PARTS, K_PARTS = (0, 0, 1, 1, 0, 2), (0, 1, 0, 1, 2, 0)
    STACK = HD * len(Q_PARTS)
    MASK_ROWS = 0 if causal else 2
    MAX_ROW = STACK + MASK_ROWS
    HH = H // 2
    VW = HD + 1
    gate_col = layer
    tag = f"a{layer}_"

    all_sems = []
    with ExitStack() as ctx:
        def sb(name, shape, dt=F32):
            return ctx.enter_context(nc.sbuf_tensor(tag + name, shape, dt))

        def pair(name, shape, dt=F32):
            return [sb(f"{name}{n}", shape, dt) for n in range(2)]

        def sem(name):
            s = ctx.enter_context(nc.semaphore(tag + name))
            all_sems.append(s)
            return s

        def sems(name):
            return [sem(f"{name}{n}") for n in range(2)]

        w_rows = sb("w_rows", [P, 4, KC, D])
        w_t = sb("w_t", [P, 4, KC, D])
        ctx_rows = pair("ctx_rows", [P, TC, D])
        xn = pair("xn", [P, TC, D])
        xn_t = pair("xn_t", [P, KC, S])
        ctx_t = pair("ctx_t", [P, KC, S])
        stats = sb("stats", [P, TC, 6])
        mean_var = sb("mean_var", [P, TC, 2])
        var_eps = sb("var_eps", [P, TC])
        eps = sb("eps", [P, TC])
        minus_half = sb("minus_half", [P, TC])
        rstd = sb("rstd", [P, TC])
        qk = pair("qk", [P, 2 * KC, S])
        rest = sb("rest", [P, 2 * KC, S])
        parts = pair("parts", [P, 2 * KC, 3, S], BF16)
        q_stack = pair("q_stack", [P, H, S], BF16)
        k_stack = pair("k_stack", [P, H, S], BF16)
        v_ones = pair("v_ones", [P, TC, H, VW])
        row_max = sb("row_max", [P, TC, H])
        max_rest = sb("max_rest", [P, TC, H])
        max_parts = sb("max_parts", [P, TC, 3, H], BF16)
        max_t = pair("max_t", [3 * H, S], BF16)
        probs = [sb(f"probs{n}", [P, 512]) for n in range(4)]
        recip = sb("recip", [P, TC, H])
        heads_out = pair("heads_out", [P, TC, D])
        heads_t = pair("heads_t", [P, KC, S])
        if causal:
            mask_st = sb("mask_st", [P, 2, P], BF16)
            mask_ts = sb("mask_ts", [P, 2, P], BF16)
            bv_rows = sb("bv_rows", [P, TC, D])
            bo_rows = sb("bo_rows", [P, D])
        else:
            lens_i = sb("lens_i", [P, B], I32)
            lens_f = sb("lens_f", [P, B])
            iota_t = sb("iota_t", [P, S])
            neg_col = sb("neg_col", [P, 1])
            valid = sb("valid", [P, S])
            mask_row = pair("mask_row", [P, S], BF16)

        stage = [ctx.enter_context(nc.psum_tensor(f"{tag}stage{n}", [P, 512], F32)) for n in range(2)]
        scores = [ctx.enter_context(nc.psum_tensor(f"{tag}scores{n}", [P, 512], F32)) for n in range(2)]
        scores_t = [ctx.enter_context(nc.psum_tensor(f"{tag}scores_t{n}", [P, 512], F32)) for n in range(2)]
        pv = [ctx.enter_context(nc.psum_tensor(f"{tag}pv{n}", [P, 512], F32)) for n in range(2)]

        w_loaded = sem("w_loaded")
        w_turned = sem("w_turned")
        w_ready = sem("w_ready")
        consts_loaded = sem("consts_loaded")
        consts_step = sem("consts_step")
        consts_ready = sem("consts_ready")
        bo_gated = sem("bo_gated")
        x_loaded = sems("x_loaded")
        ctx_loaded = sems("ctx_loaded")
        stats_done = sem("stats_done")
        mean_done = sem("mean_done")
        eps_added = sem("eps_added")
        rstd_done = sem("rstd_done")
        xn_ready = sem("xn_ready")
        x_biased = sem("x_biased")
        xn_turned = sem("xn_turned")
        ctx_turned = sem("ctx_turned")
        xn_t_ready = sem("xn_t_ready")
        ctx_t_ready = sem("ctx_t_ready")
        q_done = sem("q_done")
        k_done = sem("k_done")
        v_done = sem("v_done")
        q_ready = sem("q_ready")
        k_ready = sem("k_ready")
        v_ready = sem("v_ready")
        valid_done = sem("valid_done")
        part_hi = sem("part_hi")
        part_rest = sem("part_rest")
        part_mid = sem("part_mid")
        parts_ready = sem("parts_ready")
        parts_stored = sems("parts_stored")
        stacked = [sems(f"stacked_half{n}_") for n in range(2)]
        scores_done = sem("scores_done")
        maxed = sem("maxed")
        max_hi = sem("max_hi")
        max_r1 = sem("max_r1")
        max_mid = sem("max_mid")
        max_ready = sem("max_ready")
        max_turned = sem("max_turned")
        max_t_ready = sem("max_t_ready")
        max_stacked = sems("max_stacked")
        scores_t_done = sem("scores_t_done")
        probs_ready = sem("probs_ready")
        pv_done = sem("pv_done")
        recip_done = sem("recip_done")
        heads_ready = sem("heads_ready")
        heads_turned = sem("heads_turned")
        heads_t_ready = sem("heads_t_ready")
        o_done = sem("o_done")
        x_updated = sem("x_updated")

        x_tiles = x_in.rearrange("b (c p) d -> b p c d", p=P)
        ctx_tiles = ctx_in.rearrange("b (c p) d -> b p c d", p=P)
        N_CONSTS = 3 if causal else 1
        N_READY = 7

        FIRST, LAST, HEAD, TAIL = -2, B, 4, 5

        block = ctx.enter_context(nc.Block())

        @block.sync
        def _(sp):
            for n, w in enumerate(weights):
                sp.dma_start(w_rows[:, n], w.rearrange("(c p) d -> p c d", p=P)).then_inc(w_loaded, 16)
            if causal:
                bv, bo = biases
                for c in range(TC):
                    sp.dma_start(bv_rows[:, c], bv.rearrange("(a d) -> a d", a=1).to_broadcast((P, D))).then_inc(consts_loaded, 16)
                sp.dma_start(bo_rows[:], bo.rearrange("(a d) -> a d", a=1).to_broadcast((P, D))).then_inc(consts_loaded, 16)
            else:
                sp.dma_start(lens_i[:], lens.rearrange("(a n) -> a n", a=1).to_broadcast((P, B))).then_inc(consts_loaded, 16)
            for b in range(2):
                sp.dma_start(keep.x[:, TC * b:TC * b + TC, :], x_tiles[b]).then_inc(x_loaded[b], 16)
            sp.dma_start(ctx_rows[0][:], ctx_tiles[0]).then_inc(ctx_loaded[0], 16)
            sp.wait_ge(consts_ready, N_READY)

            def step(i):
                if i.has(4):
                    need(sp, stats_done, i.at(2) + 1)
                    sp.dma_start(keep.x[:, bass.ds(i.at(4) * TC, TC), :], x_tiles[i.at(4)]).then_inc(x_loaded[i.par(4)], 16)
                if i.has(3):
                    need(sp, ctx_turned, i.at(1) + 1)
                    sp.dma_start(ctx_rows[i.par(3)][:], ctx_tiles[i.at(3)]).then_inc(ctx_loaded[i.par(3)], 16)
                if i.has(0):
                    p = i.par(0)
                    need(sp, max_t_ready, i.at(0) + 1)
                    for j in range(3):
                        sp.dma_start(q_stack[p][MAX_ROW + j:MAX_ROW + j + 1, :, :],
                                     max_t[p][j * H:(j + 1) * H, :]).then_inc(max_stacked[p], 16)
                if i.has(2):
                    p = i.par(2)
                    need(sp, parts_ready, i.at(2) + 1)
                    sp.dma_start(scratch[p].rearrange("(n p) j s -> p n j s", p=P), parts[p][:]).then_inc(parts_stored[p], 16)
                    need(sp, parts_stored[p], (i.half(2) + 1) * 16)
                    for half in range(2):
                        need(sp, scores_t_done, i.at(0) * H + HH * (half + 1))
                        hs = slice(half * HH, half * HH + HH)
                        for n, (q, k) in enumerate(zip(Q_PARTS, K_PARTS)):
                            rows = slice(n * HD, n * HD + HD)
                            for m, (stack, j) in enumerate(((q_stack, q), (k_stack, k))):
                                src = scratch[p][m * D:(m + 1) * D, j].rearrange("(h d) s -> d h s", d=HD)
                                sp.dma_start(stack[p][rows, hs, :], src[:, hs, :]).then_inc(stacked[half][p], 16)
                        if not causal:
                            row = mask_row[p][STACK:STACK + 2, :].unsqueeze(1).to_broadcast((2, HH, S))
                            sp.dma_start(k_stack[p][STACK:STACK + 2, hs, :], row).then_inc(stacked[half][p], 16)

            pipeline(sp, step, B, FIRST, LAST, HEAD, TAIL)

        STACK_DMAS = 2 * len(Q_PARTS) + (0 if causal else 1)

        @block.gpsimd
        def _(pool):
            nc.gpsimd.memset(eps[:], LN_EPS)
            nc.gpsimd.memset(minus_half[:], -0.5).then_inc(consts_step, 1)
            if causal:
                nc.gpsimd.memset(mask_st[:], 0.0).then_inc(consts_step, 1)
                nc.gpsimd.memset(mask_ts[:], 0.0).then_inc(consts_step, 1)
                pool.wait_ge(consts_step, 3)
                nc.gpsimd.affine_select(out=mask_st[:], in_=mask_st[:], compare_op=ALU.is_gt, fill=CAUSAL_FILL,
                                        base=0, pattern=[[0, 2], [-1, P]], channel_multiplier=1).then_inc(consts_step, 1)
                nc.gpsimd.affine_select(out=mask_ts[:], in_=mask_ts[:], compare_op=ALU.is_gt, fill=CAUSAL_FILL,
                                        base=0, pattern=[[0, 2], [1, P]], channel_multiplier=-1).then_inc(consts_step, 1)
                pool.wait_ge(consts_step, 5)
                nc.gpsimd.memset(mask_st[0:1, 0, 0:1], 0.0).then_inc(consts_step, 1)
                nc.gpsimd.memset(mask_ts[0:1, 0, 0:1], 0.0).then_inc(consts_step, 1)
                pool.wait_ge(consts_step, 7)
            else:
                nc.gpsimd.iota(iota_t[:], pattern=[[1, S]], base=0, channel_multiplier=0,
                               allow_small_or_imprecise_dtypes=True).then_inc(consts_step, 1)
                nc.gpsimd.memset(neg_col[:], NEG_LO).then_inc(consts_step, 1)
                pool.wait_ge(consts_step, 3)
                nc.gpsimd.memset(neg_col[STACK:STACK + 1, :], NEG_HI).then_inc(consts_step, 1)
                pool.wait_ge(consts_step, 4)
            nc.gpsimd.memset(var_eps[:], 1.0).then_inc(consts_ready, 1)

            def rstd_of(b, base):
                pool.wait_ge(mean_done, b + 1)
                nc.gpsimd.tensor_tensor(var_eps[:], mean_var[:, :, 1], eps[:], ALU.add).then_inc(eps_added, 1)
                pool.wait_ge(eps_added, b + 1)
                nc.gpsimd.tensor_tensor(rstd[:], var_eps[:], minus_half[:], ALU.pow).then_inc(rstd_done, 1)
                if causal:
                    pool.wait_ge(xn_ready, b + 1)
                    if isinstance(b, int) and b == 0:
                        pool.wait_ge(bo_gated, 1)
                    rows = keep.x[:, bass.ds(b * TC, TC), :] if not isinstance(b, int) else keep.x[:, b * TC:b * TC + TC, :]
                    nc.gpsimd.tensor_tensor(rows, rows, bo_rows[:].unsqueeze(1).to_broadcast((P, TC, D)), ALU.add).then_inc(x_biased, 1)

            rstd_of(0, 0)

            def step(i):
                if i.has(3):
                    rstd_of(i.at(3), 0)

            pipeline(pool, step, B, FIRST, LAST, HEAD, TAIL)

        @block.vector
        def _(dve):
            for n in range(2):
                nc.vector.memset(v_ones[n][:], 1.0).then_inc(consts_ready, 1)
                nc.vector.memset(q_stack[n][STACK:P, :, :], 1.0).then_inc(consts_ready, 1)
                nc.vector.memset(k_stack[n][STACK:P, :, :], 1.0).then_inc(consts_ready, 1)
            dve.wait_ge(consts_ready, N_READY)
            dve.wait_ge(consts_loaded, 16 * N_CONSTS)
            if causal:
                nc.vector.tensor_scalar(bo_rows[:], bo_rows[:], keep.tanh_gates[:, gate_col:gate_col + 1], None, ALU.mult).then_inc(bo_gated, 1)
            else:
                nc.vector.tensor_copy(lens_f[:], lens_i[:]).then_inc(bo_gated, 1)
                dve.wait_ge(bo_gated, 1)

            def ln_stats(b, n, x_par):
                dve.wait_ge(x_loaded[x_par], (n + 1) * 16)
                for c in range(TC):
                    last = nc.vector.bn_stats(stats[:, c, :], keep.x[:, b * TC + c, :])
                last.then_inc(stats_done, 1)

            def ln_mean(b):
                for c in range(TC):
                    last = nc.vector.bn_aggr(mean_var[:, c, :], stats[:, c, :])
                last.then_inc(mean_done, 1)

            def ln_apply(b, p):
                dve.wait_ge(rstd_done, b + 1)
                need(dve, xn_turned, b - 1)
                for c in range(TC):
                    last = nc.vector.tensor_scalar(xn[p][:, c, :], keep.x[:, b * TC + c, :], mean_var[:, c, 0:1],
                                                   rstd[:, c:c + 1], ALU.subtract, ALU.mult)
                last.then_inc(xn_ready, 1)

            ln_stats(0, 0, 0)
            dve.wait_ge(stats_done, 1)
            ln_mean(0)
            ln_apply(0, 0)

            def step(i):
                if i.has(-1):
                    b = i.at(-1)
                    dve.wait_ge(o_done, b + 1)
                    if causal:
                        dve.wait_ge(x_biased, b + 1)
                    rows = keep.x[:, bass.ds(b * TC, TC), :].rearrange("p c d -> p (c d)")
                    nc.vector.scalar_tensor_tensor(out=rows, in0=stage[1][:], scalar=keep.tanh_gates[:, gate_col:gate_col + 1],
                                                   in1=rows, op0=ALU.mult, op1=ALU.add).then_inc(x_updated, 1)
                if i.has(2):
                    b, p = i.at(2), i.par(2)
                    need(dve, part_rest, b - 1)
                    if causal:
                        dve.wait_ge(k_done, b + 1)
                        nc.vector.tensor_copy(qk[p][:, KC:2 * KC, :].rearrange("p c s -> p (c s)"), stage[0][:]).then_inc(k_ready, 1)
                    else:
                        n = bass.ds(b, 1)
                        nc.vector.tensor_scalar(valid[:], iota_t[:], lens_f[:, n], None, ALU.is_lt).then_inc(valid_done, 1)
                        if i.has(0):
                            dve.wait_ge(stacked[1][p], i.half(2) * 16 * STACK_DMAS)
                        nc.vector.tensor_scalar(mask_row[p][STACK:STACK + 2, :], iota_t[STACK:STACK + 2, :], lens_f[STACK:STACK + 2, n],
                                                neg_col[STACK:STACK + 2, :], ALU.is_ge, ALU.mult).then_inc(valid_done, 1)
                        dve.wait_ge(valid_done, 2 * b + 2)
                        dve.wait_ge(k_done, b + 1)
                        nc.vector.tensor_tensor(qk[p][:, KC:2 * KC, :], stage[0][:].rearrange("p (c s) -> p c s", c=KC),
                                                valid[:].unsqueeze(1).to_broadcast((P, KC, S)), ALU.mult).then_inc(k_ready, 1)
                if i.has(1):
                    b, p = i.at(1), i.par(1)
                    dve.wait_ge(v_done, b + 1)
                    need(dve, pv_done, (b - 1) * H)
                    out = v_ones[p][:].rearrange("p c h w -> p (c h) w")[:, :, 0:HD]
                    src = stage[1][:].rearrange("p (n w) -> p n w", w=HD)
                    if causal:
                        nc.vector.tensor_tensor(out, src, bv_rows[:].rearrange("p c (h w) -> p (c h) w", w=HD), ALU.add).then_inc(v_ready, 1)
                    else:
                        nc.vector.tensor_copy(out, src).then_inc(v_ready, 1)

                def cut_hi():
                    b, p = i.at(2), i.par(2)
                    dve.wait_ge(q_ready, b + 1)
                    dve.wait_ge(k_ready, b + 1)
                    need(dve, parts_stored[p], i.half(2) * 16)
                    nc.vector.tensor_copy(parts[p][:, :, 0, :], qk[p][:]).then_inc(part_hi, 1)

                def cut_rest():
                    dve.wait_ge(part_hi, i.at(2) + 1)
                    p = i.par(2)
                    nc.vector.tensor_tensor(rest[:], qk[p][:], parts[p][:, :, 0, :], ALU.subtract).then_inc(part_rest, 1)

                def cut_mid():
                    dve.wait_ge(part_rest, i.at(2) + 1)
                    nc.vector.tensor_copy(parts[i.par(2)][:, :, 1, :], rest[:]).then_inc(part_mid, 1)

                def cut_lo():
                    dve.wait_ge(part_mid, i.at(2) + 1)
                    p = i.par(2)
                    nc.vector.tensor_tensor(parts[p][:, :, 2, :], rest[:], parts[p][:, :, 1, :], ALU.subtract).then_inc(parts_ready, 1)

                between = {}
                if i.has(2):
                    between |= {0: cut_hi, 2: cut_rest, 4: cut_mid, 6: cut_lo}
                if i.has(3):
                    b3 = i.at(3)
                    between |= {8: lambda: ln_stats(b3, i.half(3), i.par(3)), 9: lambda: ln_mean(b3), 12: lambda: ln_apply(b3, i.par(3))}
                for h in range(H):
                    if h == 9 and i.has(3):
                        dve.wait_ge(stats_done, i.at(3) + 1)
                    if i.has(1):
                        dve.wait_ge(scores_done, i.at(1) * H + h + 1)
                        bank = scores[h % 2]
                        if causal:
                            nc.vector.reduce_max(row_max[:, 0, h:h + 1], bank[:, 0:P], AX_X)
                            nc.vector.reduce_max(row_max[:, 1, h:h + 1], bank[:, P:3 * P], AX_X).then_inc(maxed, 1)
                        else:
                            nc.vector.reduce_max(row_max[:, :, h], bank[:].rearrange("p (c t) -> p c t", c=TC), AX_X).then_inc(maxed, 1)
                    if h in between:
                        between[h]()
                if i.has(1):
                    b = i.at(1)
                    dve.wait_ge(maxed, (b + 1) * H)
                    need(dve, max_turned, b)
                    nc.vector.tensor_scalar(max_parts[:, :, 0, :], row_max[:], -1.0, None, ALU.mult).then_inc(max_hi, 1)
                    dve.wait_ge(max_hi, b + 1)
                    nc.vector.scalar_tensor_tensor(out=max_rest[:], in0=row_max[:], scalar=-1.0, in1=max_parts[:, :, 0, :],
                                                   op0=ALU.mult, op1=ALU.subtract).then_inc(max_r1, 1)
                    dve.wait_ge(max_r1, b + 1)
                    nc.vector.tensor_copy(max_parts[:, :, 1, :], max_rest[:]).then_inc(max_mid, 1)
                    dve.wait_ge(max_mid, b + 1)
                    nc.vector.tensor_tensor(max_parts[:, :, 2, :], max_rest[:], max_parts[:, :, 1, :], ALU.subtract).then_inc(max_ready, 1)
                if i.has(0):
                    b, p = i.at(0), i.par(0)
                    dve.wait_ge(pv_done, (b + 1) * H)
                    views = [bank[:, 0:H * VW].rearrange("p (h w) -> p h w", w=VW) for bank in pv]
                    for c in range(TC):
                        last = nc.vector.reciprocal(recip[:, c, :], views[c][:, :, HD])
                    last.then_inc(recip_done, 1)
                    dve.wait_ge(recip_done, b + 1)
                    need(dve, heads_turned, b - 1)
                    for c in range(TC):
                        last = nc.vector.tensor_tensor(heads_out[p][:, c, :].rearrange("p (h w) -> p h w", w=HD), views[c][:, :, 0:HD],
                                                       recip[:, c, :].unsqueeze(2).to_broadcast((P, H, HD)), ALU.mult)
                    last.then_inc(heads_ready, 1)

            pipeline(dve, step, B, FIRST, LAST, HEAD, TAIL)

        @block.scalar
        def _(act):
            for n in range(4):
                act.wait_ge(w_turned, n + 1)
                nc.scalar.activation(w_t[:, n].rearrange("p c d -> p (c d)"), stage[n % 2][:], ACT.Copy).then_inc(w_ready, 1)

            def step(i):
                if i.has(2):
                    b, p = i.at(2), i.par(2)
                    act.wait_ge(xn_turned, b + 1)
                    need(act, q_done, b - 1)
                    nc.scalar.activation(xn_t[p][:].rearrange("p c s -> p (c s)"), stage[0][:], ACT.Copy).then_inc(xn_t_ready, 1)
                    act.wait_ge(ctx_turned, b + 1)
                    need(act, v_done, b - 1)
                    nc.scalar.activation(ctx_t[p][:].rearrange("p c s -> p (c s)"), stage[1][:], ACT.Copy).then_inc(ctx_t_ready, 1)
                if i.has(0):
                    b, p = i.at(0), i.par(0)
                    act.wait_ge(max_turned, b + 1)
                    need(act, max_stacked[p], i.half(0) * 48)
                    nc.scalar.activation(max_t[p][:], stage[0][0:3 * H, 0:S // 2].bitcast(BF16), ACT.Copy).then_inc(max_t_ready, 1)
                if i.has(-1):
                    b, p = i.at(-1), i.par(-1)
                    act.wait_ge(heads_turned, b + 1)
                    need(act, o_done, b - 1)
                    nc.scalar.activation(heads_t[p][:].rearrange("p c s -> p (c s)"), stage[1][:], ACT.Copy).then_inc(heads_t_ready, 1)
                if i.has(2):
                    b, p = i.at(2), i.par(2)
                    act.wait_ge(q_done, b + 1)
                    need(act, part_rest, b - 1)
                    nc.scalar.activation(qk[p][:, 0:KC, :].rearrange("p c s -> p (c s)"), stage[0][:], ACT.Copy, scale=scale).then_inc(q_ready, 1)
                if i.has(0):
                    b = i.at(0)
                    width = 3 * P if causal else 4 * P
                    for h in range(H):
                        act.wait_ge(scores_t_done, b * H + h + 1)
                        need(act, pv_done, b * H + h - 3)
                        nc.scalar.activation(probs[h % 4][:, 0:width], scores_t[h % 2][:, 0:width], ACT.Exp).then_inc(probs_ready, 1)

            pipeline(act, step, B, FIRST, LAST, HEAD, TAIL)

        @block.tensor
        def _(pe):
            for n in range(4):
                if n == 0:
                    pe.wait_ge(w_loaded, 64)
                need(pe, w_ready, n - 1)
                for kc in range(KC):
                    for oc in range(KC):
                        last = nc.tensor.transpose(stage[n % 2][:, kc * D + oc * P:kc * D + oc * P + P],
                                                   w_rows[:, n, oc, kc * P:kc * P + P], keep.ident[:])
                last.then_inc(w_turned, 1)
            pe.wait_ge(w_ready, 4)
            pe.wait_ge(consts_ready, N_READY)

            def turn(bank, rows, done):
                for kc in range(KC):
                    for c in range(TC):
                        last = nc.tensor.transpose(bank[:, kc * S + c * P:kc * S + c * P + P], rows[:, c, kc * P:kc * P + P], keep.ident[:])
                last.then_inc(done, 1)

            def project_t(bank, n, cols, done):
                for m in range(KC):
                    for kc in range(KC):
                        last = nc.tensor.matmul(bank[:, m * S:(m + 1) * S], w_t[:, n, kc, m * P:(m + 1) * P], cols[:, kc, :],
                                                start=(kc == 0), stop=(kc == KC - 1))
                last.then_inc(done, 1)

            def project(bank, n, cols, done):
                for c in range(TC):
                    for kc in range(KC):
                        last = nc.tensor.matmul(bank[:, c * D:(c + 1) * D], cols[:, kc, c * P:(c + 1) * P], w_t[:, n, kc, :],
                                                start=(kc == 0), stop=(kc == KC - 1))
                last.then_inc(done, 1)

            def front(i):
                if i.has(2):
                    b, p = i.at(2), i.par(2)
                    pe.wait_ge(xn_ready, b + 1)
                    need(pe, k_ready, b)
                    turn(stage[0], xn[p], xn_turned)
                    pe.wait_ge(ctx_loaded[p], (i.half(2) + 1) * 16)
                    need(pe, v_ready, i.at(0) + 1)
                    turn(stage[1], ctx_rows[p], ctx_turned)
                if i.has(0):
                    wait_apart(pe, max_ready, i.at(0) + 1, consts_ready, N_READY)
                    need(pe, xn_t_ready, i.upto(2))
                    need(pe, k_ready, i.upto(1))
                    turned = stage[0][0:3 * H, 0:S // 2].bitcast(BF16)
                    for c in range(TC):
                        last = nc.tensor.transpose(turned[:, c * P:(c + 1) * P], max_parts[:, c].rearrange("p j h -> p (j h)"), keep.ident16[:])
                    last.then_inc(max_turned, 1)
                if i.has(-1):
                    pe.wait_ge(heads_ready, i.at(-1) + 1)
                    need(pe, ctx_t_ready, i.upto(2))
                    need(pe, v_ready, i.upto(0))
                    turn(stage[1], heads_out[i.par(-1)], heads_turned)
                if i.has(2):
                    b, p = i.at(2), i.par(2)
                    pe.wait_ge(xn_t_ready, b + 1)
                    need(pe, max_t_ready, i.at(0) + 1)
                    project_t(stage[0], 0, xn_t[p], q_done)
                if i.has(-1):
                    pe.wait_ge(heads_t_ready, i.at(-1) + 1)
                    project(stage[1], 3, heads_t[i.par(-1)], o_done)
                if i.has(2):
                    b, p = i.at(2), i.par(2)
                    pe.wait_ge(ctx_t_ready, b + 1)
                    pe.wait_ge(q_ready, b + 1)
                    project_t(stage[0], 1, ctx_t[p], k_done)
                if i.has(1):
                    need(pe, ctx_t_ready, i.upto(2))
                    need(pe, x_updated, i.at(0))
                    project(stage[1], 2, ctx_t[i.par(1)], v_done)

            def score_head(i, h):
                b, p = i.at(1), i.par(1)
                if h % HH == 0:
                    pe.wait_ge(stacked[h // HH][p], (i.half(1) + 1) * 16 * STACK_DMAS)
                need(pe, maxed, b * H + h - 1)
                bank, q, k = scores[h % 2], q_stack[p], k_stack[p]
                rows = slice(0, STACK + MASK_ROWS)
                if causal:
                    nc.tensor.matmul(bank[:, 0:P], keep.ident16[:], mask_st[:, 0, :], start=True, stop=False)
                    nc.tensor.matmul(bank[:, 0:P], q[rows, h, 0:P], k[rows, h, 0:P], start=False, stop=True)
                    nc.tensor.matmul(bank[:, P:2 * P], q[rows, h, P:S], k[rows, h, 0:P], start=True, stop=True)
                    nc.tensor.matmul(bank[:, 2 * P:3 * P], keep.ident16[:], mask_st[:, 1, :], start=True, stop=False)
                    last = nc.tensor.matmul(bank[:, 2 * P:3 * P], q[rows, h, P:S], k[rows, h, P:S], start=False, stop=True)
                else:
                    for c in range(TC):
                        last = nc.tensor.matmul(bank[:, c * S:(c + 1) * S], q[rows, h, c * P:(c + 1) * P], k[rows, h, :], start=True, stop=True)
                last.then_inc(scores_done, 1)

            def score_head_t(i, h):
                b, p = i.at(0), i.par(0)
                if h == 0:
                    pe.wait_ge(max_stacked[p], (i.half(0) + 1) * 48)
                need(pe, probs_ready, b * H + h - 1)
                bank, q, k = scores_t[h % 2], q_stack[p], k_stack[p]
                rows = slice(0, MAX_ROW + 3)
                if causal:
                    nc.tensor.matmul(bank[:, 0:P], keep.ident16[:], mask_ts[:, 0, :], start=True, stop=False)
                    nc.tensor.matmul(bank[:, 0:P], k[rows, h, 0:P], q[rows, h, 0:P], start=False, stop=True)
                    nc.tensor.matmul(bank[:, P:2 * P], k[rows, h, 0:P], q[rows, h, P:S], start=True, stop=True)
                    nc.tensor.matmul(bank[:, 2 * P:3 * P], keep.ident16[:], mask_ts[:, 1, :], start=True, stop=False)
                    last = nc.tensor.matmul(bank[:, 2 * P:3 * P], k[rows, h, P:S], q[rows, h, P:S], start=False, stop=True)
                else:
                    for c in range(TC):
                        last = nc.tensor.matmul(bank[:, c * S:(c + 1) * S], k[rows, h, c * P:(c + 1) * P], q[rows, h, :], start=True, stop=True)
                last.then_inc(scores_t_done, 1)

            def mix_head(i, h):
                b, p = i.at(0), i.par(0)
                pe.wait_ge(probs_ready, b * H + h + 1)
                if h == 0:
                    pe.wait_ge(v_ready, b + 1)
                    need(pe, heads_ready, b)
                pr = probs[h % 4]
                blocks = ({0: {0: 0}, 1: {0: P, 1: 2 * P}} if causal
                          else {c: {t: t * S + c * P for t in range(TC)} for c in range(TC)})
                for c in range(TC):
                    for n, (t, col) in enumerate(blocks[c].items()):
                        last = nc.tensor.matmul(pv[c][:, h * VW:(h + 1) * VW], pr[:, col:col + P], v_ones[p][:, t, h, :],
                                                start=(n == 0), stop=(n == len(blocks[c]) - 1))
                last.then_inc(pv_done, 1)

            def step(i):
                front(i)
                for h in range(H):
                    if i.has(1):
                        score_head(i, h)
                    if i.has(0):
                        score_head_t(i, h)
                        if h:
                            mix_head(i, h - 1)
                if i.has(0):
                    mix_head(i, H - 1)

            pipeline(pe, step, B, FIRST, LAST, HEAD, TAIL)

    clear_semaphores(nc, all_sems)


TS = 256
TT = TS // P
ROW = 258
EXPERTS = 8


def region_rows(tokens):
    return tokens + TS


def tile_count(tokens):
    return 2 * tokens // TS + EXPERTS


def routed_rows(tokens):
    return EXPERTS * region_rows(tokens) + (EXPERTS + 1) * TS


class Routed:

    def __init__(self, nc, ctx, tag, tokens, F):
        def sb(name, shape, dt):
            return ctx.enter_context(nc.sbuf_tensor(f"{tag}_{name}", shape, dt))

        tiles = tile_count(tokens) + 1
        self.tile_expert = sb("tile_expert", [P, 1 + tiles], I32)
        self.tile_row = sb("tile_row", [P, tiles], I32)
        self.up_bias = sb("up_bias", [P, EXPERTS * F // P], F32)


def route_phase(nc, keep, routed, layer, F, up_b, gate, shared, xs, x_acc):
    NT = keep.x.shape[1]
    D = keep.x.shape[2]
    C, KC = 2, D // P
    S = C * P
    NB = NT // C
    tokens = NT * P
    R = region_rows(tokens)
    E = EXPERTS
    FC = F // P
    tiles = tile_count(tokens) + 1
    soft = layer == 0
    gate_col = 2 + layer
    GW = E if soft else D + E
    tag = f"r{layer}_"
    J = tokens // TS

    all_sems = []
    with ExitStack() as ctx:
        def sb(name, shape, dt=F32):
            return ctx.enter_context(nc.sbuf_tensor(tag + name, shape, dt))

        def sem(name):
            s = ctx.enter_context(nc.semaphore(tag + name))
            all_sems.append(s)
            return s

        rows = [sb(f"rows{n}", [P, 2, C, ROW]) for n in range(2)]
        stats = sb("stats", [P, C, 6])
        mean_var = sb("mean_var", [P, C, 2])
        var_eps = sb("var_eps", [P, C])
        eps = sb("eps", [P, C])
        minus_half = sb("minus_half", [P, C])
        rstd = sb("rstd", [P, C])
        xn_t = sb("xn_t", [P, KC, S])
        gate_w = sb("gate_w", [P, KC, GW])
        scores = sb("scores", [P, C, E])
        top = sb("top", [P, C, E])
        top_index = sb("top_index", [P, C, E], U32)
        top_index_f = sb("top_index_f", [P, 2, C])
        below_top = sb("below_top", [P, C, E])
        exps = sb("exps", [P, C, E])
        exp_sum = sb("exp_sum", [P, C])
        exp_recip = sb("exp_recip", [P, C])
        share = sb("share", [P, C, 2])
        share_sum = sb("share_sum", [P, C])
        share_recip = sb("share_recip", [P, C])
        one_hot = sb("one_hot", [P, 2, C, E])
        chosen = sb("chosen", [P, C, E], BF16)
        next_row = sb("next_row", [P, E])
        place = sb("place", [P, C, E])
        place_of = sb("place_of", [P, 2, C, E])
        slot_f = sb("slot_f", [P, 2, C])
        slot = [sb(f"slot{n}", [P, 2, C], U32) for n in range(2)]
        expert_iota = sb("expert_iota", [P, E])
        region_start = sb("region_start", [P, E])
        token_ids = sb("token_ids", [P, NT])
        ones16 = sb("ones16", [P, P], BF16)
        before16 = sb("before16", [P, P], BF16)
        pad_rows = sb("pad_rows", [P, TT, ROW])
        pad_offset = sb("pad_offset", [P, TT])
        pad_slot_f = sb("pad_slot_f", [P, E, TT])
        pad_slot = sb("pad_slot", [P, E, TT], U32)
        count = sb("count", [P, E])
        full_steps = sb("full_steps", [P, J])
        beyond = sb("beyond", [P, E, J])
        n_tiles = sb("n_tiles", [P, E])
        ends = sb("ends", [P, E])
        tile_iota = sb("tile_iota", [P, tiles])
        past = sb("past", [P, tiles, E])
        past_tiles = sb("past_tiles", [P, tiles, E])
        region = sb("region", [P, tiles])
        first_tile = sb("first_tile", [P, tiles])
        in_region = sb("in_region", [P, tiles])
        row_f = sb("row_f", [P, tiles])
        up_b_rows = sb("up_b_rows", [E * FC, P])
        if soft:
            gate_rows = sb("gate_rows", [E, D])
            sh_up = sb("sh_up", [P, KC, D])
            sh_down = sb("sh_down", [P, KC, D])
            sh_up_bias = sb("sh_up_bias", [P, KC])
            sh_up_b_rows = sb("sh_up_b_rows", [KC, P])
            sh_down_bias = sb("sh_down_bias", [P, D])
            sh_hidden = sb("sh_hidden", [P, KC, S])
        else:
            wp_rows = sb("wp_rows", [P, KC, D])
            sim_rows = sb("sim_rows", [E, D])
            sim_sq = sb("sim_sq", [E, D])
            sim_ss = sb("sim_ss", [E, 1])
            sim_ss_min = sb("sim_ss_min", [E, 1])
            sim_rnorm = sb("sim_rnorm", [E, 1])
            sim_unit = sb("sim_unit", [E, D])
            sim_t = sb("sim_t", [P, KC, E])
            temp = sb("temp", [P, 1])
            temp_recip = sb("temp_recip", [P, 1])
            proj_sq = sb("proj_sq", [P, C, D])
            proj_ss = sb("proj_ss", [P, C])
            proj_ss_min = sb("proj_ss_min", [P, C])
            proj_rnorm = sb("proj_rnorm", [P, C])

        def bank(name):
            return ctx.enter_context(nc.psum_tensor(tag + name, [P, 512], F32))

        turned = bank("turned")
        gated = [bank(f"gated{n}") for n in range(2)]
        ranked = bank("ranked")
        sh_h = bank("sh_h")
        sh_y = bank("sh_y")

        w_loaded = sem("w_loaded")
        consts_step = sem("consts_step")
        consts_ready = sem("consts_ready")
        prep_turned = sem("prep_turned")
        prep_copied = sem("prep_copied")
        sim_step = sem("sim_step")
        temp_done = sem("temp_done")
        stats_done = sem("stats_done")
        mean_done = sem("mean_done")
        eps_added = sem("eps_added")
        rstd_done = sem("rstd_done")
        xn_ready = sem("xn_ready")
        rows_copied = sem("rows_copied")
        xn_turned = sem("xn_turned")
        xn_t_ready = sem("xn_t_ready")
        gate_done = sem("gate_done")
        ss_done = sem("ss_done")
        ss_floored = sem("ss_floored")
        rnorm_done = sem("rnorm_done")
        scores_ready = sem("scores_ready")
        top_done = sem("top_done")
        index_done = sem("index_done")
        below_done = sem("below_done")
        exps_done = sem("exps_done")
        index_f_done = sem("index_f_done")
        one_hot_done = sem("one_hot_done")
        chosen_ready = sem("chosen_ready")
        share_step = sem("share_step")
        rank_done = sem("rank_done")
        placed = sem("placed")
        counted = sem("counted")
        place_picked = sem("place_picked")
        slot_summed = sem("slot_summed")
        rows_ready = sem("rows_ready")
        rows_sent = keep.rows_sent[layer]
        pads_sent = keep.pads_sent[layer]
        table_step = sem("table_step")
        pad_slots_ready = sem("pad_slots_ready")
        x_stored = sem("x_stored")
        if soft:
            x_biased = sem("x_biased")
            sh_bias_gated = sem("sh_bias_gated")
            sh_up_done = sem("sh_up_done")
            sh_hidden_ready = sem("sh_hidden_ready")
            sh_down_done = sem("sh_down_done")
            x_updated = sem("x_updated")

        acc_tiles = x_acc[0:tokens, :].rearrange("(n c p) d -> n p c d", c=C, p=P)
        N_LOADS = 6 if soft else 4
        FIRST, LAST, HEAD, TAIL = 0, NB - 1, 2, 2
        SHARES = 5 if soft else 2

        block = ctx.enter_context(nc.Block())

        @block.sync
        def _(sp):
            sp.dma_start(up_b_rows[:], up_b.rearrange("e (c p) -> (e c) p", p=P)).then_inc(w_loaded, 16)
            if soft:
                sh_up_w, sh_up_b, sh_down_w, sh_down_b = shared
                sp.dma_start(gate_rows[:], gate[0]).then_inc(w_loaded, 16)
                sp.dma_start(sh_up[:], sh_up_w.rearrange("(c p) f -> p c f", p=P)).then_inc(w_loaded, 16)
                sp.dma_start(sh_down[:], sh_down_w.rearrange("(c p) d -> p c d", p=P)).then_inc(w_loaded, 16)
                sp.dma_start(sh_up_b_rows[:], sh_up_b.rearrange("(c p) -> c p", p=P)).then_inc(w_loaded, 16)
                sp.dma_start(sh_down_bias[:], sh_down_b.rearrange("(a d) -> a d", a=1).to_broadcast((P, D))).then_inc(w_loaded, 16)
            else:
                wp, sim, temperature = gate
                sp.dma_start(wp_rows[:], wp.rearrange("(c p) d -> p c d", p=P)).then_inc(w_loaded, 16)
                sp.dma_start(sim_rows[:], sim).then_inc(w_loaded, 16)
                sp.dma_start(temp[:], temperature.rearrange("(a d) -> a d", a=1).to_broadcast((P, 1))).then_inc(w_loaded, 16)
            sp.wait_ge(consts_ready, 1)
            for n in range(E + 1):
                at = E * R + n * TS
                sp.dma_start(xs[at:at + TS, :].rearrange("(c p) w -> p c w", p=P), pad_rows[:]).then_inc(x_stored, 16)
            sp.dma_start(x_acc[tokens:tokens + TS, :].rearrange("(c p) d -> p c d", p=P), pad_rows[:, :, 0:D]).then_inc(x_stored, 16)
            n_stores = E + 2
            if soft:
                with sp.Fori(0, NB) as b:
                    sp.wait_ge(x_updated, b + 1)
                    sp.dma_start(acc_tiles[b], keep.x[:, bass.ds(b * C, C), :]).then_inc(x_stored, 16)
                n_stores += NB
            else:
                sp.dma_start(x_acc[0:tokens, :].rearrange("(n p) d -> p n d", p=P), keep.x[:]).then_inc(x_stored, 16)
                n_stores += 1
            sp.wait_ge(x_stored, n_stores * 16)

        @block.gpsimd
        def _(pool):
            nc.gpsimd.memset(pad_rows[:], 0.0).then_inc(consts_step, 1)
            nc.gpsimd.iota(token_ids[:], pattern=[[P, NT]], base=0, channel_multiplier=1,
                           allow_small_or_imprecise_dtypes=True)
            nc.gpsimd.iota(expert_iota[:], pattern=[[1, E]], base=0, channel_multiplier=0, allow_small_or_imprecise_dtypes=True)
            nc.gpsimd.iota(region_start[:], pattern=[[R, E]], base=0, channel_multiplier=0, allow_small_or_imprecise_dtypes=True)
            nc.gpsimd.iota(next_row[:], pattern=[[R, E]], base=0, channel_multiplier=0, allow_small_or_imprecise_dtypes=True)
            nc.gpsimd.iota(pad_offset[:], pattern=[[P, TT]], base=0, channel_multiplier=1, allow_small_or_imprecise_dtypes=True)
            nc.gpsimd.iota(tile_iota[:], pattern=[[1, tiles]], base=0, channel_multiplier=0, allow_small_or_imprecise_dtypes=True)
            nc.gpsimd.iota(full_steps[:], pattern=[[TS, J]], base=0, channel_multiplier=0,
                           allow_small_or_imprecise_dtypes=True).then_inc(consts_step, 1)
            nc.gpsimd.memset(minus_half[:], -0.5)
            nc.gpsimd.memset(eps[:], LN_EPS)
            nc.gpsimd.memset(ones16[:], 1.0)
            nc.gpsimd.memset(before16[:], 1.0).then_inc(consts_step, 1)
            pool.wait_ge(consts_step, 3)
            nc.gpsimd.memset(full_steps[:, 0:1], -1.0).then_inc(consts_step, 1)
            nc.gpsimd.affine_select(out=before16[:], in_=before16[:], compare_op=ALU.is_gt, fill=0.0, base=0,
                                    pattern=[[1, P]], channel_multiplier=-1).then_inc(consts_step, 1)
            nc.gpsimd.iota(pad_rows[:, :, D + 1], pattern=[[P, TT]], base=tokens, channel_multiplier=1,
                           allow_small_or_imprecise_dtypes=True).then_inc(consts_step, 1)
            pool.wait_ge(consts_step, 6)
            nc.gpsimd.memset(rstd[:], 1.0).then_inc(consts_ready, 1)
            if not soft:
                pool.wait_ge(sim_step, 1)
                nc.gpsimd.tensor_scalar(sim_ss_min[:], sim_ss[:], 1e-24, None, ALU.max).then_inc(sim_step, 1)
                pool.wait_ge(sim_step, 2)
                nc.gpsimd.tensor_tensor(sim_rnorm[:], sim_ss_min[:], minus_half[0:E, 0:1], ALU.pow).then_inc(sim_step, 1)

            def add_eps(b):
                pool.wait_ge(mean_done, b + 1)
                nc.gpsimd.tensor_tensor(var_eps[:], mean_var[:, :, 1], eps[:], ALU.add).then_inc(eps_added, 1)

            def rstd_of(b):
                pool.wait_ge(eps_added, b + 1)
                nc.gpsimd.tensor_tensor(rstd[:], var_eps[:], minus_half[:], ALU.pow).then_inc(rstd_done, 1)

            def bias_x(b):
                pool.wait_ge(xn_ready, b + 1)
                if isinstance(b, int) and b == 0:
                    pool.wait_ge(sh_bias_gated, 1)
                x_rows = keep.x[:, bass.ds(b * C, C), :]
                nc.gpsimd.tensor_tensor(x_rows, x_rows, sh_down_bias[:].unsqueeze(1).to_broadcast((P, C, D)), ALU.add).then_inc(x_biased, 1)

            for b in range(2):
                add_eps(b)
                rstd_of(b)
                if soft:
                    bias_x(b)

            def step(i):
                b, p = i.at(0), i.par(0)
                if not soft:
                    pool.wait_ge(ss_floored, b + 1)
                    nc.gpsimd.tensor_tensor(proj_rnorm[:], proj_ss_min[:], minus_half[:], ALU.pow).then_inc(rnorm_done, 1)
                if i.has(2):
                    add_eps(i.at(2))
                pool.wait_ge(rows_ready, b + 1)
                pool.wait_ge(rows_copied, b + 1)
                if i.has(2):
                    rstd_of(i.at(2))
                for k in range(2):
                    for c in range(C):
                        pool.indirect_dma_start(out=xs, out_offset=bass.IndirectOffsetOnAxis(ap=slot[p][:, k, c:c + 1], axis=0),
                                                in_=rows[p][:, k, c, :], in_offset=None).then_inc(rows_sent[p], 16)
                if soft and i.has(2):
                    bias_x(i.at(2))

            pipeline(pool, step, NB, FIRST, LAST, HEAD, TAIL)
            pool.wait_ge(pad_slots_ready, 1)
            for e in range(E):
                for c in range(TT):
                    pool.indirect_dma_start(out=xs, out_offset=bass.IndirectOffsetOnAxis(ap=pad_slot[:, e, c:c + 1], axis=0),
                                            in_=pad_rows[:, c, :], in_offset=None).then_inc(pads_sent, 16)
            pool.wait_ge(pads_sent, 16 * E * TT)
            for n in range(2):
                pool.wait_ge(rows_sent[n], 16 * 2 * C * NB // 2)

        @block.vector
        def _(dve):
            dve.wait_ge(consts_ready, 1)
            dve.wait_ge(w_loaded, 16 * N_LOADS)
            if soft:
                nc.vector.tensor_scalar(sh_down_bias[:], sh_down_bias[:], keep.tanh_gates[:, gate_col:gate_col + 1], None, ALU.mult).then_inc(sh_bias_gated, 1)
            else:
                nc.vector.reciprocal(temp_recip[:], temp[:]).then_inc(temp_done, 1)
                dve.wait_ge(sim_step, 3)
                nc.vector.tensor_scalar(sim_unit[:], sim_rows[:], sim_rnorm[:, 0:1], None, ALU.mult).then_inc(sim_step, 1)

            def ln(b):
                for c in range(C):
                    last = nc.vector.bn_stats(stats[:, c, :], keep.x[:, b * C + c, :])
                last.then_inc(stats_done, 1)

            def ln_mean(b):
                for c in range(C):
                    last = nc.vector.bn_aggr(mean_var[:, c, :], stats[:, c, :])
                last.then_inc(mean_done, 1)

            def ln_apply(b, p, sent):
                dve.wait_ge(rstd_done, b + 1)
                need(dve, rows_sent[p], sent)
                for c in range(C):
                    last = nc.vector.tensor_scalar(rows[p][:, 0, c, 0:D], keep.x[:, b * C + c, :], mean_var[:, c, 0:1],
                                                   rstd[:, c:c + 1], ALU.subtract, ALU.mult)
                last.then_inc(xn_ready, 1)

            for b in range(2):
                ln(b)
                dve.wait_ge(stats_done, b + 1)
                ln_mean(b)
                ln_apply(b, b, 0)

            def step(i):
                b, p = i.at(0), i.par(0)
                dve.wait_ge(gate_done, b + 1)
                if soft:
                    nc.vector.tensor_copy(scores[:], gated[0][:, 0:C * E].rearrange("p (c e) -> p c e", c=C)).then_inc(scores_ready, 1)
                else:
                    dve.wait_ge(ss_done, b + 1)
                    nc.vector.tensor_scalar(proj_ss_min[:], proj_ss[:], 1e-24, None, ALU.max).then_inc(ss_floored, 1)
                    dve.wait_ge(rnorm_done, b + 1)
                    if i.off == 0:
                        dve.wait_ge(temp_done, 1)
                    for c in range(C):
                        last = nc.vector.tensor_scalar(scores[:, c, :], gated[c][:, D:D + E], proj_rnorm[:, c:c + 1], temp_recip[:, 0:1], ALU.mult, ALU.mult)
                    last.then_inc(scores_ready, 1)
                wait_apart(dve, scores_ready, b + 1, consts_ready, 1)
                for c in range(C):
                    last = nc.vector.max(top[:, c, :], scores[:, c, :])
                last.then_inc(top_done, 1)
                wait_apart(dve, top_done, b + 1, consts_ready, 1)
                for c in range(C):
                    last = nc.vector.max_index(top_index[:, c, :], top[:, c, :], scores[:, c, :])
                last.then_inc(index_done, 1)
                nc.vector.tensor_tensor(below_top[:], top[:], top[:, :, 0:1].to_broadcast((P, C, E)), ALU.subtract).then_inc(below_done, 1)
                dve.wait_ge(index_done, b + 1)
                nc.vector.tensor_copy(top_index_f[:].rearrange("p k c -> p c k"), top_index[:, :, 0:2]).then_inc(index_f_done, 1)
                dve.wait_ge(index_f_done, b + 1)
                nc.vector.tensor_tensor(one_hot[:].rearrange("p k c e -> p (k c) e"),
                                        expert_iota[:].unsqueeze(1).to_broadcast((P, 2 * C, E)),
                                        top_index_f[:].rearrange("p k c -> p (k c)").unsqueeze(2).to_broadcast((P, 2 * C, E)),
                                        ALU.is_equal).then_inc(one_hot_done, 1)
                dve.wait_ge(one_hot_done, b + 1)
                nc.vector.tensor_tensor(chosen[:], one_hot[:, 0], one_hot[:, 1], ALU.add).then_inc(chosen_ready, 1)
                dve.wait_ge(exps_done, b + 1)
                steps = b * SHARES
                if soft:
                    nc.vector.reduce_sum(exp_sum[:], exps[:], AX_X).then_inc(share_step, 1)
                    dve.wait_ge(share_step, steps + 1)
                    nc.vector.reciprocal(exp_recip[:], exp_sum[:]).then_inc(share_step, 1)
                    dve.wait_ge(share_step, steps + 2)
                    nc.vector.tensor_tensor(share[:], exps[:, :, 0:2], exp_recip[:].unsqueeze(2).to_broadcast((P, C, 2)), ALU.mult).then_inc(share_step, 1)
                    dve.wait_ge(share_step, steps + 3)
                    nc.vector.scalar_tensor_tensor(out=share_sum[:], in0=share[:, :, 0], scalar=1e-20, in1=share[:, :, 1],
                                                   op0=ALU.add, op1=ALU.add).then_inc(share_step, 1)
                    dve.wait_ge(share_step, steps + 4)
                    parts2 = share
                else:
                    nc.vector.tensor_tensor(share_sum[:], exps[:, :, 0], exps[:, :, 1], ALU.add).then_inc(share_step, 1)
                    dve.wait_ge(share_step, steps + 1)
                    parts2 = exps
                nc.vector.reciprocal(share_recip[:], share_sum[:]).then_inc(share_step, 1)
                dve.wait_ge(share_step, steps + SHARES)
                nc.vector.scalar_tensor_tensor(out=rows[p][:, :, :, D].rearrange("p k c -> p c k"), in0=parts2[:, :, 0:2],
                                               scalar=keep.tanh_gates[:, gate_col:gate_col + 1],
                                               in1=share_recip[:].unsqueeze(2).to_broadcast((P, C, 2)), op0=ALU.mult, op1=ALU.mult)
                nc.vector.tensor_copy(rows[p][:, :, :, D + 1], token_ids[:, bass.ds(b * C, C)].unsqueeze(1).to_broadcast((P, 2, C)))
                if i.has(2):
                    ln(i.at(2))
                dve.wait_ge(rank_done, b + 1)
                need(dve, counted, b)
                if i.has(2):
                    dve.wait_ge(stats_done, i.at(2) + 1)
                nc.vector.tensor_tensor(place[:], ranked[:, 0:C * E].rearrange("p (c e) -> p c e", c=C),
                                        next_row[:].unsqueeze(1).to_broadcast((P, C, E)), ALU.add).then_inc(placed, 1)
                if i.has(2):
                    ln_mean(i.at(2))
                dve.wait_ge(placed, b + 1)
                nc.vector.tensor_tensor(next_row[:], next_row[:], ranked[:, C * E:C * E + E], ALU.add).then_inc(counted, 1)
                nc.vector.tensor_tensor(place_of[:].rearrange("p k c e -> p k (c e)"), one_hot[:].rearrange("p k c e -> p k (c e)"),
                                        place[:].rearrange("p c e -> p (c e)").unsqueeze(1).to_broadcast((P, 2, C * E)), ALU.mult).then_inc(place_picked, 1)
                dve.wait_ge(place_picked, b + 1)
                nc.vector.reduce_sum(slot_f[:], place_of[:], AX_X).then_inc(slot_summed, 1)
                dve.wait_ge(slot_summed, b + 1)
                nc.vector.tensor_copy(slot[p][:], slot_f[:]).then_inc(rows_ready, 1)
                if soft:
                    dve.wait_ge(sh_down_done, b + 1)
                    dve.wait_ge(x_biased, b + 1)
                    x_rows = keep.x[:, bass.ds(b * C, C), :].rearrange("p c d -> p (c d)")
                    nc.vector.scalar_tensor_tensor(out=x_rows, in0=sh_y[:], scalar=keep.tanh_gates[:, gate_col:gate_col + 1],
                                                   in1=x_rows, op0=ALU.mult, op1=ALU.add).then_inc(x_updated, 1)
                if i.has(2):
                    ln_apply(i.at(2), p, (i.half(0) + 1) * 16 * 2 * C)

            pipeline(dve, step, NB, FIRST, LAST, HEAD, TAIL)

            steps = [0]

            def tail_step(ins):
                steps[0] += 1
                ins.then_inc(table_step, 1)
                dve.wait_ge(table_step, steps[0])

            dve.wait_ge(counted, NB)
            tail_step(nc.vector.tensor_tensor(pad_slot_f[:], next_row[:].unsqueeze(2).to_broadcast((P, E, TT)),
                                              pad_offset[:].unsqueeze(1).to_broadcast((P, E, TT)), ALU.add))
            nc.vector.tensor_copy(pad_slot[:], pad_slot_f[:]).then_inc(pad_slots_ready, 1)
            tail_step(nc.vector.tensor_tensor(count[:], next_row[:], region_start[:], ALU.subtract))
            tail_step(nc.vector.tensor_tensor(beyond[:], count[:].unsqueeze(2).to_broadcast((P, E, J)),
                                              full_steps[:].unsqueeze(1).to_broadcast((P, E, J)), ALU.is_gt))
            tail_step(nc.vector.reduce_sum(n_tiles[:], beyond[:], AX_X))
            tail_step(nc.vector.tensor_copy(ends[:, 0:1], n_tiles[:, 0:1]))
            for e in range(1, E):
                tail_step(nc.vector.tensor_tensor(ends[:, e:e + 1], ends[:, e - 1:e], n_tiles[:, e:e + 1], ALU.add))
            tail_step(nc.vector.tensor_tensor(past[:], tile_iota[:].unsqueeze(2).to_broadcast((P, tiles, E)),
                                              ends[:].unsqueeze(1).to_broadcast((P, tiles, E)), ALU.is_ge))
            tail_step(nc.vector.reduce_sum(region[:], past[:], AX_X))
            tail_step(nc.vector.tensor_tensor(past_tiles[:], past[:], n_tiles[:].unsqueeze(1).to_broadcast((P, tiles, E)), ALU.mult))
            tail_step(nc.vector.reduce_sum(first_tile[:], past_tiles[:], AX_X))
            tail_step(nc.vector.tensor_tensor(in_region[:], tile_iota[:], first_tile[:], ALU.subtract))
            tail_step(nc.vector.tensor_scalar(row_f[:], region[:], float(R), None, ALU.mult))
            tail_step(nc.vector.scalar_tensor_tensor(out=row_f[:], in0=in_region[:], scalar=float(TS), in1=row_f[:], op0=ALU.mult, op1=ALU.add))
            nc.vector.tensor_copy(routed.tile_row[:], row_f[:])
            tail_step(nc.vector.tensor_scalar(region[:], region[:], float(E - 1), None, ALU.min))
            nc.vector.tensor_copy(routed.tile_expert[:, 0:1], region[:, 0:1])
            nc.vector.tensor_copy(routed.tile_expert[:, 1:1 + tiles], region[:])

        @block.scalar
        def _(act):
            act.wait_ge(prep_turned, 1)
            nc.scalar.activation(routed.up_bias[:], ranked[:, 0:E * FC], ACT.Copy).then_inc(prep_copied, 1)
            if soft:
                act.wait_ge(prep_turned, 2)
                nc.scalar.activation(gate_w[:], turned[:, 0:KC * E].rearrange("p (k e) -> p k e", k=KC), ACT.Copy).then_inc(prep_copied, 1)
                act.wait_ge(prep_turned, 3)
                nc.scalar.activation(sh_up_bias[:], ranked[:, 0:KC], ACT.Copy).then_inc(prep_copied, 1)
            else:
                act.wait_ge(w_loaded, 16 * N_LOADS)
                nc.scalar.activation(sim_sq[:], sim_rows[:], ACT.Square, accum_out=sim_ss[:, 0:1]).then_inc(sim_step, 1)
                act.wait_ge(prep_turned, 2)
                nc.scalar.activation(gate_w[:, :, 0:D], turned[:].rearrange("p (k d) -> p k d", k=KC), ACT.Copy).then_inc(prep_copied, 1)
                act.wait_ge(prep_turned, 3)
                nc.scalar.activation(sim_t[:], ranked[:, 0:KC * E].rearrange("p (k e) -> p k e", k=KC), ACT.Copy).then_inc(prep_copied, 1)
                act.wait_ge(prep_turned, 4)
                nc.scalar.activation(gate_w[:, :, D:D + E], turned[:, 0:KC * E].rearrange("p (k e) -> p k e", k=KC), ACT.Copy).then_inc(prep_copied, 1)

            def turn_out(b, p):
                act.wait_ge(xn_turned, b + 1)
                nc.scalar.activation(xn_t[:].rearrange("p k s -> p (k s)"), turned[:], ACT.Copy).then_inc(xn_t_ready, 1)

            turn_out(0, 0)

            def step(i):
                b, p = i.at(0), i.par(0)
                act.wait_ge(xn_ready, b + 1)
                nc.scalar.activation(rows[p][:, 1, :, 0:D], rows[p][:, 0, :, 0:D], ACT.Copy).then_inc(rows_copied, 1)
                if not soft:
                    act.wait_ge(gate_done, b + 1)
                    need(act, rnorm_done, b)
                    for c in range(C):
                        last = nc.scalar.activation(proj_sq[:, c, :], gated[c][:, 0:D], ACT.Square, accum_out=proj_ss[:, c:c + 1])
                    last.then_inc(ss_done, 1)
                else:
                    act.wait_ge(sh_up_done, b + 1)
                    need(act, sh_down_done, b)
                    for fc in range(KC):
                        last = nc.scalar.activation(sh_hidden[:, fc, :], sh_h[:, fc * S:(fc + 1) * S], ACT.Silu, bias=sh_up_bias[:, fc:fc + 1])
                    last.then_inc(sh_hidden_ready, 1)
                if i.has(1):
                    turn_out(i.at(1), i.par(1))
                act.wait_ge(below_done, b + 1)
                nc.scalar.activation(exps[:], below_top[:], ACT.Exp).then_inc(exps_done, 1)

            pipeline(act, step, NB, FIRST, LAST, HEAD, TAIL)

        @block.tensor
        def _(pe):
            pe.wait_ge(w_loaded, 16 * N_LOADS)
            nc.tensor.transpose(ranked[:, 0:E * FC], up_b_rows[:], keep.ident[0:E * FC, 0:E * FC]).then_inc(prep_turned, 1)
            if soft:
                for kc in range(KC):
                    last = nc.tensor.transpose(turned[:, kc * E:(kc + 1) * E], gate_rows[:, kc * P:(kc + 1) * P], keep.ident[0:E, 0:E])
                last.then_inc(prep_turned, 1)
                pe.wait_ge(prep_copied, 1)
                nc.tensor.transpose(ranked[:, 0:KC], sh_up_b_rows[:], keep.ident[0:KC, 0:KC]).then_inc(prep_turned, 1)
                pe.wait_ge(prep_copied, 3)
            else:
                for kc in range(KC):
                    for oc in range(KC):
                        last = nc.tensor.transpose(turned[:, kc * D + oc * P:kc * D + oc * P + P], wp_rows[:, oc, kc * P:kc * P + P], keep.ident[:])
                last.then_inc(prep_turned, 1)
                pe.wait_ge(prep_copied, 1)
                pe.wait_ge(sim_step, 4)
                for kc in range(KC):
                    last = nc.tensor.transpose(ranked[:, kc * E:(kc + 1) * E], sim_unit[:, kc * P:(kc + 1) * P], keep.ident[0:E, 0:E])
                last.then_inc(prep_turned, 1)
                pe.wait_ge(prep_copied, 3)
                for kc in range(KC):
                    for oc in range(KC):
                        last = nc.tensor.matmul(turned[:, kc * E:(kc + 1) * E], wp_rows[:, oc, kc * P:(kc + 1) * P], sim_t[:, oc, :],
                                                start=(oc == 0), stop=(oc == KC - 1))
                last.then_inc(prep_turned, 1)
                pe.wait_ge(prep_copied, 4)
            pe.wait_ge(consts_ready, 1)

            def turn(b, p):
                pe.wait_ge(xn_ready, b + 1)
                need(pe, xn_t_ready, b)
                for kc in range(KC):
                    for c in range(C):
                        last = nc.tensor.transpose(turned[:, kc * S + c * P:kc * S + c * P + P], rows[p][:, 0, c, kc * P:(kc + 1) * P], keep.ident[:])
                last.then_inc(xn_turned, 1)

            turn(0, 0)

            def step(i):
                b = i.at(0)
                pe.wait_ge(xn_t_ready, b + 1)
                need(pe, scores_ready, b)
                for c in range(C):
                    out = gated[0][:, c * E:(c + 1) * E] if soft else gated[c][:, 0:GW]
                    for kc in range(KC):
                        last = nc.tensor.matmul(out, xn_t[:, kc, c * P:(c + 1) * P], gate_w[:, kc, :], start=(kc == 0), stop=(kc == KC - 1))
                last.then_inc(gate_done, 1)
                if soft:
                    need(pe, sh_hidden_ready, b)
                    for fc in range(KC):
                        for kc in range(KC):
                            last = nc.tensor.matmul(sh_h[:, fc * S:(fc + 1) * S], sh_up[:, kc, fc * P:(fc + 1) * P], xn_t[:, kc, :],
                                                    start=(kc == 0), stop=(kc == KC - 1))
                    last.then_inc(sh_up_done, 1)
                if i.has(1):
                    turn(i.at(1), i.par(1))
                if soft:
                    pe.wait_ge(sh_hidden_ready, b + 1)
                    need(pe, x_updated, b)
                    for c in range(C):
                        for fc in range(KC):
                            last = nc.tensor.matmul(sh_y[:, c * D:(c + 1) * D], sh_hidden[:, fc, c * P:(c + 1) * P], sh_down[:, fc, :],
                                                    start=(fc == 0), stop=(fc == KC - 1))
                    last.then_inc(sh_down_done, 1)
                pe.wait_ge(chosen_ready, b + 1)
                need(pe, counted, b)
                for c in range(C):
                    out = ranked[:, c * E:(c + 1) * E]
                    nc.tensor.matmul(out, before16[:], chosen[:, c, :], start=True, stop=(c == 0))
                    for q in range(c):
                        nc.tensor.matmul(out, ones16[:], chosen[:, q, :], start=False, stop=(q == c - 1))
                for c in range(C):
                    last = nc.tensor.matmul(ranked[:, C * E:C * E + E], ones16[:], chosen[:, c, :], start=(c == 0), stop=(c == C - 1))
                last.then_inc(rank_done, 1)

            pipeline(pe, step, NB, FIRST, LAST, HEAD, TAIL)

    clear_semaphores(nc, all_sems)


def expert_phase(nc, keep, routed, layer, F, act_func, up_w, down_w, down_b, xs, x_acc):
    D = keep.x.shape[2]
    tokens = keep.x.shape[1] * P
    E = EXPERTS
    KC, FC = D // P, F // P
    tiles = tile_count(tokens)
    tag = f"e{layer}_"
    PER_BANK = 512 // TS
    N_BANKS = max(1, FC // PER_BANK)

    all_sems = []
    with ExitStack() as ctx:
        def sb(name, shape, dt=F32):
            return ctx.enter_context(nc.sbuf_tensor(tag + name, shape, dt))

        def sem(name):
            s = ctx.enter_context(nc.semaphore(tag + name))
            all_sems.append(s)
            return s

        up = [sb(f"up{n}", [P, KC, F]) for n in range(2)]
        down = [sb(f"down{n}", [P, FC, D]) for n in range(2)]
        down_bias = sb("down_bias", [P, E, D])
        xs_rows = sb("xs_rows", [P, TT, ROW])
        xs_t = sb("xs_t", [P, KC, TS])
        hidden = sb("hidden", [P, FC, TS])
        weight = sb("weight", [P, TT])
        token = sb("token", [P, TT], U32)
        y_biased = sb("y_biased", [P, TT, D])
        y = sb("y", [P, TT, D])

        def bank(name):
            return ctx.enter_context(nc.psum_tensor(tag + name, [P, 512], F32))

        turned = bank("turned")
        h_bank = [bank(f"h{n}") for n in range(N_BANKS)]
        y_bank = bank("y_bank")

        bias_loaded = sem("bias_loaded")
        w_loaded = [sem(f"w_loaded{n}") for n in range(2)]
        xs_loaded = sem("xs_loaded")
        xs_turned = sem("xs_turned")
        xs_t_ready = sem("xs_t_ready")
        up_done = sem("up_done")
        hidden_ready = sem("hidden_ready")
        y_done = sem("y_done")
        bias_added = sem("bias_added")
        y_ready = sem("y_ready")
        meta_ready = sem("meta_ready")
        y_sent = keep.y_sent[layer]

        block = ctx.enter_context(nc.Block())

        def expert_of(eng, t):
            return eng.value_load(routed.tile_expert[0:1, bass.ds(t + 1, 1)], min_val=0, max_val=E - 1)

        @block.sync
        def _(sp):
            def load_weights(e, n):
                sp.dma_start(up[n][:], up_w[e].rearrange("(c p) f -> p c f", p=P)).then_inc(w_loaded[n], 16)
                sp.dma_start(down[n][:], down_w[e].rearrange("(c p) d -> p c d", p=P)).then_inc(w_loaded[n], 16)

            def load_rows(t):
                row = sp.value_load(routed.tile_row[0:1, bass.ds(t, 1)], min_val=0, max_val=routed_rows(tokens) - TS)
                sp.dma_start(xs_rows[:], xs[bass.ds(row, TS), :].rearrange("(c p) w -> p c w", p=P)).then_inc(xs_loaded, 16)

            load_rows(0)
            for e in range(2):
                load_weights(e, e)
            sp.dma_start(down_bias[:], down_b.rearrange("(a e) d -> a e d", a=1).to_broadcast((P, E, D))).then_inc(bias_loaded, 16)
            with sp.Fori(0, tiles) as t:
                sp.wait_ge(meta_ready, t + 1)
                sp.wait_ge(xs_turned, t + 1)
                load_rows(t + 1)
                e = expert_of(sp, t)
                before = expert_of(sp, t - 1)
                with sp.If(e > before):
                    with sp.If(e < E - 1):
                        sp.wait_ge(y_done, t)
                        nxt = nc.s_assert_within(e + 1, 1, E - 1, skip_runtime_bounds_check_because="e < E - 1 here")
                        with sp.If(nxt % 2 == 0):
                            load_weights(nxt, 0)
                        with sp.Else():
                            load_weights(nxt, 1)

        @block.gpsimd
        def _(pool):
            with pool.Fori(1, tiles + 1) as t:
                wait_apart(pool, y_ready, t, w_loaded[0], 32)
                for c in range(TT):
                    pool.indirect_dma_start(out=x_acc, out_offset=bass.IndirectOffsetOnAxis(ap=token[:, c:c + 1], axis=0),
                                            in_=y[:, c, :], in_offset=None, compute_op=ALU.add).then_inc(y_sent, 16)
            pool.wait_ge(y_sent, 16 * TT * tiles)

        @block.vector
        def _(dve):
            def meta(t):
                dve.wait_ge(xs_loaded, 16 * (t + 1))
                nc.vector.tensor_copy(weight[:], xs_rows[:, :, D])
                nc.vector.tensor_copy(token[:], xs_rows[:, :, D + 1]).then_inc(meta_ready, 1)

            meta(0)
            dve.wait_ge(bias_loaded, 16)
            with dve.Fori(0, tiles) as t:
                e = expert_of(dve, t)
                dve.wait_ge(y_done, t + 1)
                nc.vector.tensor_tensor(y_biased[:], y_bank[:].rearrange("p (c d) -> p c d", c=TT),
                                        down_bias[:, bass.ds(e, 1), :].to_broadcast((P, TT, D)), ALU.add).then_inc(bias_added, 1)
                dve.wait_ge(bias_added, t + 1)
                dve.wait_ge(meta_ready, t + 1)
                for c in range(TT):
                    last = nc.vector.tensor_scalar(y[:, c, :], y_biased[:, c, :], weight[:, c:c + 1], None, ALU.mult)
                last.then_inc(y_ready, 1)
                dve.wait_ge(y_sent, 16 * TT * (t + 1))
                meta(t + 1)

        @block.scalar
        def _(act):
            def turn_out(t):
                act.wait_ge(xs_turned, t + 1)
                nc.scalar.activation(xs_t[:].rearrange("p k s -> p (k s)"), turned[:, 0:KC * TS], ACT.Copy).then_inc(xs_t_ready, 1)

            turn_out(0)
            with act.Fori(0, tiles) as t:
                e = expert_of(act, t)
                for fc in range(FC):
                    if fc % PER_BANK == 0:
                        act.wait_ge(up_done, N_BANKS * t + fc // PER_BANK + 1)
                    g, at = fc // PER_BANK, fc % PER_BANK * TS
                    nc.scalar.activation(hidden[:, fc, :], h_bank[g][:, at:at + TS], act_func,
                                         bias=routed.up_bias[:, bass.ds(e * FC + fc, 1)]).then_inc(hidden_ready, 1)
                turn_out(t + 1)

        @block.tensor
        def _(pe):
            def turn(t):
                pe.wait_ge(xs_loaded, 16 * (t + 1))
                for kc in range(KC):
                    for c in range(TT):
                        last = nc.tensor.transpose(turned[:, kc * TS + c * P:kc * TS + c * P + P], xs_rows[:, c, kc * P:(kc + 1) * P], keep.ident[:])
                last.then_inc(xs_turned, 1)

            turn(0)
            with pe.Fori(0, tiles) as t:
                e = expert_of(pe, t)

                def through(n):
                    pe.wait_ge(w_loaded[n], (e // 2 + 1) * 32)
                    pe.wait_ge(xs_t_ready, t + 1)
                    for fc in range(FC):
                        g, at = fc // PER_BANK, fc % PER_BANK * TS
                        for kc in range(KC):
                            last = nc.tensor.matmul(h_bank[g][:, at:at + TS], up[n][:, kc, fc * P:(fc + 1) * P], xs_t[:, kc, :],
                                                    start=(kc == 0), stop=(kc == KC - 1))
                        if fc % PER_BANK == PER_BANK - 1:
                            last.then_inc(up_done, 1)
                    turn(t + 1)
                    for c in range(TT):
                        for fc in range(FC):
                            if c == 0:
                                pe.wait_ge(hidden_ready, FC * t + fc + 1)
                            if c == 0 and fc == 0:
                                pe.wait_ge(bias_added, t)
                            last = nc.tensor.matmul(y_bank[:, c * D:(c + 1) * D], hidden[:, fc, c * P:(c + 1) * P], down[n][:, fc, :],
                                                    start=(fc == 0), stop=(fc == FC - 1))
                    last.then_inc(y_done, 1)

                with pe.If(e % 2 == 0):
                    through(0)
                with pe.Else():
                    through(1)

    clear_semaphores(nc, all_sems)


def gated_flamingo(nc, p, out):
    x, ctx_in, lens = p["x"], p["ctx_1024"], p["mask_B_ik0"]
    B, S, D = x.shape
    tokens = B * S
    F0 = p["L0_ffn_up_w"].shape[2]
    F1 = p["L1_ffn_W1"].shape[2]
    scratch = [nc.dram_tensor(f"parts_dram{n}", (2 * D, 3, S), BF16, kind="Internal").ap() for n in range(2)]
    xs = nc.dram_tensor("routed_rows_dram", (routed_rows(tokens), ROW), F32, kind="Internal").ap()
    x_mid = nc.dram_tensor("x_mid_dram", (tokens + TS, D), F32, kind="Internal").ap()

    with ExitStack() as ctx:
        keep = Resident(nc, ctx, tokens, D)
        setup_phase(nc, keep, p["g_xattn"], p["g_ffn"])

        attention_phase(nc, keep, 0, x, ctx_in, None, [p[f"L0_xattn_{w}"] for w in ("Wq", "Wk", "Wv", "Wo")],
                        [p["L0_xattn_bv"], p["L0_xattn_bo"]], scratch)
        with ExitStack() as tables:
            routed = Routed(nc, tables, "t0", tokens, F0)
            route_phase(nc, keep, routed, 0, F0, p["L0_ffn_up_b"], [p["L0_ffn_gate_w"]],
                        [p[f"L0_ffn_sh_{w}"] for w in ("up_w", "up_b", "down_w", "down_b")], xs, x_mid)
            expert_phase(nc, keep, routed, 0, F0, ACT.Silu, p["L0_ffn_up_w"], p["L0_ffn_down_w"], p["L0_ffn_down_b"], xs, x_mid)

        attention_phase(nc, keep, 1, x_mid[0:tokens, :].rearrange("(b s) d -> b s d", s=S), ctx_in, lens,
                        [p[f"L1_xattn_{w}"] for w in ("W_q", "W_k", "W_v", "W_o")], None, scratch)
        with ExitStack() as tables:
            routed = Routed(nc, tables, "t1", tokens, F1)
            route_phase(nc, keep, routed, 1, F1, p["L1_ffn_b1"],
                        [p["L1_ffn_Wp"], p["L1_ffn_sim_matrix"], p["L1_ffn_temperature"]], None, xs, out)
            expert_phase(nc, keep, routed, 1, F1, ACT.Gelu, p["L1_ffn_W1"], p["L1_ffn_W2"], p["L1_ffn_b2"], xs, out)


INPUTS = (["x", "ctx_1024", "mask_B_ik0", "g_xattn", "g_ffn"]
          + [f"L0_xattn_{n}" for n in ("Wq", "Wk", "Wv", "bv", "Wo", "bo")]
          + [f"L0_ffn_{n}" for n in ("gate_w", "up_w", "up_b", "down_w", "down_b", "sh_up_w", "sh_up_b", "sh_down_w", "sh_down_b")]
          + [f"L1_xattn_{n}" for n in ("W_q", "W_k", "W_v", "W_o")]
          + [f"L1_ffn_{n}" for n in ("Wp", "sim_matrix", "temperature", "W1", "b1", "W2", "b2")])


def kernel(**inputs):
    import numpy as _np
    import concourse.bacc as _bacc
    from concourse.bass_utils import run_bass_kernel_spmd as _run

    nc = _bacc.Bacc("TRN2", target_bir_lowering=False, num_devices=1)
    arrays, params = {}, {}
    for name in INPUTS:
        a = _np.ascontiguousarray(inputs[name])
        a = a.reshape(a.shape or (1,))
        arrays[f"in_{name}"] = a
        params[name] = nc.dram_tensor(f"in_{name}", a.shape, mybir.dt.from_np(a.dtype), kind="ExternalInput").ap()
    B, S, D = inputs["x"].shape
    out = nc.dram_tensor("out_rows", (B * S + TS, D), F32, kind="ExternalOutput").ap()
    gated_flamingo(nc, params, out)
    r = _run(nc, [arrays], core_ids=[0])
    return _np.asarray(r.results[0]["out_rows"])[:B * S].reshape(B, S, D)
```

```python
from contextlib import ExitStack

import concourse.bass as bass
from concourse import mybir

P = 128
F32 = mybir.dt.float32
BF16 = mybir.dt.bfloat16
I32 = mybir.dt.int32
U32 = mybir.dt.uint32
ALU = mybir.AluOpType
ACT = mybir.ActivationFunctionType
AX_X = mybir.AxisListType.X

LN_EPS = 1e-5
CAUSAL_FILL = -1e30
NEG_HI, NEG_LO = -999424.0, -576.0


class Step:

    def __init__(self, pair, off, count):
        self.pair, self.off, self.count = pair, off, count

    def at(self, d):
        return self.pair * 2 + (self.off + d)

    def half(self, d):
        return self.pair + (self.off + d) // 2

    def par(self, d):
        return (self.off + d) % 2

    def has(self, d):
        return not isinstance(self.pair, int) or 0 <= self.at(d) < self.count

    def upto(self, d):
        n = self.at(d) + 1
        return min(n, self.count) if isinstance(n, int) else n


def pipeline(eng, step, count, first, last, head, tail):
    for i in range(first, first + head):
        step(Step(0, i, count))
    lo, hi = first + head, last + 1 - tail
    assert lo % 2 == 0 and (hi - lo) % 2 == 0
    with eng.Fori(lo // 2, hi // 2) as pair:
        step(Step(pair, 0, count))
        step(Step(pair, 1, count))
    for i in range(hi, last + 1):
        step(Step(0, i, count))


def need(eng, sem, value, base=0):
    if isinstance(value, int) and value <= 0:
        return
    eng.wait_ge(sem, value + base)


def wait_apart(eng, sem, value, met, met_value):
    if not isinstance(value, int):
        value = eng.snap(value)
    eng.wait_ge(met, met_value)
    eng.wait_ge(sem, value)


class Resident:

    def __init__(self, nc, ctx, tokens, width):
        def sb(name, shape, dt):
            return ctx.enter_context(nc.sbuf_tensor(name, shape, dt))

        self.x = sb("x_rows", [P, tokens // P, width], F32)
        self.ident = sb("ident", [P, P], F32)
        self.ident16 = sb("ident16", [P, P], BF16)
        self.rows_sent = [[ctx.enter_context(nc.semaphore(f"rows_sent{layer}{n}")) for n in range(2)] for layer in range(2)]
        self.pads_sent = [ctx.enter_context(nc.semaphore(f"pads_sent{layer}")) for layer in range(2)]
        self.y_sent = [[ctx.enter_context(nc.semaphore(f"y_sent{layer}{n}")) for n in range(2)] for layer in range(2)]
        self.tanh_gates = sb("tanh_gates", [P, 4], F32)


def clear_semaphores(nc, ctx_sems):
    with nc.Block() as block:
        @block.gpsimd
        def _(pool):
            for s in ctx_sems:
                pool.sem_clear(s)


def setup_phase(nc, keep, g_xattn, g_ffn):
    with ExitStack() as ctx:
        gates = ctx.enter_context(nc.sbuf_tensor("gates", [P, 4], F32))
        gates_loaded = ctx.enter_context(nc.semaphore("gates_loaded"))
        idents_cleared = ctx.enter_context(nc.semaphore("idents_cleared"))
        block = ctx.enter_context(nc.Block())

        @block.sync
        def _(sp):
            for n, g in enumerate((g_xattn, g_ffn)):
                row = g.rearrange("(a n) -> a n", a=1)
                sp.dma_start(gates[:, 2 * n:2 * n + 2], row.to_broadcast((P, 2))).then_inc(gates_loaded, 16)

        @block.scalar
        def _(act):
            act.wait_ge(gates_loaded, 32)
            nc.scalar.activation(keep.tanh_gates[:], gates[:], ACT.Tanh)

        @block.gpsimd
        def _(pool):
            nc.gpsimd.memset(keep.ident[:], 0.0).then_inc(idents_cleared, 1)
            nc.gpsimd.memset(keep.ident16[:], 0.0).then_inc(idents_cleared, 1)
            pool.wait_ge(idents_cleared, 2)
            for ident in (keep.ident, keep.ident16):
                nc.gpsimd.affine_select(out=ident[:], in_=ident[:], compare_op=ALU.not_equal, fill=1.0,
                                        base=0, pattern=[[-1, P]], channel_multiplier=1)

    clear_semaphores(nc, [gates_loaded, idents_cleared])


def attention_phase(nc, keep, layer, x_in, ctx_in, lens, weights, biases, scratch):
    B, S, D = ctx_in.shape
    H, HD = 16, D // 16
    KC, TC = D // P, S // P
    causal = layer == 0
    scale = HD ** -0.5
    RUNS = (((0, 1, 2), 0), ((0, 1), 1), ((0,), 2))
    STACK = HD * sum(len(qs) for qs, _ in RUNS)
    MASK_ROWS = 0 if causal else 2
    MAX_ROW = STACK + MASK_ROWS
    HH = H // 2
    VW = 2 * HD
    GH = P // VW
    GROUPS = H // GH
    PER_BANK = 512 // S
    NP = 2 * GH
    gate_col = layer
    tag = f"a{layer}_"

    all_sems = []
    with ExitStack() as ctx:
        def sb(name, shape, dt=F32):
            return ctx.enter_context(nc.sbuf_tensor(tag + name, shape, dt))

        def pair(name, shape, dt=F32):
            return [sb(f"{name}{n}", shape, dt) for n in range(2)]

        def sem(name):
            s = ctx.enter_context(nc.semaphore(tag + name))
            all_sems.append(s)
            return s

        def sems(name):
            return [sem(f"{name}{n}") for n in range(2)]

        w_rows = sb("w_rows", [P, 4, KC, D])
        w_t = sb("w_t", [P, 3, KC, D])
        assert HH * HD == P
        ctx_rows = pair("ctx_rows", [P, TC, D])
        xn = pair("xn", [P, TC, D])
        xn_t = pair("xn_t", [P, KC, S])
        ctx_t = pair("ctx_t", [P, KC, S])
        stats = sb("stats", [P, TC, 6])
        mean_var = sb("mean_var", [P, TC, 2])
        var_eps = sb("var_eps", [P, TC])
        eps = sb("eps", [P, TC])
        minus_half = sb("minus_half", [P, TC])
        rstd = sb("rstd", [P, TC])
        qk = pair("qk", [P, 2 * KC, S])
        rest = sb("rest", [P, 2 * KC, S])
        parts = pair("parts", [P, 2 * KC, 3, S], BF16)
        q_stack = pair("q_stack", [P, H, S], BF16)
        k_stack = pair("k_stack", [P, H, S], BF16)
        v_ones = pair("v_ones", [P, TC, H, VW])
        row_max = sb("row_max", [P, TC, H])
        max_rest = sb("max_rest", [P, TC, H])
        max_parts = sb("max_parts", [P, TC, 3, H], BF16)
        max_t = pair("max_t", [3 * H, S], BF16)
        probs = [sb(f"probs{n}", [P, 512]) for n in range(NP)]
        wo_rows = sb("wo_rows", [P, KC, H, VW])
        wo_t = sb("wo_t", [P, GROUPS, D])
        den_rows = sb("den_rows", [P, GH])
        den_recip = sb("den_recip", [P, TC, H])
        strip_recip = sb("strip_recip", [P, TC, H, VW])
        mixed = sb("mixed", [P, GROUPS, S])
        heads_t = pair("heads_t", [P, GROUPS, S])
        if causal:
            mask_st = sb("mask_st", [P, 2, P], BF16)
            mask_ts = sb("mask_ts", [P, 2, P], BF16)
            bv_rows = sb("bv_rows", [P, TC, D])
            bo_rows = sb("bo_rows", [P, D])
        else:
            lens_i = sb("lens_i", [P, B], I32)
            lens_f = sb("lens_f", [P, B])
            iota_t = sb("iota_t", [P, S])
            neg_col = sb("neg_col", [P, 1])
            valid = sb("valid", [P, S])
            mask_row = pair("mask_row", [P, S], BF16)

        stage = [ctx.enter_context(nc.psum_tensor(f"{tag}stage{n}", [P, 512], F32)) for n in range(2)]
        scores = [ctx.enter_context(nc.psum_tensor(f"{tag}scores{n}", [P, 512], F32)) for n in range(2)]
        scores_t = [ctx.enter_context(nc.psum_tensor(f"{tag}scores_t{n}", [P, 512], F32)) for n in range(2)]
        pv = [ctx.enter_context(nc.psum_tensor(f"{tag}pv{n}", [P, 512], F32)) for n in range(2)]

        w_loaded = sem("w_loaded")
        w_turned = sem("w_turned")
        w_ready = sem("w_ready")
        consts_loaded = sem("consts_loaded")
        consts_step = sem("consts_step")
        consts_ready = sem("consts_ready")
        bo_gated = sem("bo_gated")
        wo_cleared = sem("wo_cleared")
        wo_spread = sem("wo_spread")
        x_loaded = sems("x_loaded")
        ctx_loaded = sems("ctx_loaded")
        stats_done = sem("stats_done")
        mean_done = sem("mean_done")
        eps_added = sem("eps_added")
        rstd_done = sem("rstd_done")
        xn_ready = sem("xn_ready")
        x_biased = sem("x_biased")
        xn_turned = sem("xn_turned")
        ctx_turned = sem("ctx_turned")
        xn_t_ready = sem("xn_t_ready")
        ctx_t_ready = sem("ctx_t_ready")
        q_done = sem("q_done")
        k_done = sem("k_done")
        v_done = sem("v_done")
        q_ready = sem("q_ready")
        k_ready = sem("k_ready")
        v_ready = sem("v_ready")
        valid_done = sem("valid_done")
        part_hi = sem("part_hi")
        part_rest = sem("part_rest")
        part_mid = sem("part_mid")
        parts_ready = sem("parts_ready")
        parts_stored = sems("parts_stored")
        stacked = [sems(f"stacked_half{n}_") for n in range(2)]
        scores_done = sem("scores_done")
        maxed = sem("maxed")
        max_hi = sem("max_hi")
        max_r1 = sem("max_r1")
        max_mid = sem("max_mid")
        max_ready = sem("max_ready")
        max_turned = sem("max_turned")
        max_t_ready = sem("max_t_ready")
        max_stacked = sems("max_stacked")
        scores_t_done = sem("scores_t_done")
        probs_ready = sem("probs_ready")
        pv_done = sem("pv_done")
        mixed_ready = sem("mixed_ready")
        recip_done = sem("recip_done")
        recip_copied = sem("recip_copied")
        den_picked = sem("den_picked")
        recip_spread = sem("recip_spread")
        heads_t_ready = sem("heads_t_ready")
        o_done = sem("o_done")
        x_updated = sem("x_updated")

        x_tiles = x_in.rearrange("b (c p) d -> b p c d", p=P)
        ctx_tiles = ctx_in.rearrange("b (c p) d -> b p c d", p=P)
        N_CONSTS = 3 if causal else 1
        N_READY = 7

        FIRST, LAST, HEAD, TAIL = -3, B, 5, 7

        block = ctx.enter_context(nc.Block())

        @block.sync
        def _(sp):
            for n, w in enumerate(weights):
                sp.dma_start(w_rows[:, n], w.rearrange("(c p) d -> p c d", p=P)).then_inc(w_loaded, 16)
            if causal:
                bv, bo = biases
                for c in range(TC):
                    sp.dma_start(bv_rows[:, c], bv.rearrange("(a d) -> a d", a=1).to_broadcast((P, D))).then_inc(consts_loaded, 16)
                sp.dma_start(bo_rows[:], bo.rearrange("(a d) -> a d", a=1).to_broadcast((P, D))).then_inc(consts_loaded, 16)
            else:
                sp.dma_start(lens_i[:], lens.rearrange("(a n) -> a n", a=1).to_broadcast((P, B))).then_inc(consts_loaded, 16)
            for b in range(2):
                sp.dma_start(keep.x[:, TC * b:TC * b + TC, :], x_tiles[b]).then_inc(x_loaded[b], 16)
            sp.dma_start(ctx_rows[0][:], ctx_tiles[0]).then_inc(ctx_loaded[0], 16)
            sp.wait_ge(consts_ready, N_READY)

            def step(i):
                if i.has(5):
                    need(sp, stats_done, i.at(3) + 1)
                    sp.dma_start(keep.x[:, bass.ds(i.at(5) * TC, TC), :], x_tiles[i.at(5)]).then_inc(x_loaded[i.par(5)], 16)
                if i.has(4):
                    need(sp, ctx_turned, i.at(2) + 1)
                    sp.dma_start(ctx_rows[i.par(4)][:], ctx_tiles[i.at(4)]).then_inc(ctx_loaded[i.par(4)], 16)
                if i.has(2):
                    p = i.par(2)
                    need(sp, parts_ready, i.at(2) + 1)
                    sp.dma_start(scratch[p].rearrange("n j p s -> p (n j) s"), parts[p][:].rearrange("p n j s -> p (n j) s")).then_inc(parts_stored[p], 16)
                    need(sp, parts_stored[p], (i.half(2) + 1) * 16)
                    for half in range(2):
                        need(sp, scores_t_done, i.at(0) * H + HH * (half + 1))
                        hs = slice(half * HH, half * HH + HH)
                        row = 0
                        for qs, k in RUNS:
                            rows = slice(row, row + HD * len(qs))
                            row = rows.stop
                            q_src = scratch[p][half, qs[0]:qs[-1] + 1].rearrange("j (d h) s -> (j d) (h s)", d=HD)
                            k_src = scratch[p][KC + half, k:k + 1].rearrange("a (d h) s -> a d (h s)", d=HD)
                            sp.dma_start(q_stack[p][rows, hs, :].rearrange("r h s -> r (h s)"), q_src).then_inc(stacked[half][p], 16)
                            sp.dma_start(k_stack[p][rows, hs, :].rearrange("r h s -> r (h s)"),
                                         k_src.to_broadcast((len(qs), HD, HH * S))).then_inc(stacked[half][p], 16)
                        if not causal:
                            row = mask_row[p][STACK:STACK + 2, :].unsqueeze(1).to_broadcast((2, HH, S))
                            sp.dma_start(k_stack[p][STACK:STACK + 2, hs, :], row).then_inc(stacked[half][p], 16)

            pipeline(sp, step, B, FIRST, LAST, HEAD, TAIL)

        STACK_DMAS = 2 * len(RUNS) + (0 if causal else 1)

        @block.gpsimd
        def _(pool):
            nc.gpsimd.memset(eps[:], LN_EPS)
            nc.gpsimd.memset(wo_rows[:], 0.0).then_inc(wo_cleared, 1)
            nc.gpsimd.memset(den_rows[:], 0.0).then_inc(wo_cleared, 1)
            pool.wait_ge(wo_cleared, 2)
            nc.gpsimd.affine_select(out=den_rows[:], in_=den_rows[:], compare_op=ALU.not_equal, fill=1.0,
                                    base=-HD, pattern=[[-VW, GH]], channel_multiplier=1).then_inc(wo_cleared, 1)
            nc.gpsimd.memset(minus_half[:], -0.5).then_inc(consts_step, 1)
            if causal:
                nc.gpsimd.memset(mask_st[:], 0.0).then_inc(consts_step, 1)
                nc.gpsimd.memset(mask_ts[:], 0.0).then_inc(consts_step, 1)
                pool.wait_ge(consts_step, 3)
                nc.gpsimd.affine_select(out=mask_st[:], in_=mask_st[:], compare_op=ALU.is_gt, fill=CAUSAL_FILL,
                                        base=0, pattern=[[0, 2], [-1, P]], channel_multiplier=1).then_inc(consts_step, 1)
                nc.gpsimd.affine_select(out=mask_ts[:], in_=mask_ts[:], compare_op=ALU.is_gt, fill=CAUSAL_FILL,
                                        base=0, pattern=[[0, 2], [1, P]], channel_multiplier=-1).then_inc(consts_step, 1)
                pool.wait_ge(consts_step, 5)
                nc.gpsimd.memset(mask_st[0:1, 0, 0:1], 0.0).then_inc(consts_step, 1)
                nc.gpsimd.memset(mask_ts[0:1, 0, 0:1], 0.0).then_inc(consts_step, 1)
                pool.wait_ge(consts_step, 7)
            else:
                nc.gpsimd.iota(iota_t[:], pattern=[[1, S]], base=0, channel_multiplier=0,
                               allow_small_or_imprecise_dtypes=True).then_inc(consts_step, 1)
                nc.gpsimd.memset(neg_col[:], NEG_LO).then_inc(consts_step, 1)
                pool.wait_ge(consts_step, 3)
                nc.gpsimd.memset(neg_col[STACK:STACK + 1, :], NEG_HI).then_inc(consts_step, 1)
                pool.wait_ge(consts_step, 4)
            nc.gpsimd.memset(var_eps[:], 1.0).then_inc(consts_ready, 1)

            def rstd_of(b, base):
                pool.wait_ge(mean_done, b + 1)
                nc.gpsimd.tensor_tensor(var_eps[:], mean_var[:, :, 1], eps[:], ALU.add).then_inc(eps_added, 1)
                pool.wait_ge(eps_added, b + 1)
                nc.gpsimd.tensor_tensor(rstd[:], var_eps[:], minus_half[:], ALU.pow).then_inc(rstd_done, 1)
                if causal:
                    pool.wait_ge(xn_ready, b + 1)
                    if isinstance(b, int) and b == 0:
                        pool.wait_ge(bo_gated, 1)
                    rows = keep.x[:, bass.ds(b * TC, TC), :] if not isinstance(b, int) else keep.x[:, b * TC:b * TC + TC, :]
                    nc.gpsimd.tensor_tensor(rows, rows, bo_rows[:].unsqueeze(1).to_broadcast((P, TC, D)), ALU.add).then_inc(x_biased, 1)

            rstd_of(0, 0)

            def step(i):
                if i.has(4):
                    rstd_of(i.at(4), 0)

            pipeline(pool, step, B, FIRST, LAST, HEAD, TAIL)

        @block.vector
        def _(dve):
            for n in range(2):
                nc.vector.memset(v_ones[n][:], 1.0).then_inc(consts_ready, 1)
                nc.vector.memset(q_stack[n][STACK:P, :, :], 1.0).then_inc(consts_ready, 1)
                nc.vector.memset(k_stack[n][STACK:P, :, :], 1.0).then_inc(consts_ready, 1)
            dve.wait_ge(consts_ready, N_READY)
            dve.wait_ge(consts_loaded, 16 * N_CONSTS)
            if causal:
                nc.vector.tensor_scalar(bo_rows[:], bo_rows[:], keep.tanh_gates[:, gate_col:gate_col + 1], None, ALU.mult).then_inc(bo_gated, 1)
            else:
                nc.vector.tensor_copy(lens_f[:], lens_i[:]).then_inc(bo_gated, 1)
                dve.wait_ge(bo_gated, 1)

            def ln_stats(b, n, x_par):
                dve.wait_ge(x_loaded[x_par], (n + 1) * 16)
                for c in range(TC):
                    last = nc.vector.bn_stats(stats[:, c, :], keep.x[:, b * TC + c, :])
                last.then_inc(stats_done, 1)

            def ln_mean(b):
                for c in range(TC):
                    last = nc.vector.bn_aggr(mean_var[:, c, :], stats[:, c, :])
                last.then_inc(mean_done, 1)

            def ln_apply(b, p):
                dve.wait_ge(rstd_done, b + 1)
                need(dve, xn_turned, b - 1)
                for c in range(TC):
                    last = nc.vector.tensor_scalar(xn[p][:, c, :], keep.x[:, b * TC + c, :], mean_var[:, c, 0:1],
                                                   rstd[:, c:c + 1], ALU.subtract, ALU.mult)
                last.then_inc(xn_ready, 1)

            dve.wait_ge(wo_cleared, 2)
            dve.wait_ge(w_loaded, 64)
            for c in range(KC):
                last = nc.vector.tensor_copy(wo_rows[:, c, :, 0:HD], w_rows[:, 3, c, :].rearrange("p (h w) -> p h w", w=HD))
            last.then_inc(wo_spread, 1)
            ln_stats(0, 0, 0)
            dve.wait_ge(stats_done, 1)
            ln_mean(0)
            ln_apply(0, 0)

            def evac_k(i):
                b, p = i.at(2), i.par(2)
                need(dve, part_rest, b - 1)
                if causal:
                    dve.wait_ge(k_done, b + 1)
                    nc.vector.tensor_copy(qk[p][:, KC:2 * KC, :].rearrange("p c s -> p (c s)"), stage[0][:]).then_inc(k_ready, 1)
                else:
                    n = bass.ds(b, 1)
                    nc.vector.tensor_scalar(valid[:], iota_t[:], lens_f[:, n], None, ALU.is_lt).then_inc(valid_done, 1)
                    if i.has(0):
                        dve.wait_ge(stacked[1][p], i.half(2) * 16 * STACK_DMAS)
                    nc.vector.tensor_scalar(mask_row[p][STACK:STACK + 2, :], iota_t[STACK:STACK + 2, :], lens_f[STACK:STACK + 2, n],
                                            neg_col[STACK:STACK + 2, :], ALU.is_ge, ALU.mult).then_inc(valid_done, 1)
                    dve.wait_ge(valid_done, 2 * b + 2)
                    dve.wait_ge(k_done, b + 1)
                    nc.vector.tensor_tensor(qk[p][:, KC:2 * KC, :], stage[0][:].rearrange("p (c s) -> p c s", c=KC),
                                            valid[:].unsqueeze(1).to_broadcast((P, KC, S)), ALU.mult).then_inc(k_ready, 1)

            def step(i):
                if i.has(-1):
                    b, p = i.at(-1), i.par(-1)
                    dve.wait_ge(den_picked, b + 1)
                    nc.vector.reciprocal(den_recip[:].rearrange("p c h -> p (c h)"), stage[1][:, 0:TC * H]).then_inc(recip_done, 1)
                if i.has(2):
                    evac_k(i)
                if i.has(-1):
                    b, p = i.at(-1), i.par(-1)
                    need(dve, o_done, b - 1)
                    for n in range(GROUPS // PER_BANK):
                        gs = slice(n * PER_BANK, (n + 1) * PER_BANK)
                        dve.wait_ge(recip_spread, b * (GROUPS // PER_BANK) + n + 1)
                        nc.vector.tensor_tensor(heads_t[p][:, gs, :].rearrange("p g s -> p (g s)"), mixed[:, gs, :].rearrange("p g s -> p (g s)"),
                                                pv[n][:], ALU.mult).then_inc(heads_t_ready, 1)

                def update_x():
                    b = i.at(-1)
                    dve.wait_ge(o_done, b + 1)
                    if causal:
                        dve.wait_ge(x_biased, b + 1)
                    rows = keep.x[:, bass.ds(b * TC, TC), :].rearrange("p c d -> p (c d)")
                    nc.vector.scalar_tensor_tensor(out=rows, in0=stage[1][:], scalar=keep.tanh_gates[:, gate_col:gate_col + 1],
                                                   in1=rows, op0=ALU.mult, op1=ALU.add).then_inc(x_updated, 1)

                def evac_v():
                    b, p = i.at(1), i.par(1)
                    dve.wait_ge(v_done, b + 1)
                    need(dve, pv_done, (b - 1) * GROUPS)
                    out = v_ones[p][:].rearrange("p c h w -> p (c h) w")[:, :, 0:HD]
                    src = stage[1][:].rearrange("p (n w) -> p n w", w=HD)
                    if causal:
                        nc.vector.tensor_tensor(out, src, bv_rows[:].rearrange("p c (h w) -> p (c h) w", w=HD), ALU.add).then_inc(v_ready, 1)
                    else:
                        nc.vector.tensor_copy(out, src).then_inc(v_ready, 1)

                def cut_rest():
                    dve.wait_ge(part_hi, i.at(2) + 1)
                    p = i.par(2)
                    nc.vector.tensor_tensor(rest[:], qk[p][:], parts[p][:, :, 0, :], ALU.subtract).then_inc(part_rest, 1)

                def cut_lo():
                    dve.wait_ge(part_mid, i.at(2) + 1)
                    p = i.par(2)
                    nc.vector.tensor_tensor(parts[p][:, :, 2, :], rest[:], parts[p][:, :, 1, :], ALU.subtract).then_inc(parts_ready, 1)

                between = {}
                if i.has(-1):
                    between |= {3: update_x}
                if i.has(1):
                    between |= {6: evac_v}
                if i.has(2):
                    between |= {4: cut_rest, 8: cut_lo}
                if i.has(4):
                    b4 = i.at(4)
                    between |= {10: lambda: ln_stats(b4, i.half(4), i.par(4)), 11: lambda: ln_mean(b4), 13: lambda: ln_apply(b4, i.par(4))}
                for h in range(H):
                    if h == 11 and i.has(4):
                        dve.wait_ge(stats_done, i.at(4) + 1)
                    if i.has(1):
                        dve.wait_ge(scores_done, i.at(1) * H + h + 1)
                        bank = scores[h % 2]
                        if causal:
                            nc.vector.reduce_max(row_max[:, 0, h:h + 1], bank[:, 0:P], AX_X)
                            nc.vector.reduce_max(row_max[:, 1, h:h + 1], bank[:, P:3 * P], AX_X).then_inc(maxed, 1)
                        else:
                            nc.vector.reduce_max(row_max[:, :, h], bank[:].rearrange("p (c t) -> p c t", c=TC), AX_X).then_inc(maxed, 1)
                    if h in between:
                        between[h]()
                if i.has(1):
                    b = i.at(1)
                    dve.wait_ge(maxed, (b + 1) * H)
                    need(dve, max_turned, b)
                    nc.vector.tensor_scalar(max_parts[:, :, 0, :], row_max[:], -1.0, None, ALU.mult).then_inc(max_hi, 1)
                    dve.wait_ge(max_hi, b + 1)
                    nc.vector.scalar_tensor_tensor(out=max_rest[:], in0=row_max[:], scalar=-1.0, in1=max_parts[:, :, 0, :],
                                                   op0=ALU.mult, op1=ALU.subtract).then_inc(max_r1, 1)
                    dve.wait_ge(max_r1, b + 1)
                    nc.vector.tensor_copy(max_parts[:, :, 1, :], max_rest[:]).then_inc(max_mid, 1)
                    dve.wait_ge(max_mid, b + 1)
                    nc.vector.tensor_tensor(max_parts[:, :, 2, :], max_rest[:], max_parts[:, :, 1, :], ALU.subtract).then_inc(max_ready, 1)

            pipeline(dve, step, B, FIRST, LAST, HEAD, TAIL)

        @block.scalar
        def _(act):
            for n in range(3):
                act.wait_ge(w_turned, n + 1)
                if n < 2:
                    nc.scalar.activation(w_t[:, n].rearrange("p c (o d h) -> p (c o) d h", o=KC, d=HD),
                                         stage[n % 2][:].rearrange("p (c h d) -> p c d h", c=KC * KC, d=HD), ACT.Copy).then_inc(w_ready, 1)
                else:
                    nc.scalar.activation(w_t[:, n].rearrange("p c d -> p (c d)"), stage[n % 2][:], ACT.Copy).then_inc(w_ready, 1)
            for n in range(GROUPS // 2):
                act.wait_ge(w_turned, 4 + n)
                nc.scalar.activation(wo_t[:, 2 * n:2 * n + 2].rearrange("p g d -> p (g d)"), stage[(3 + n) % 2][:], ACT.Copy).then_inc(w_ready, 1)

            def cut_hi(i):
                b, p = i.at(2), i.par(2)
                act.wait_ge(q_ready, b + 1)
                act.wait_ge(k_ready, b + 1)
                need(act, parts_stored[p], i.half(2) * 16)
                nc.scalar.activation(parts[p][:, :, 0, :], qk[p][:], ACT.Copy).then_inc(part_hi, 1)

            def cut_mid(i):
                act.wait_ge(part_rest, i.at(2) + 1)
                nc.scalar.activation(parts[i.par(2)][:, :, 1, :], rest[:], ACT.Copy).then_inc(part_mid, 1)

            def evac_xn(i):
                b, p = i.at(3), i.par(3)
                act.wait_ge(xn_turned, b + 1)
                need(act, q_done, b - 1)
                nc.scalar.activation(xn_t[p][:].rearrange("p c s -> p (c s)"), stage[0][:], ACT.Copy).then_inc(xn_t_ready, 1)

            def evac_ctx(i):
                b, p = i.at(3), i.par(3)
                act.wait_ge(ctx_turned, b + 1)
                need(act, v_done, b - 1)
                nc.scalar.activation(ctx_t[p][:].rearrange("p c s -> p (c s)"), stage[1][:], ACT.Copy).then_inc(ctx_t_ready, 1)

            def copy_mixed(i, n):
                b = i.at(0)
                act.wait_ge(pv_done, b * GROUPS + (n + 1) * PER_BANK)
                need(act, heads_t_ready, (b - 1) * (GROUPS // PER_BANK) + n + 1)
                nc.scalar.activation(mixed[:, n * PER_BANK:(n + 1) * PER_BANK, :].rearrange("p g s -> p (g s)"),
                                     pv[n][:], ACT.Copy).then_inc(mixed_ready, 1)

            def step(i):
                if i.has(2):
                    b, p = i.at(2), i.par(2)
                    act.wait_ge(q_done, b + 1)
                    need(act, part_rest, b - 1)
                    nc.scalar.activation(qk[p][:, 0:KC, :].rearrange("p c s -> p (c s)"), stage[0][:], ACT.Copy, scale=scale).then_inc(q_ready, 1)
                if i.has(0):
                    b, p = i.at(0), i.par(0)
                    act.wait_ge(max_turned, b + 1)
                    need(act, max_stacked[p], i.half(0) * 48)
                    nc.scalar.activation(max_t[p][:], stage[1][0:3 * H, 0:S // 2].bitcast(BF16), ACT.Copy).then_inc(max_t_ready, 1)
                    act.wait_ge(max_t_ready, b + 1)
                    for j in range(3):
                        act.dma_start(q_stack[p][MAX_ROW + j:MAX_ROW + j + 1, :, :],
                                      max_t[p][j * H:(j + 1) * H, :]).then_inc(max_stacked[p], 16)
                if i.has(-1):
                    b = i.at(-1)
                    act.wait_ge(recip_done, b + 1)
                    need(act, recip_spread, b * (GROUPS // PER_BANK))
                    nc.scalar.activation(strip_recip[:].rearrange("p c h w -> p (c h) w"),
                                         den_recip[:].rearrange("p c h -> p (c h)").unsqueeze(2).to_broadcast((P, TC * H, VW)),
                                         ACT.Copy).then_inc(recip_copied, 1)
                between = {}
                if i.has(0):
                    between |= {12: lambda: copy_mixed(i, 0), 15: lambda: copy_mixed(i, 1)}
                if i.has(2):
                    between |= {1: lambda: cut_hi(i), 5: lambda: cut_mid(i)}
                if i.has(3):
                    between |= {9: lambda: evac_xn(i), 11: lambda: evac_ctx(i)}
                for h in range(H):
                    if i.has(0):
                        b = i.at(0)
                        width = 3 * P if causal else 4 * P
                        act.wait_ge(scores_t_done, b * H + h + 1)
                        if h % GH == 0:
                            need(act, pv_done, b * GROUPS + h // GH - 1)
                        nc.scalar.activation(probs[h % NP][:, 0:width], scores_t[h % 2][:, 0:width], ACT.Exp).then_inc(probs_ready, 1)
                    if h in between:
                        between[h]()

            pipeline(act, step, B, FIRST, LAST, HEAD, TAIL)

        @block.tensor
        def _(pe):
            pe.wait_ge(w_loaded, 64)
            for n in range(3):
                need(pe, w_ready, n - 1)
                for kc in range(KC):
                    for oc in range(KC):
                        last = nc.tensor.transpose(stage[n % 2][:, kc * D + oc * P:kc * D + oc * P + P],
                                                   w_rows[:, n, oc, kc * P:kc * P + P], keep.ident[:])
                last.then_inc(w_turned, 1)
            pe.wait_ge(wo_spread, 1)
            pe.wait_ge(wo_cleared, 3)
            for n in range(GROUPS // 2):
                pe.wait_ge(w_ready, n + 2)
                for k in range(2):
                    g = 2 * n + k
                    for oc in range(KC):
                        last = nc.tensor.transpose(stage[(3 + n) % 2][:, k * D + oc * P:k * D + oc * P + P],
                                                   wo_rows[:, oc, g * GH:(g + 1) * GH, :].rearrange("p h w -> p (h w)"), keep.ident[:])
                last.then_inc(w_turned, 1)
            pe.wait_ge(w_ready, 3 + GROUPS // 2)
            pe.wait_ge(consts_ready, N_READY)

            def turn(bank, rows, done):
                for kc in range(KC):
                    for c in range(TC):
                        last = nc.tensor.transpose(bank[:, kc * S + c * P:kc * S + c * P + P], rows[:, c, kc * P:kc * P + P], keep.ident[:])
                last.then_inc(done, 1)

            def project_t(bank, n, cols, done):
                for m in range(KC):
                    for kc in range(KC):
                        last = nc.tensor.matmul(bank[:, m * S:(m + 1) * S], w_t[:, n, kc, m * P:(m + 1) * P], cols[:, kc, :],
                                                start=(kc == 0), stop=(kc == KC - 1))
                last.then_inc(done, 1)

            def project(bank, n, cols, done):
                for c in range(TC):
                    for kc in range(KC):
                        last = nc.tensor.matmul(bank[:, c * D:(c + 1) * D], cols[:, kc, c * P:(c + 1) * P], w_t[:, n, kc, :],
                                                start=(kc == 0), stop=(kc == KC - 1))
                last.then_inc(done, 1)

            def pick_dens(i):
                pe.wait_ge(mixed_ready, i.at(-1) * 2 + 2)
                for c in range(TC):
                    for g in range(GROUPS):
                        at = c * H + g * GH
                        last = nc.tensor.matmul(stage[1][:, at:at + GH], mixed[:, g, c * P:(c + 1) * P], den_rows[:], start=True, stop=True)
                last.then_inc(den_picked, 1)

            def spread_recips(i):
                pe.wait_ge(recip_copied, i.at(-1) + 1)
                for g in range(GROUPS):
                    for c in range(TC):
                        at = g % PER_BANK * S + c * P
                        last = nc.tensor.matmul(pv[g // PER_BANK][:, at:at + P],
                                                strip_recip[:, c, g * GH:(g + 1) * GH, :].rearrange("p h w -> p (h w)"),
                                                keep.ident[:], start=True, stop=True)
                    if g % PER_BANK == PER_BANK - 1:
                        last.then_inc(recip_spread, 1)

            def front(i):
                if i.has(0):
                    need(pe, ctx_t_ready, i.upto(2))
                    need(pe, v_ready, i.upto(0))
                    need(pe, x_updated, i.at(-1))
                if i.has(2):
                    b, p = i.at(2), i.par(2)
                    pe.wait_ge(xn_t_ready, b + 1)
                    project_t(stage[0], 0, xn_t[p], q_done)
                if i.has(0):
                    wait_apart(pe, max_ready, i.at(0) + 1, consts_ready, N_READY)
                    turned = stage[1][0:3 * H, 0:S // 2].bitcast(BF16)
                    for c in range(TC):
                        last = nc.tensor.transpose(turned[:, c * P:(c + 1) * P], max_parts[:, c].rearrange("p j h -> p (j h)"), keep.ident16[:])
                    last.then_inc(max_turned, 1)
                if i.has(-1):
                    need(pe, max_t_ready, i.upto(0))
                    need(pe, v_ready, i.upto(0))
                    need(pe, x_updated, i.at(-1))
                    pick_dens(i)
                if i.has(2):
                    b, p = i.at(2), i.par(2)
                    pe.wait_ge(ctx_t_ready, b + 1)
                    pe.wait_ge(q_ready, b + 1)
                    project_t(stage[0], 1, ctx_t[p], k_done)
                if i.has(-1):
                    spread_recips(i)

            def project_heads(i):
                pe.wait_ge(heads_t_ready, i.at(-1) * 2 + 2)
                for c in range(TC):
                    for g in range(GROUPS):
                        last = nc.tensor.matmul(stage[1][:, c * D:(c + 1) * D], heads_t[i.par(-1)][:, g, c * P:(c + 1) * P], wo_t[:, g, :],
                                                start=(g == 0), stop=(g == GROUPS - 1))
                last.then_inc(o_done, 1)

            def project_v(i):
                need(pe, ctx_t_ready, i.upto(2))
                need(pe, max_t_ready, i.upto(0))
                need(pe, x_updated, i.at(0))
                project(stage[1], 2, ctx_t[i.par(1)], v_done)

            def turn_xn(i):
                b, p = i.at(3), i.par(3)
                pe.wait_ge(xn_ready, b + 1)
                need(pe, k_ready, i.upto(2))
                turn(stage[0], xn[p], xn_turned)

            def turn_ctx(i):
                p = i.par(3)
                pe.wait_ge(ctx_loaded[p], (i.half(3) + 1) * 16)
                need(pe, v_ready, i.upto(1))
                need(pe, x_updated, i.at(0))
                turn(stage[1], ctx_rows[p], ctx_turned)

            def score_head(i, h):
                b, p = i.at(1), i.par(1)
                if h % HH == 0:
                    pe.wait_ge(stacked[h // HH][p], (i.half(1) + 1) * 16 * STACK_DMAS)
                need(pe, maxed, b * H + h - 1)
                bank, q, k = scores[h % 2], q_stack[p], k_stack[p]
                rows = slice(0, STACK + MASK_ROWS)
                if causal:
                    nc.tensor.matmul(bank[:, 0:P], keep.ident16[:], mask_st[:, 0, :], start=True, stop=False)
                    nc.tensor.matmul(bank[:, 0:P], q[rows, h, 0:P], k[rows, h, 0:P], start=False, stop=True)
                    nc.tensor.matmul(bank[:, P:2 * P], q[rows, h, P:S], k[rows, h, 0:P], start=True, stop=True)
                    nc.tensor.matmul(bank[:, 2 * P:3 * P], keep.ident16[:], mask_st[:, 1, :], start=True, stop=False)
                    last = nc.tensor.matmul(bank[:, 2 * P:3 * P], q[rows, h, P:S], k[rows, h, P:S], start=False, stop=True)
                else:
                    for c in range(TC):
                        last = nc.tensor.matmul(bank[:, c * S:(c + 1) * S], q[rows, h, c * P:(c + 1) * P], k[rows, h, :], start=True, stop=True)
                last.then_inc(scores_done, 1)

            def score_head_t(i, h):
                b, p = i.at(0), i.par(0)
                if h == 0:
                    pe.wait_ge(max_stacked[p], (i.half(0) + 1) * 48)
                need(pe, probs_ready, b * H + h - 1)
                bank, q, k = scores_t[h % 2], q_stack[p], k_stack[p]
                rows = slice(0, MAX_ROW + 3)
                if causal:
                    nc.tensor.matmul(bank[:, 0:P], keep.ident16[:], mask_ts[:, 0, :], start=True, stop=False)
                    nc.tensor.matmul(bank[:, 0:P], k[rows, h, 0:P], q[rows, h, 0:P], start=False, stop=True)
                    nc.tensor.matmul(bank[:, P:2 * P], k[rows, h, 0:P], q[rows, h, P:S], start=True, stop=True)
                    nc.tensor.matmul(bank[:, 2 * P:3 * P], keep.ident16[:], mask_ts[:, 1, :], start=True, stop=False)
                    last = nc.tensor.matmul(bank[:, 2 * P:3 * P], k[rows, h, P:S], q[rows, h, P:S], start=False, stop=True)
                else:
                    for c in range(TC):
                        last = nc.tensor.matmul(bank[:, c * S:(c + 1) * S], k[rows, h, c * P:(c + 1) * P], q[rows, h, :], start=True, stop=True)
                last.then_inc(scores_t_done, 1)

            def mix_group(i, g):
                b, p = i.at(0), i.par(0)
                pe.wait_ge(probs_ready, b * H + (g + 1) * GH)
                if g == 0:
                    pe.wait_ge(v_ready, b + 1)
                if g % PER_BANK == 0:
                    need(pe, heads_t_ready, (b - 1) * 2 + g // PER_BANK + 1)
                bank, at = pv[g // PER_BANK], g % PER_BANK * S
                for t in range(TC):
                    first, col = (t * P, t * S) if causal else (0, t * S)
                    for n in range(GH):
                        h = g * GH + n
                        last = nc.tensor.matmul(bank[n * VW:(n + 1) * VW, at + first:at + S], v_ones[p][:, t, h, :],
                                                probs[h % NP][:, col:col + S - first], start=(t == 0), stop=(t == TC - 1),
                                                tile_position=(0, n * VW))
                last.then_inc(pv_done, 1)

            def step(i):
                front(i)
                between = {}
                if i.has(-1):
                    between |= {2: project_heads}
                if i.has(1):
                    between |= {5: project_v}
                if i.has(3):
                    between |= {8: turn_xn, 10: turn_ctx}
                for h in range(H):
                    if i.has(1):
                        score_head(i, h)
                    if i.has(0):
                        score_head_t(i, h)
                        if h % GH == 1 and h > GH:
                            mix_group(i, h // GH - 1)
                    if h in between:
                        between[h](i)
                if i.has(0):
                    mix_group(i, GROUPS - 1)

            pipeline(pe, step, B, FIRST, LAST, HEAD, TAIL)

    clear_semaphores(nc, all_sems)


TS = 256
TT = TS // P
ROW = 258
EXPERTS = 8


def region_rows(tokens):
    return tokens + TS


def tile_count(tokens):
    return 2 * tokens // TS + EXPERTS


def routed_rows(tokens):
    return EXPERTS * region_rows(tokens) + (EXPERTS + 1) * TS


class Routed:

    def __init__(self, nc, ctx, tag, tokens, F):
        def sb(name, shape, dt):
            return ctx.enter_context(nc.sbuf_tensor(f"{tag}_{name}", shape, dt))

        tiles = tile_count(tokens)
        self.tile_expert = sb("tile_expert", [P, 1 + tiles], I32)
        self.tile_group = sb("tile_group", [P, 1 + tiles], I32)
        self.tile_row = sb("tile_row", [P, tiles], I32)
        self.up_bias = sb("up_bias", [P, EXPERTS * F // P], F32)


def route_phase(nc, keep, routed, layer, F, up_b, gate, shared, xs, x_acc):
    NT = keep.x.shape[1]
    D = keep.x.shape[2]
    C, KC = 2, D // P
    S = C * P
    NB = NT // C
    tokens = NT * P
    R = region_rows(tokens)
    E = EXPERTS
    FC = F // P
    tiles = tile_count(tokens)
    soft = layer == 0
    gate_col = 2 + layer
    GW = E if soft else D + E
    tag = f"r{layer}_"
    J = tokens // TS

    all_sems = []
    with ExitStack() as ctx:
        def sb(name, shape, dt=F32):
            return ctx.enter_context(nc.sbuf_tensor(tag + name, shape, dt))

        def sem(name):
            s = ctx.enter_context(nc.semaphore(tag + name))
            all_sems.append(s)
            return s

        rows = [sb(f"rows{n}", [P, 2, C, ROW]) for n in range(2)]
        stats = sb("stats", [P, C, 6])
        mean_var = sb("mean_var", [P, C, 2])
        var_eps = sb("var_eps", [P, C])
        eps = sb("eps", [P, C])
        minus_half = sb("minus_half", [P, C])
        rstd = sb("rstd", [P, C])
        xn_t = sb("xn_t", [P, KC, S])
        gate_w = sb("gate_w", [P, KC, GW])
        scores = sb("scores", [P, C, E])
        top = sb("top", [P, C, E])
        top_index = sb("top_index", [P, C, E], U32)
        top_index_f = sb("top_index_f", [P, 2, C])
        below_top = sb("below_top", [P, C, E])
        exps = sb("exps", [P, C, E])
        exp_sum = sb("exp_sum", [P, C])
        exp_recip = sb("exp_recip", [P, C])
        share = sb("share", [P, C, 2])
        share_sum = sb("share_sum", [P, C])
        share_recip = sb("share_recip", [P, C])
        one_hot = sb("one_hot", [P, 2, C, E])
        chosen = sb("chosen", [P, C, E], BF16)
        next_row = sb("next_row", [P, E])
        place = sb("place", [P, C, E])
        place_of = sb("place_of", [P, 2, C, E])
        slot_f = sb("slot_f", [P, 2, C])
        slot = [sb(f"slot{n}", [P, 2, C], U32) for n in range(2)]
        expert_iota = sb("expert_iota", [P, E])
        region_start = sb("region_start", [P, E])
        token_ids = sb("token_ids", [P, NT])
        ones16 = sb("ones16", [P, P], BF16)
        before16 = sb("before16", [P, P], BF16)
        pad_rows = sb("pad_rows", [P, TT, ROW])
        pad_offset = sb("pad_offset", [P, TT])
        pad_slot_f = sb("pad_slot_f", [P, E, TT])
        pad_slot = sb("pad_slot", [P, E, TT], U32)
        count = sb("count", [P, E])
        full_steps = sb("full_steps", [P, J])
        beyond = sb("beyond", [P, E, J])
        n_tiles = sb("n_tiles", [P, E])
        ends = sb("ends", [P, E])
        tile_iota = sb("tile_iota", [P, tiles])
        past = sb("past", [P, tiles, E])
        past_tiles = sb("past_tiles", [P, tiles, E])
        region = sb("region", [P, tiles])
        first_tile = sb("first_tile", [P, tiles])
        in_region = sb("in_region", [P, tiles])
        row_f = sb("row_f", [P, tiles])
        group_f = sb("group_f", [P, tiles])
        up_b_rows = sb("up_b_rows", [E * FC, P])
        if soft:
            gate_rows = sb("gate_rows", [E, D])
            sh_up = sb("sh_up", [P, KC, D])
            sh_down = sb("sh_down", [P, KC, D])
            sh_up_bias = sb("sh_up_bias", [P, KC])
            sh_up_b_rows = sb("sh_up_b_rows", [KC, P])
            sh_down_bias = sb("sh_down_bias", [P, D])
            sh_hidden = sb("sh_hidden", [P, KC, S])
        else:
            wp_rows = sb("wp_rows", [P, KC, D])
            sim_rows = sb("sim_rows", [E, D])
            sim_sq = sb("sim_sq", [E, D])
            sim_ss = sb("sim_ss", [E, 1])
            sim_ss_min = sb("sim_ss_min", [E, 1])
            sim_rnorm = sb("sim_rnorm", [E, 1])
            sim_unit = sb("sim_unit", [E, D])
            sim_t = sb("sim_t", [P, KC, E])
            temp = sb("temp", [P, 1])
            temp_recip = sb("temp_recip", [P, 1])
            proj_sq = sb("proj_sq", [P, C, D])
            proj_ss = sb("proj_ss", [P, C])
            proj_ss_min = sb("proj_ss_min", [P, C])
            proj_rnorm = sb("proj_rnorm", [P, C])

        def bank(name):
            return ctx.enter_context(nc.psum_tensor(tag + name, [P, 512], F32))

        turned = bank("turned")
        gated = [bank(f"gated{n}") for n in range(2)]
        ranked = bank("ranked")
        sh_h = bank("sh_h")
        sh_y = bank("sh_y")

        w_loaded = sem("w_loaded")
        consts_step = sem("consts_step")
        consts_ready = sem("consts_ready")
        prep_turned = sem("prep_turned")
        prep_copied = sem("prep_copied")
        sim_step = sem("sim_step")
        temp_done = sem("temp_done")
        stats_done = sem("stats_done")
        mean_done = sem("mean_done")
        eps_added = sem("eps_added")
        rstd_done = sem("rstd_done")
        xn_ready = sem("xn_ready")
        rows_copied = sem("rows_copied")
        xn_turned = sem("xn_turned")
        xn_t_ready = sem("xn_t_ready")
        gate_done = sem("gate_done")
        ss_done = sem("ss_done")
        ss_floored = sem("ss_floored")
        rnorm_done = sem("rnorm_done")
        scores_ready = sem("scores_ready")
        top_done = sem("top_done")
        index_done = sem("index_done")
        below_done = sem("below_done")
        exps_done = sem("exps_done")
        index_f_done = sem("index_f_done")
        one_hot_done = sem("one_hot_done")
        chosen_ready = sem("chosen_ready")
        share_step = sem("share_step")
        rank_done = sem("rank_done")
        placed = sem("placed")
        counted = sem("counted")
        place_picked = sem("place_picked")
        slot_summed = sem("slot_summed")
        rows_ready = sem("rows_ready")
        rows_sent = keep.rows_sent[layer]
        pads_sent = keep.pads_sent[layer]
        table_step = sem("table_step")
        pad_slots_ready = sem("pad_slots_ready")
        x_stored = sem("x_stored")
        if soft:
            x_biased = sem("x_biased")
            sh_bias_gated = sem("sh_bias_gated")
            sh_up_done = sem("sh_up_done")
            sh_hidden_ready = sem("sh_hidden_ready")
            sh_down_done = sem("sh_down_done")
            x_updated = sem("x_updated")

        acc_tiles = x_acc[0:tokens, :].rearrange("(n c p) d -> n p c d", c=C, p=P)
        N_LOADS = 6 if soft else 4
        FIRST, LAST, HEAD, TAIL = 0, NB - 1, 2, 2
        SHARES = 5 if soft else 2

        block = ctx.enter_context(nc.Block())

        @block.sync
        def _(sp):
            sp.dma_start(up_b_rows[:], up_b.rearrange("e (c p) -> (e c) p", p=P)).then_inc(w_loaded, 16)
            if soft:
                sh_up_w, sh_up_b, sh_down_w, sh_down_b = shared
                sp.dma_start(gate_rows[:], gate[0]).then_inc(w_loaded, 16)
                sp.dma_start(sh_up[:], sh_up_w.rearrange("(c p) f -> p c f", p=P)).then_inc(w_loaded, 16)
                sp.dma_start(sh_down[:], sh_down_w.rearrange("(c p) d -> p c d", p=P)).then_inc(w_loaded, 16)
                sp.dma_start(sh_up_b_rows[:], sh_up_b.rearrange("(c p) -> c p", p=P)).then_inc(w_loaded, 16)
                sp.dma_start(sh_down_bias[:], sh_down_b.rearrange("(a d) -> a d", a=1).to_broadcast((P, D))).then_inc(w_loaded, 16)
            else:
                wp, sim, temperature = gate
                sp.dma_start(wp_rows[:], wp.rearrange("(c p) d -> p c d", p=P)).then_inc(w_loaded, 16)
                sp.dma_start(sim_rows[:], sim).then_inc(w_loaded, 16)
                sp.dma_start(temp[:], temperature.rearrange("(a d) -> a d", a=1).to_broadcast((P, 1))).then_inc(w_loaded, 16)
            sp.wait_ge(consts_ready, 1)
            for n in range(E + 1):
                at = E * R + n * TS
                sp.dma_start(xs[at:at + TS, :].rearrange("(c p) w -> p c w", p=P), pad_rows[:]).then_inc(x_stored, 16)
            sp.dma_start(x_acc[tokens:tokens + TS, :].rearrange("(c p) d -> p c d", p=P), pad_rows[:, :, 0:D]).then_inc(x_stored, 16)
            n_stores = E + 2
            if soft:
                with sp.Fori(0, NB) as b:
                    sp.wait_ge(x_updated, b + 1)
                    sp.dma_start(acc_tiles[b], keep.x[:, bass.ds(b * C, C), :]).then_inc(x_stored, 16)
                n_stores += NB
            else:
                sp.dma_start(x_acc[0:tokens, :].rearrange("(n p) d -> p n d", p=P), keep.x[:]).then_inc(x_stored, 16)
                n_stores += 1
            sp.wait_ge(x_stored, n_stores * 16)

        @block.gpsimd
        def _(pool):
            nc.gpsimd.memset(pad_rows[:], 0.0).then_inc(consts_step, 1)
            nc.gpsimd.iota(token_ids[:], pattern=[[P, NT]], base=0, channel_multiplier=1,
                           allow_small_or_imprecise_dtypes=True)
            nc.gpsimd.iota(expert_iota[:], pattern=[[1, E]], base=0, channel_multiplier=0, allow_small_or_imprecise_dtypes=True)
            nc.gpsimd.iota(region_start[:], pattern=[[R, E]], base=0, channel_multiplier=0, allow_small_or_imprecise_dtypes=True)
            nc.gpsimd.iota(next_row[:], pattern=[[R, E]], base=0, channel_multiplier=0, allow_small_or_imprecise_dtypes=True)
            nc.gpsimd.iota(pad_offset[:], pattern=[[P, TT]], base=0, channel_multiplier=1, allow_small_or_imprecise_dtypes=True)
            nc.gpsimd.iota(tile_iota[:], pattern=[[1, tiles]], base=0, channel_multiplier=0, allow_small_or_imprecise_dtypes=True)
            nc.gpsimd.iota(full_steps[:], pattern=[[TS, J]], base=0, channel_multiplier=0,
                           allow_small_or_imprecise_dtypes=True).then_inc(consts_step, 1)
            nc.gpsimd.memset(minus_half[:], -0.5)
            nc.gpsimd.memset(eps[:], LN_EPS)
            nc.gpsimd.memset(ones16[:], 1.0)
            nc.gpsimd.memset(before16[:], 1.0).then_inc(consts_step, 1)
            pool.wait_ge(consts_step, 3)
            nc.gpsimd.memset(full_steps[:, 0:1], -1.0).then_inc(consts_step, 1)
            nc.gpsimd.affine_select(out=before16[:], in_=before16[:], compare_op=ALU.is_gt, fill=0.0, base=0,
                                    pattern=[[1, P]], channel_multiplier=-1).then_inc(consts_step, 1)
            nc.gpsimd.iota(pad_rows[:, :, D + 1], pattern=[[P, TT]], base=tokens, channel_multiplier=1,
                           allow_small_or_imprecise_dtypes=True).then_inc(consts_step, 1)
            pool.wait_ge(consts_step, 6)
            nc.gpsimd.memset(rstd[:], 1.0).then_inc(consts_ready, 1)
            if not soft:
                pool.wait_ge(sim_step, 1)
                nc.gpsimd.tensor_scalar(sim_ss_min[:], sim_ss[:], 1e-24, None, ALU.max).then_inc(sim_step, 1)
                pool.wait_ge(sim_step, 2)
                nc.gpsimd.tensor_tensor(sim_rnorm[:], sim_ss_min[:], minus_half[0:E, 0:1], ALU.pow).then_inc(sim_step, 1)

            def add_eps(b):
                pool.wait_ge(mean_done, b + 1)
                nc.gpsimd.tensor_tensor(var_eps[:], mean_var[:, :, 1], eps[:], ALU.add).then_inc(eps_added, 1)

            def rstd_of(b):
                pool.wait_ge(eps_added, b + 1)
                nc.gpsimd.tensor_tensor(rstd[:], var_eps[:], minus_half[:], ALU.pow).then_inc(rstd_done, 1)

            def bias_x(b):
                pool.wait_ge(xn_ready, b + 1)
                if isinstance(b, int) and b == 0:
                    pool.wait_ge(sh_bias_gated, 1)
                x_rows = keep.x[:, bass.ds(b * C, C), :]
                nc.gpsimd.tensor_tensor(x_rows, x_rows, sh_down_bias[:].unsqueeze(1).to_broadcast((P, C, D)), ALU.add).then_inc(x_biased, 1)

            for b in range(2):
                add_eps(b)
                rstd_of(b)
                if soft:
                    bias_x(b)

            def step(i):
                b, p = i.at(0), i.par(0)
                if not soft:
                    pool.wait_ge(ss_floored, b + 1)
                    nc.gpsimd.tensor_tensor(proj_rnorm[:], proj_ss_min[:], minus_half[:], ALU.pow).then_inc(rnorm_done, 1)
                if i.has(2):
                    add_eps(i.at(2))
                pool.wait_ge(rows_ready, b + 1)
                pool.wait_ge(rows_copied, b + 1)
                if i.has(2):
                    rstd_of(i.at(2))
                for k in range(2):
                    for c in range(C):
                        pool.indirect_dma_start(out=xs, out_offset=bass.IndirectOffsetOnAxis(ap=slot[p][:, k, c:c + 1], axis=0),
                                                in_=rows[p][:, k, c, :], in_offset=None).then_inc(rows_sent[p], 16)
                if soft and i.has(2):
                    bias_x(i.at(2))

            pipeline(pool, step, NB, FIRST, LAST, HEAD, TAIL)
            pool.wait_ge(pad_slots_ready, 1)
            for e in range(E):
                for c in range(TT):
                    pool.indirect_dma_start(out=xs, out_offset=bass.IndirectOffsetOnAxis(ap=pad_slot[:, e, c:c + 1], axis=0),
                                            in_=pad_rows[:, c, :], in_offset=None).then_inc(pads_sent, 16)
            pool.wait_ge(pads_sent, 16 * E * TT)
            for n in range(2):
                pool.wait_ge(rows_sent[n], 16 * 2 * C * NB // 2)

        @block.vector
        def _(dve):
            dve.wait_ge(consts_ready, 1)
            dve.wait_ge(w_loaded, 16 * N_LOADS)
            if soft:
                nc.vector.tensor_scalar(sh_down_bias[:], sh_down_bias[:], keep.tanh_gates[:, gate_col:gate_col + 1], None, ALU.mult).then_inc(sh_bias_gated, 1)
            else:
                nc.vector.reciprocal(temp_recip[:], temp[:]).then_inc(temp_done, 1)
                dve.wait_ge(sim_step, 3)
                nc.vector.tensor_scalar(sim_unit[:], sim_rows[:], sim_rnorm[:, 0:1], None, ALU.mult).then_inc(sim_step, 1)

            def ln(b):
                for c in range(C):
                    last = nc.vector.bn_stats(stats[:, c, :], keep.x[:, b * C + c, :])
                last.then_inc(stats_done, 1)

            def ln_mean(b):
                for c in range(C):
                    last = nc.vector.bn_aggr(mean_var[:, c, :], stats[:, c, :])
                last.then_inc(mean_done, 1)

            def ln_apply(b, p, sent):
                dve.wait_ge(rstd_done, b + 1)
                need(dve, rows_sent[p], sent)
                for c in range(C):
                    last = nc.vector.tensor_scalar(rows[p][:, 0, c, 0:D], keep.x[:, b * C + c, :], mean_var[:, c, 0:1],
                                                   rstd[:, c:c + 1], ALU.subtract, ALU.mult)
                last.then_inc(xn_ready, 1)

            for b in range(2):
                ln(b)
                dve.wait_ge(stats_done, b + 1)
                ln_mean(b)
                ln_apply(b, b, 0)

            def step(i):
                b, p = i.at(0), i.par(0)
                dve.wait_ge(gate_done, b + 1)
                if soft:
                    nc.vector.tensor_copy(scores[:], gated[0][:, 0:C * E].rearrange("p (c e) -> p c e", c=C)).then_inc(scores_ready, 1)
                else:
                    dve.wait_ge(ss_done, b + 1)
                    nc.vector.tensor_scalar(proj_ss_min[:], proj_ss[:], 1e-24, None, ALU.max).then_inc(ss_floored, 1)
                    dve.wait_ge(rnorm_done, b + 1)
                    if i.off == 0:
                        dve.wait_ge(temp_done, 1)
                    for c in range(C):
                        last = nc.vector.tensor_scalar(scores[:, c, :], gated[c][:, D:D + E], proj_rnorm[:, c:c + 1], temp_recip[:, 0:1], ALU.mult, ALU.mult)
                    last.then_inc(scores_ready, 1)
                wait_apart(dve, scores_ready, b + 1, consts_ready, 1)
                for c in range(C):
                    last = nc.vector.max(top[:, c, :], scores[:, c, :])
                last.then_inc(top_done, 1)
                wait_apart(dve, top_done, b + 1, consts_ready, 1)
                for c in range(C):
                    last = nc.vector.max_index(top_index[:, c, :], top[:, c, :], scores[:, c, :])
                last.then_inc(index_done, 1)
                nc.vector.tensor_tensor(below_top[:], top[:], top[:, :, 0:1].to_broadcast((P, C, E)), ALU.subtract).then_inc(below_done, 1)
                dve.wait_ge(index_done, b + 1)
                nc.vector.tensor_copy(top_index_f[:].rearrange("p k c -> p c k"), top_index[:, :, 0:2]).then_inc(index_f_done, 1)
                dve.wait_ge(index_f_done, b + 1)
                nc.vector.tensor_tensor(one_hot[:].rearrange("p k c e -> p (k c) e"),
                                        expert_iota[:].unsqueeze(1).to_broadcast((P, 2 * C, E)),
                                        top_index_f[:].rearrange("p k c -> p (k c)").unsqueeze(2).to_broadcast((P, 2 * C, E)),
                                        ALU.is_equal).then_inc(one_hot_done, 1)
                dve.wait_ge(one_hot_done, b + 1)
                nc.vector.tensor_tensor(chosen[:], one_hot[:, 0], one_hot[:, 1], ALU.add).then_inc(chosen_ready, 1)
                dve.wait_ge(exps_done, b + 1)
                steps = b * SHARES
                if soft:
                    nc.vector.reduce_sum(exp_sum[:], exps[:], AX_X).then_inc(share_step, 1)
                    dve.wait_ge(share_step, steps + 1)
                    nc.vector.reciprocal(exp_recip[:], exp_sum[:]).then_inc(share_step, 1)
                    dve.wait_ge(share_step, steps + 2)
                    nc.vector.tensor_tensor(share[:], exps[:, :, 0:2], exp_recip[:].unsqueeze(2).to_broadcast((P, C, 2)), ALU.mult).then_inc(share_step, 1)
                    dve.wait_ge(share_step, steps + 3)
                    nc.vector.scalar_tensor_tensor(out=share_sum[:], in0=share[:, :, 0], scalar=1e-20, in1=share[:, :, 1],
                                                   op0=ALU.add, op1=ALU.add).then_inc(share_step, 1)
                    dve.wait_ge(share_step, steps + 4)
                    parts2 = share
                else:
                    nc.vector.tensor_tensor(share_sum[:], exps[:, :, 0], exps[:, :, 1], ALU.add).then_inc(share_step, 1)
                    dve.wait_ge(share_step, steps + 1)
                    parts2 = exps
                nc.vector.reciprocal(share_recip[:], share_sum[:]).then_inc(share_step, 1)
                dve.wait_ge(share_step, steps + SHARES)
                nc.vector.scalar_tensor_tensor(out=rows[p][:, :, :, D].rearrange("p k c -> p c k"), in0=parts2[:, :, 0:2],
                                               scalar=keep.tanh_gates[:, gate_col:gate_col + 1],
                                               in1=share_recip[:].unsqueeze(2).to_broadcast((P, C, 2)), op0=ALU.mult, op1=ALU.mult)
                nc.vector.tensor_copy(rows[p][:, :, :, D + 1], token_ids[:, bass.ds(b * C, C)].unsqueeze(1).to_broadcast((P, 2, C)))
                if i.has(2):
                    ln(i.at(2))
                dve.wait_ge(rank_done, b + 1)
                need(dve, counted, b)
                if i.has(2):
                    dve.wait_ge(stats_done, i.at(2) + 1)
                nc.vector.tensor_tensor(place[:], ranked[:, 0:C * E].rearrange("p (c e) -> p c e", c=C),
                                        next_row[:].unsqueeze(1).to_broadcast((P, C, E)), ALU.add).then_inc(placed, 1)
                if i.has(2):
                    ln_mean(i.at(2))
                dve.wait_ge(placed, b + 1)
                nc.vector.tensor_tensor(next_row[:], next_row[:], ranked[:, C * E:C * E + E], ALU.add).then_inc(counted, 1)
                nc.vector.tensor_tensor(place_of[:].rearrange("p k c e -> p k (c e)"), one_hot[:].rearrange("p k c e -> p k (c e)"),
                                        place[:].rearrange("p c e -> p (c e)").unsqueeze(1).to_broadcast((P, 2, C * E)), ALU.mult).then_inc(place_picked, 1)
                dve.wait_ge(place_picked, b + 1)
                nc.vector.reduce_sum(slot_f[:], place_of[:], AX_X).then_inc(slot_summed, 1)
                dve.wait_ge(slot_summed, b + 1)
                nc.vector.tensor_copy(slot[p][:], slot_f[:]).then_inc(rows_ready, 1)
                if soft:
                    dve.wait_ge(sh_down_done, b + 1)
                    dve.wait_ge(x_biased, b + 1)
                    x_rows = keep.x[:, bass.ds(b * C, C), :].rearrange("p c d -> p (c d)")
                    nc.vector.scalar_tensor_tensor(out=x_rows, in0=sh_y[:], scalar=keep.tanh_gates[:, gate_col:gate_col + 1],
                                                   in1=x_rows, op0=ALU.mult, op1=ALU.add).then_inc(x_updated, 1)
                if i.has(2):
                    ln_apply(i.at(2), p, (i.half(0) + 1) * 16 * 2 * C)

            pipeline(dve, step, NB, FIRST, LAST, HEAD, TAIL)

            steps = [0]

            def tail_step(ins):
                steps[0] += 1
                ins.then_inc(table_step, 1)
                dve.wait_ge(table_step, steps[0])

            dve.wait_ge(counted, NB)
            tail_step(nc.vector.tensor_tensor(pad_slot_f[:], next_row[:].unsqueeze(2).to_broadcast((P, E, TT)),
                                              pad_offset[:].unsqueeze(1).to_broadcast((P, E, TT)), ALU.add))
            nc.vector.tensor_copy(pad_slot[:], pad_slot_f[:]).then_inc(pad_slots_ready, 1)
            tail_step(nc.vector.tensor_tensor(count[:], next_row[:], region_start[:], ALU.subtract))
            tail_step(nc.vector.tensor_tensor(beyond[:], count[:].unsqueeze(2).to_broadcast((P, E, J)),
                                              full_steps[:].unsqueeze(1).to_broadcast((P, E, J)), ALU.is_gt))
            tail_step(nc.vector.reduce_sum(n_tiles[:], beyond[:], AX_X))
            tail_step(nc.vector.tensor_copy(ends[:, 0:1], n_tiles[:, 0:1]))
            for e in range(1, E):
                tail_step(nc.vector.tensor_tensor(ends[:, e:e + 1], ends[:, e - 1:e], n_tiles[:, e:e + 1], ALU.add))
            tail_step(nc.vector.tensor_tensor(past[:], tile_iota[:].unsqueeze(2).to_broadcast((P, tiles, E)),
                                              ends[:].unsqueeze(1).to_broadcast((P, tiles, E)), ALU.is_ge))
            tail_step(nc.vector.reduce_sum(region[:], past[:], AX_X))
            tail_step(nc.vector.tensor_tensor(past_tiles[:], past[:], n_tiles[:].unsqueeze(1).to_broadcast((P, tiles, E)), ALU.mult))
            tail_step(nc.vector.reduce_sum(first_tile[:], past_tiles[:], AX_X))
            tail_step(nc.vector.tensor_tensor(in_region[:], tile_iota[:], first_tile[:], ALU.subtract))
            tail_step(nc.vector.tensor_scalar(row_f[:], region[:], float(R), None, ALU.mult))
            tail_step(nc.vector.scalar_tensor_tensor(out=row_f[:], in0=in_region[:], scalar=float(TS), in1=row_f[:], op0=ALU.mult, op1=ALU.add))
            nc.vector.tensor_copy(routed.tile_row[:], row_f[:])
            tail_step(nc.vector.tensor_tensor(group_f[:], past[:, :, E - 1], in_region[:], ALU.mult))
            tail_step(nc.vector.tensor_tensor(group_f[:], group_f[:], region[:], ALU.add))
            nc.vector.tensor_copy(routed.tile_group[:, 0:1], group_f[:, 0:1])
            nc.vector.tensor_copy(routed.tile_group[:, 1:1 + tiles], group_f[:])
            tail_step(nc.vector.tensor_scalar(region[:], region[:], float(E - 1), None, ALU.min))
            nc.vector.tensor_copy(routed.tile_expert[:, 0:1], region[:, 0:1])
            nc.vector.tensor_copy(routed.tile_expert[:, 1:1 + tiles], region[:])

        @block.scalar
        def _(act):
            act.wait_ge(prep_turned, 1)
            nc.scalar.activation(routed.up_bias[:], ranked[:, 0:E * FC], ACT.Copy).then_inc(prep_copied, 1)
            if soft:
                act.wait_ge(prep_turned, 2)
                nc.scalar.activation(gate_w[:], turned[:, 0:KC * E].rearrange("p (k e) -> p k e", k=KC), ACT.Copy).then_inc(prep_copied, 1)
                act.wait_ge(prep_turned, 3)
                nc.scalar.activation(sh_up_bias[:], ranked[:, 0:KC], ACT.Copy).then_inc(prep_copied, 1)
            else:
                act.wait_ge(w_loaded, 16 * N_LOADS)
                nc.scalar.activation(sim_sq[:], sim_rows[:], ACT.Square, accum_out=sim_ss[:, 0:1]).then_inc(sim_step, 1)
                act.wait_ge(prep_turned, 2)
                nc.scalar.activation(gate_w[:, :, 0:D], turned[:].rearrange("p (k d) -> p k d", k=KC), ACT.Copy).then_inc(prep_copied, 1)
                act.wait_ge(prep_turned, 3)
                nc.scalar.activation(sim_t[:], ranked[:, 0:KC * E].rearrange("p (k e) -> p k e", k=KC), ACT.Copy).then_inc(prep_copied, 1)
                act.wait_ge(prep_turned, 4)
                nc.scalar.activation(gate_w[:, :, D:D + E], turned[:, 0:KC * E].rearrange("p (k e) -> p k e", k=KC), ACT.Copy).then_inc(prep_copied, 1)

            def turn_out(b, p):
                act.wait_ge(xn_turned, b + 1)
                nc.scalar.activation(xn_t[:].rearrange("p k s -> p (k s)"), turned[:], ACT.Copy).then_inc(xn_t_ready, 1)

            turn_out(0, 0)

            def step(i):
                b, p = i.at(0), i.par(0)
                act.wait_ge(xn_ready, b + 1)
                nc.scalar.activation(rows[p][:, 1, :, 0:D], rows[p][:, 0, :, 0:D], ACT.Copy).then_inc(rows_copied, 1)
                if not soft:
                    act.wait_ge(gate_done, b + 1)
                    need(act, rnorm_done, b)
                    for c in range(C):
                        last = nc.scalar.activation(proj_sq[:, c, :], gated[c][:, 0:D], ACT.Square, accum_out=proj_ss[:, c:c + 1])
                    last.then_inc(ss_done, 1)
                else:
                    act.wait_ge(sh_up_done, b + 1)
                    need(act, sh_down_done, b)
                    for fc in range(KC):
                        last = nc.scalar.activation(sh_hidden[:, fc, :], sh_h[:, fc * S:(fc + 1) * S], ACT.Silu, bias=sh_up_bias[:, fc:fc + 1])
                    last.then_inc(sh_hidden_ready, 1)
                if i.has(1):
                    turn_out(i.at(1), i.par(1))
                act.wait_ge(below_done, b + 1)
                nc.scalar.activation(exps[:], below_top[:], ACT.Exp).then_inc(exps_done, 1)

            pipeline(act, step, NB, FIRST, LAST, HEAD, TAIL)

        @block.tensor
        def _(pe):
            pe.wait_ge(w_loaded, 16 * N_LOADS)
            nc.tensor.transpose(ranked[:, 0:E * FC], up_b_rows[:], keep.ident[0:E * FC, 0:E * FC]).then_inc(prep_turned, 1)
            if soft:
                for kc in range(KC):
                    last = nc.tensor.transpose(turned[:, kc * E:(kc + 1) * E], gate_rows[:, kc * P:(kc + 1) * P], keep.ident[0:E, 0:E])
                last.then_inc(prep_turned, 1)
                pe.wait_ge(prep_copied, 1)
                nc.tensor.transpose(ranked[:, 0:KC], sh_up_b_rows[:], keep.ident[0:KC, 0:KC]).then_inc(prep_turned, 1)
                pe.wait_ge(prep_copied, 3)
            else:
                for kc in range(KC):
                    for oc in range(KC):
                        last = nc.tensor.transpose(turned[:, kc * D + oc * P:kc * D + oc * P + P], wp_rows[:, oc, kc * P:kc * P + P], keep.ident[:])
                last.then_inc(prep_turned, 1)
                pe.wait_ge(prep_copied, 1)
                pe.wait_ge(sim_step, 4)
                for kc in range(KC):
                    last = nc.tensor.transpose(ranked[:, kc * E:(kc + 1) * E], sim_unit[:, kc * P:(kc + 1) * P], keep.ident[0:E, 0:E])
                last.then_inc(prep_turned, 1)
                pe.wait_ge(prep_copied, 3)
                for kc in range(KC):
                    for oc in range(KC):
                        last = nc.tensor.matmul(turned[:, kc * E:(kc + 1) * E], wp_rows[:, oc, kc * P:(kc + 1) * P], sim_t[:, oc, :],
                                                start=(oc == 0), stop=(oc == KC - 1))
                last.then_inc(prep_turned, 1)
                pe.wait_ge(prep_copied, 4)
            pe.wait_ge(consts_ready, 1)

            def turn(b, p):
                pe.wait_ge(xn_ready, b + 1)
                need(pe, xn_t_ready, b)
                for kc in range(KC):
                    for c in range(C):
                        last = nc.tensor.transpose(turned[:, kc * S + c * P:kc * S + c * P + P], rows[p][:, 0, c, kc * P:(kc + 1) * P], keep.ident[:])
                last.then_inc(xn_turned, 1)

            turn(0, 0)

            def step(i):
                b = i.at(0)
                pe.wait_ge(xn_t_ready, b + 1)
                need(pe, scores_ready, b)
                for c in range(C):
                    out = gated[0][:, c * E:(c + 1) * E] if soft else gated[c][:, 0:GW]
                    for kc in range(KC):
                        last = nc.tensor.matmul(out, xn_t[:, kc, c * P:(c + 1) * P], gate_w[:, kc, :], start=(kc == 0), stop=(kc == KC - 1))
                last.then_inc(gate_done, 1)
                if soft:
                    need(pe, sh_hidden_ready, b)
                    for fc in range(KC):
                        for kc in range(KC):
                            last = nc.tensor.matmul(sh_h[:, fc * S:(fc + 1) * S], sh_up[:, kc, fc * P:(fc + 1) * P], xn_t[:, kc, :],
                                                    start=(kc == 0), stop=(kc == KC - 1))
                    last.then_inc(sh_up_done, 1)
                if i.has(1):
                    turn(i.at(1), i.par(1))
                if soft:
                    pe.wait_ge(sh_hidden_ready, b + 1)
                    need(pe, x_updated, b)
                    for c in range(C):
                        for fc in range(KC):
                            last = nc.tensor.matmul(sh_y[:, c * D:(c + 1) * D], sh_hidden[:, fc, c * P:(c + 1) * P], sh_down[:, fc, :],
                                                    start=(fc == 0), stop=(fc == KC - 1))
                    last.then_inc(sh_down_done, 1)
                pe.wait_ge(chosen_ready, b + 1)
                need(pe, counted, b)
                for c in range(C):
                    out = ranked[:, c * E:(c + 1) * E]
                    nc.tensor.matmul(out, before16[:], chosen[:, c, :], start=True, stop=(c == 0))
                    for q in range(c):
                        nc.tensor.matmul(out, ones16[:], chosen[:, q, :], start=False, stop=(q == c - 1))
                for c in range(C):
                    last = nc.tensor.matmul(ranked[:, C * E:C * E + E], ones16[:], chosen[:, c, :], start=(c == 0), stop=(c == C - 1))
                last.then_inc(rank_done, 1)

            pipeline(pe, step, NB, FIRST, LAST, HEAD, TAIL)

    clear_semaphores(nc, all_sems)


def expert_phase(nc, keep, routed, layer, F, act_func, up_w, down_w, down_b, xs, x_acc):
    D = keep.x.shape[2]
    tokens = keep.x.shape[1] * P
    E = EXPERTS
    KC, FC = D // P, F // P
    tiles = tile_count(tokens)
    tag = f"e{layer}_"
    PER_BANK = 512 // TS
    N_BANKS = max(1, FC // PER_BANK)

    all_sems = []
    with ExitStack() as ctx:
        def sb(name, shape, dt=F32):
            return ctx.enter_context(nc.sbuf_tensor(tag + name, shape, dt))

        def sem(name):
            s = ctx.enter_context(nc.semaphore(tag + name))
            all_sems.append(s)
            return s

        up = [sb(f"up{n}", [P, KC, F]) for n in range(2)]
        down = [sb(f"down{n}", [P, FC, D]) for n in range(2)]
        down_bias = sb("down_bias", [P, E, D])
        xs_rows = [sb(f"xs_rows{n}", [P, TT, ROW]) for n in range(2)]
        xs_t = [sb(f"xs_t{n}", [P, KC, TS]) for n in range(2)]
        hidden = sb("hidden", [P, FC, TS])
        weight = [sb(f"weight{n}", [P, TT]) for n in range(2)]
        token = [sb(f"token{n}", [P, TT], U32) for n in range(2)]
        y_biased = [sb(f"y_biased{n}", [P, TT, D]) for n in range(2)]
        y = [sb(f"y{n}", [P, TT, D]) for n in range(2)]

        def bank(name):
            return ctx.enter_context(nc.psum_tensor(tag + name, [P, 512], F32))

        turned = bank("turned")
        h_bank = [bank(f"h{n}") for n in range(N_BANKS)]
        y_bank = bank("y_bank")

        bias_loaded = sem("bias_loaded")
        w_loaded = [sem(f"w_loaded{n}") for n in range(2)]
        xs_loaded = [sem(f"xs_loaded{n}") for n in range(2)]
        xs_turned = sem("xs_turned")
        xs_t_ready = sem("xs_t_ready")
        up_done = sem("up_done")
        hidden_ready = sem("hidden_ready")
        y_done = sem("y_done")
        bias_added = sem("bias_added")
        y_ready = sem("y_ready")
        meta_ready = sem("meta_ready")
        y_sent = keep.y_sent[layer]
        SENT = 16 * TT

        FIRST, LAST, HEAD, TAIL = 0, tiles - 1, 2, 2
        block = ctx.enter_context(nc.Block())

        def expert_of(eng, t):
            return eng.value_load(routed.tile_expert[0:1, bass.ds(t + 1, 1)], min_val=0, max_val=E - 1)

        @block.sync
        def _(sp):
            def load_weights(e, n):
                sp.dma_start(up[n][:], up_w[e].rearrange("(c p) f -> p c f", p=P)).then_inc(w_loaded[n], 16)
                sp.dma_start(down[n][:], down_w[e].rearrange("(c p) d -> p c d", p=P)).then_inc(w_loaded[n], 16)

            def load_rows(t, n):
                row = sp.value_load(routed.tile_row[0:1, bass.ds(t, 1)], min_val=0, max_val=routed_rows(tokens) - TS)
                sp.dma_start(xs_rows[n][:], xs[bass.ds(row, TS), :].rearrange("(c p) w -> p c w", p=P)).then_inc(xs_loaded[n], 16)

            load_rows(0, 0)
            load_weights(0, 0)
            load_rows(1, 1)
            load_weights(1, 1)
            sp.dma_start(down_bias[:], down_b.rearrange("(a e) d -> a e d", a=1).to_broadcast((P, E, D))).then_inc(bias_loaded, 16)

            def step(i):
                t = i.at(0)
                if not (isinstance(t, int) and t == 0):
                    e = expert_of(sp, t)
                    before = expert_of(sp, t - 1)
                    with sp.If(e > before):
                        with sp.If(e < E - 1):
                            sp.wait_ge(y_done, t)
                            nxt = nc.s_assert_within(e + 1, 1, E - 1, skip_runtime_bounds_check_because="e < E - 1 here")
                            with sp.If(nxt % 2 == 0):
                                load_weights(nxt, 0)
                            with sp.Else():
                                load_weights(nxt, 1)
                if i.has(2):
                    sp.wait_ge(meta_ready, t + 1)
                    sp.wait_ge(xs_turned, t + 1)
                    load_rows(i.at(2), i.par(0))

            pipeline(sp, step, tiles, FIRST, LAST, HEAD, TAIL)

        @block.gpsimd
        def _(pool):
            def group_of(t):
                return pool.value_load(routed.tile_group[0:1, bass.ds(t + 1, 1)], min_val=0, max_val=E + tiles)

            def step(i):
                t, p = i.at(0), i.par(0)
                group, before = group_of(t), group_of(t - 1)
                with pool.If(group > before):
                    need(pool, y_sent[1 - p], i.half(1) * SENT)
                    pool.wait_ge(y_ready, t + 1)
                with pool.Else():
                    pool.wait_ge(y_ready, t + 1)
                for c in range(TT):
                    pool.indirect_dma_start(out=x_acc, out_offset=bass.IndirectOffsetOnAxis(ap=token[p][:, c:c + 1], axis=0),
                                            in_=y[p][:, c, :], in_offset=None, compute_op=ALU.add).then_inc(y_sent[p], 16)

            pipeline(pool, step, tiles, FIRST, LAST, HEAD, TAIL)
            for n in range(2):
                pool.wait_ge(y_sent[n], SENT * tiles // 2)

        @block.vector
        def _(dve):
            def turn_out(t, n):
                dve.wait_ge(xs_turned, t + 1)
                nc.vector.tensor_copy(xs_t[n][:].rearrange("p k s -> p (k s)"), turned[:, 0:KC * TS]).then_inc(xs_t_ready, 1)

            turn_out(0, 0)
            dve.wait_ge(bias_loaded, 16)

            def step(i):
                t, p = i.at(0), i.par(0)
                e = expert_of(dve, t)
                if i.has(1):
                    turn_out(i.at(1), i.par(1))
                dve.wait_ge(xs_loaded[p], 16 * (i.half(0) + 1))
                need(dve, y_sent[p], i.half(0) * SENT)
                nc.vector.tensor_copy(weight[p][:], xs_rows[p][:, :, D])
                nc.vector.tensor_copy(token[p][:], xs_rows[p][:, :, D + 1]).then_inc(meta_ready, 1)
                dve.wait_ge(y_done, t + 1)
                nc.vector.tensor_tensor(y_biased[p][:], y_bank[:].rearrange("p (c d) -> p c d", c=TT),
                                        down_bias[:, bass.ds(e, 1), :].to_broadcast((P, TT, D)), ALU.add).then_inc(bias_added, 1)
                dve.wait_ge(bias_added, t + 1)
                dve.wait_ge(meta_ready, t + 1)
                for c in range(TT):
                    last = nc.vector.tensor_scalar(y[p][:, c, :], y_biased[p][:, c, :], weight[p][:, c:c + 1], None, ALU.mult)
                last.then_inc(y_ready, 1)

            pipeline(dve, step, tiles, FIRST, LAST, HEAD, TAIL)

        @block.scalar
        def _(act):
            def step(i):
                t = i.at(0)
                e = expert_of(act, t)
                for fc in range(FC):
                    if fc % PER_BANK == 0:
                        act.wait_ge(up_done, N_BANKS * t + fc // PER_BANK + 1)
                    g, at = fc // PER_BANK, fc % PER_BANK * TS
                    nc.scalar.activation(hidden[:, fc, :], h_bank[g][:, at:at + TS], act_func,
                                         bias=routed.up_bias[:, bass.ds(e * FC + fc, 1)]).then_inc(hidden_ready, 1)

            pipeline(act, step, tiles, FIRST, LAST, HEAD, TAIL)

        @block.tensor
        def _(pe):
            def turn(t, n, half):
                pe.wait_ge(xs_loaded[n], 16 * (half + 1))
                for kc in range(KC):
                    for c in range(TT):
                        last = nc.tensor.transpose(turned[:, kc * TS + c * P:kc * TS + c * P + P], xs_rows[n][:, c, kc * P:(kc + 1) * P], keep.ident[:])
                last.then_inc(xs_turned, 1)

            turn(0, 0, 0)

            def step(i):
                t, p = i.at(0), i.par(0)
                e = expert_of(pe, t)

                def through(n):
                    pe.wait_ge(w_loaded[n], (e // 2 + 1) * 32)
                    pe.wait_ge(xs_t_ready, t + 1)
                    for fc in range(FC):
                        g, at = fc // PER_BANK, fc % PER_BANK * TS
                        for kc in range(KC):
                            last = nc.tensor.matmul(h_bank[g][:, at:at + TS], up[n][:, kc, fc * P:(fc + 1) * P], xs_t[p][:, kc, :],
                                                    start=(kc == 0), stop=(kc == KC - 1))
                        if fc % PER_BANK == PER_BANK - 1:
                            last.then_inc(up_done, 1)
                    if i.has(1):
                        turn(i.at(1), i.par(1), i.half(1))
                    for c in range(TT):
                        for fc in range(FC):
                            if c == 0:
                                pe.wait_ge(hidden_ready, FC * t + fc + 1)
                            if c == 0 and fc == 0:
                                need(pe, bias_added, t)
                            last = nc.tensor.matmul(y_bank[:, c * D:(c + 1) * D], hidden[:, fc, c * P:(c + 1) * P], down[n][:, fc, :],
                                                    start=(fc == 0), stop=(fc == FC - 1))
                    last.then_inc(y_done, 1)

                with pe.If(e % 2 == 0):
                    through(0)
                with pe.Else():
                    through(1)

            pipeline(pe, step, tiles, FIRST, LAST, HEAD, TAIL)

    clear_semaphores(nc, all_sems)


def gated_flamingo(nc, p, out):
    x, ctx_in, lens = p["x"], p["ctx_1024"], p["mask_B_ik0"]
    B, S, D = x.shape
    tokens = B * S
    F0 = p["L0_ffn_up_w"].shape[2]
    F1 = p["L1_ffn_W1"].shape[2]
    scratch = [nc.dram_tensor(f"parts_dram{n}", (2 * D // P, 3, P, S), BF16, kind="Internal").ap() for n in range(2)]
    xs = nc.dram_tensor("routed_rows_dram", (routed_rows(tokens), ROW), F32, kind="Internal").ap()
    x_mid = nc.dram_tensor("x_mid_dram", (tokens + TS, D), F32, kind="Internal").ap()

    with ExitStack() as ctx:
        keep = Resident(nc, ctx, tokens, D)
        setup_phase(nc, keep, p["g_xattn"], p["g_ffn"])

        attention_phase(nc, keep, 0, x, ctx_in, None, [p[f"L0_xattn_{w}"] for w in ("Wq", "Wk", "Wv", "Wo")],
                        [p["L0_xattn_bv"], p["L0_xattn_bo"]], scratch)
        with ExitStack() as tables:
            routed = Routed(nc, tables, "t0", tokens, F0)
            route_phase(nc, keep, routed, 0, F0, p["L0_ffn_up_b"], [p["L0_ffn_gate_w"]],
                        [p[f"L0_ffn_sh_{w}"] for w in ("up_w", "up_b", "down_w", "down_b")], xs, x_mid)
            expert_phase(nc, keep, routed, 0, F0, ACT.Silu, p["L0_ffn_up_w"], p["L0_ffn_down_w"], p["L0_ffn_down_b"], xs, x_mid)

        attention_phase(nc, keep, 1, x_mid[0:tokens, :].rearrange("(b s) d -> b s d", s=S), ctx_in, lens,
                        [p[f"L1_xattn_{w}"] for w in ("W_q", "W_k", "W_v", "W_o")], None, scratch)
        with ExitStack() as tables:
            routed = Routed(nc, tables, "t1", tokens, F1)
            route_phase(nc, keep, routed, 1, F1, p["L1_ffn_b1"],
                        [p["L1_ffn_Wp"], p["L1_ffn_sim_matrix"], p["L1_ffn_temperature"]], None, xs, out)
            expert_phase(nc, keep, routed, 1, F1, ACT.Gelu, p["L1_ffn_W1"], p["L1_ffn_W2"], p["L1_ffn_b2"], xs, out)


INPUTS = (["x", "ctx_1024", "mask_B_ik0", "g_xattn", "g_ffn"]
          + [f"L0_xattn_{n}" for n in ("Wq", "Wk", "Wv", "bv", "Wo", "bo")]
          + [f"L0_ffn_{n}" for n in ("gate_w", "up_w", "up_b", "down_w", "down_b", "sh_up_w", "sh_up_b", "sh_down_w", "sh_down_b")]
          + [f"L1_xattn_{n}" for n in ("W_q", "W_k", "W_v", "W_o")]
          + [f"L1_ffn_{n}" for n in ("Wp", "sim_matrix", "temperature", "W1", "b1", "W2", "b2")])


def kernel(**inputs):
    import numpy as _np
    import concourse.bacc as _bacc
    from concourse.bass_utils import run_bass_kernel_spmd as _run

    nc = _bacc.Bacc("TRN2", target_bir_lowering=False, num_devices=1)
    arrays, params = {}, {}
    for name in INPUTS:
        a = _np.ascontiguousarray(inputs[name])
        a = a.reshape(a.shape or (1,))
        arrays[f"in_{name}"] = a
        params[name] = nc.dram_tensor(f"in_{name}", a.shape, mybir.dt.from_np(a.dtype), kind="ExternalInput").ap()
    B, S, D = inputs["x"].shape
    out = nc.dram_tensor("out_rows", (B * S + TS, D), F32, kind="ExternalOutput").ap()
    gated_flamingo(nc, params, out)
    r = _run(nc, [arrays], core_ids=[0])
    return _np.asarray(r.results[0]["out_rows"])[:B * S].reshape(B, S, D)
```

```python
from contextlib import ExitStack, nullcontext

import concourse.bass as bass
from concourse import mybir

P = 128
F32 = mybir.dt.float32
F32R = mybir.dt.float32r
BF16 = mybir.dt.bfloat16
I32 = mybir.dt.int32
U32 = mybir.dt.uint32
ALU = mybir.AluOpType
ACT = mybir.ActivationFunctionType
AX_X = mybir.AxisListType.X

LN_EPS = 1e-5
CAUSAL_FILL = -1e30
NEG_HI, NEG_LO = -999424.0, -576.0


class Step:

    def __init__(self, pair, off, count):
        self.pair, self.off, self.count = pair, off, count

    def at(self, d):
        return self.pair * 2 + (self.off + d)

    def half(self, d):
        return self.pair + (self.off + d) // 2

    def par(self, d):
        return (self.off + d) % 2

    def has(self, d):
        return not isinstance(self.pair, int) or 0 <= self.at(d) < self.count

    def upto(self, d):
        n = self.at(d) + 1
        return min(n, self.count) if isinstance(n, int) else n


def pipeline(eng, step, count, first, last, head, tail, while_below=None):
    for i in range(first, first + head):
        step(Step(0, i, count))
    lo, hi = first + head, last + 1 - tail
    assert lo % 2 == 0 and (hi - lo) % 2 == 0
    with eng.Fori(lo // 2, hi // 2) as pair:
        with eng.If(pair * 2 < while_below) if while_below is not None else nullcontext():
            step(Step(pair, 0, count))
            step(Step(pair, 1, count))
    for i in range(hi, last + 1):
        step(Step(0, i, count))


def need(eng, sem, value, base=0):
    if isinstance(value, int) and value <= 0:
        return
    eng.wait_ge(sem, value + base)


def wait_apart(eng, sem, value, met, met_value):
    if not isinstance(value, int):
        value = eng.snap(value)
    eng.wait_ge(met, met_value)
    eng.wait_ge(sem, value)


class Resident:

    def __init__(self, nc, ctx, tokens, width):
        def sb(name, shape, dt):
            return ctx.enter_context(nc.sbuf_tensor(name, shape, dt))

        self.x = sb("x_rows", [P, tokens // P, width], F32)
        self.ident = sb("ident", [P, P], F32)
        self.ident16 = sb("ident16", [P, P], BF16)
        self.rows_sent = [[ctx.enter_context(nc.semaphore(f"rows_sent{layer}{n}")) for n in range(2)] for layer in range(2)]
        self.pads_sent = [ctx.enter_context(nc.semaphore(f"pads_sent{layer}")) for layer in range(2)]
        self.y_sent = [[ctx.enter_context(nc.semaphore(f"y_sent{layer}{n}")) for n in range(2)] for layer in range(2)]
        self.tanh_gates = sb("tanh_gates", [P, 4], F32)


def clear_semaphores(nc, ctx_sems):
    with nc.Block() as block:
        @block.gpsimd
        def _(pool):
            for s in ctx_sems:
                pool.sem_clear(s)


def setup_phase(nc, keep, g_xattn, g_ffn):
    with ExitStack() as ctx:
        gates = ctx.enter_context(nc.sbuf_tensor("gates", [P, 4], F32))
        gates_loaded = ctx.enter_context(nc.semaphore("gates_loaded"))
        idents_cleared = ctx.enter_context(nc.semaphore("idents_cleared"))
        block = ctx.enter_context(nc.Block())

        @block.sync
        def _(sp):
            for n, g in enumerate((g_xattn, g_ffn)):
                row = g.rearrange("(a n) -> a n", a=1)
                sp.dma_start(gates[:, 2 * n:2 * n + 2], row.to_broadcast((P, 2))).then_inc(gates_loaded, 16)

        @block.scalar
        def _(act):
            act.wait_ge(gates_loaded, 32)
            nc.scalar.activation(keep.tanh_gates[:], gates[:], ACT.Tanh)

        @block.gpsimd
        def _(pool):
            nc.gpsimd.memset(keep.ident[:], 0.0).then_inc(idents_cleared, 1)
            nc.gpsimd.memset(keep.ident16[:], 0.0).then_inc(idents_cleared, 1)
            pool.wait_ge(idents_cleared, 2)
            for ident in (keep.ident, keep.ident16):
                nc.gpsimd.affine_select(out=ident[:], in_=ident[:], compare_op=ALU.not_equal, fill=1.0,
                                        base=0, pattern=[[-1, P]], channel_multiplier=1)

    clear_semaphores(nc, [gates_loaded, idents_cleared])


def attention_phase(nc, keep, layer, x_in, ctx_in, lens, weights, biases, scratch):
    B, S, D = ctx_in.shape
    H, HD = 16, D // 16
    KC, TC = D // P, S // P
    causal = layer == 0
    scale = HD ** -0.5
    RUNS = (((0, 1, 2), 0), ((0, 1), 1), ((0,), 2))
    STACK = HD * sum(len(qs) for qs, _ in RUNS)
    MASK_ROWS = 0 if causal else 2
    MAX_ROW = STACK + MASK_ROWS
    HH = H // 2
    VW = 2 * HD
    GH = P // VW
    GROUPS = H // GH
    PER_BANK = 512 // S
    NP = 2 * GH
    gate_col = layer
    tag = f"a{layer}_"

    all_sems = []
    with ExitStack() as ctx:
        def sb(name, shape, dt=F32):
            return ctx.enter_context(nc.sbuf_tensor(tag + name, shape, dt))

        def pair(name, shape, dt=F32):
            return [sb(f"{name}{n}", shape, dt) for n in range(2)]

        def sem(name):
            s = ctx.enter_context(nc.semaphore(tag + name))
            all_sems.append(s)
            return s

        def sems(name):
            return [sem(f"{name}{n}") for n in range(2)]

        w_rows = sb("w_rows", [P, 4, KC, D])
        w_t = [sb(f"w_{part}", [P, 3, KC, D], F32R) for part in ("hi", "lo")]
        assert HH * HD == P
        ctx_rows = pair("ctx_rows", [P, TC, D])
        xn = pair("xn", [P, TC, D])
        xn_t = [pair(f"xn_t{n}_", [P, KC, S], F32R) for n in range(2)]
        ctx_t = [pair(f"ctx_t{n}_", [P, KC, S], F32R) for n in range(2)]
        stats = sb("stats", [P, TC, 6])
        mean_var = sb("mean_var", [P, TC, 2])
        var_eps = sb("var_eps", [P, TC])
        eps = sb("eps", [P, TC])
        minus_half = sb("minus_half", [P, TC])
        rstd = sb("rstd", [P, TC])
        qk = pair("qk", [P, 2 * KC, S])
        rest = sb("rest", [P, 2 * KC, S])
        parts = pair("parts", [P, 2 * KC, 3, S], BF16)
        q_stack = pair("q_stack", [P, H, S], BF16)
        k_stack = pair("k_stack", [P, H, S], BF16)
        v_ones = pair("v_ones", [P, TC, H, VW])
        row_max = sb("row_max", [P, TC, H])
        max_rest = sb("max_rest", [P, TC, H])
        max_parts = sb("max_parts", [P, TC, 3, H], BF16)
        max_t = pair("max_t", [3 * H, S], BF16)
        probs = [sb(f"probs{n}", [P, 512]) for n in range(NP)]
        wo_rows = sb("wo_rows", [P, KC, H, VW])
        wo_t = sb("wo_t", [P, GROUPS, D])
        den_rows = sb("den_rows", [P, GH])
        den_recip = sb("den_recip", [P, TC, H])
        strip_recip = sb("strip_recip", [P, TC, H, VW])
        mixed = sb("mixed", [P, GROUPS, S])
        heads_t = pair("heads_t", [P, GROUPS, S])
        if causal:
            mask_st = sb("mask_st", [P, 2, P], BF16)
            mask_ts = sb("mask_ts", [P, 2, P], BF16)
            bv_rows = sb("bv_rows", [P, TC, D])
            bo_rows = sb("bo_rows", [P, D])
        else:
            lens_i = sb("lens_i", [P, B], I32)
            lens_f = sb("lens_f", [P, B])
            iota_t = sb("iota_t", [P, S])
            neg_col = sb("neg_col", [P, 1])
            valid = sb("valid", [P, S])
            mask_row = pair("mask_row", [P, S], BF16)

        stage = [ctx.enter_context(nc.psum_tensor(f"{tag}stage{n}", [P, 512], F32)) for n in range(2)]
        scores = [ctx.enter_context(nc.psum_tensor(f"{tag}scores{n}", [P, 512], F32)) for n in range(2)]
        scores_t = [ctx.enter_context(nc.psum_tensor(f"{tag}scores_t{n}", [P, 512], F32)) for n in range(2)]
        pv = [ctx.enter_context(nc.psum_tensor(f"{tag}pv{n}", [P, 512], F32)) for n in range(2)]

        w_loaded = sem("w_loaded")
        w_turned = sem("w_turned")
        w_hi_done = sem("w_hi_done")
        w_ready = sem("w_ready")
        wo_ready = sem("wo_ready")
        consts_loaded = sem("consts_loaded")
        ones_filled = sem("ones_filled")
        consts_step = sem("consts_step")
        consts_ready = sem("consts_ready")
        bo_gated = sem("bo_gated")
        wo_cleared = sem("wo_cleared")
        wo_spread = sem("wo_spread")
        x_loaded = sems("x_loaded")
        ctx_loaded = sems("ctx_loaded")
        stats_done = sem("stats_done")
        mean_done = sem("mean_done")
        eps_added = sem("eps_added")
        rstd_done = sem("rstd_done")
        xn_ready = sem("xn_ready")
        x_biased = sem("x_biased")
        xn_turned = sem("xn_turned")
        ctx_turned = sem("ctx_turned")
        xn_hi_done = sem("xn_hi_done")
        ctx_hi_done = sem("ctx_hi_done")
        xn_t_ready = sem("xn_t_ready")
        ctx_t_ready = sem("ctx_t_ready")
        q_done = sem("q_done")
        k_done = sem("k_done")
        v_done = sem("v_done")
        q_ready = sem("q_ready")
        k_ready = sem("k_ready")
        v_ready = sem("v_ready")
        valid_done = sem("valid_done")
        part_hi = sem("part_hi")
        part_rest = sem("part_rest")
        part_mid = sem("part_mid")
        parts_ready = sem("parts_ready")
        parts_stored = sems("parts_stored")
        stacked = [sems(f"stacked_half{n}_") for n in range(2)]
        scores_done = sem("scores_done")
        maxed = sem("maxed")
        max_hi = sem("max_hi")
        max_r1 = sem("max_r1")
        max_mid = sem("max_mid")
        max_ready = sem("max_ready")
        max_turned = sem("max_turned")
        max_t_ready = sem("max_t_ready")
        max_stacked = sems("max_stacked")
        scores_t_done = sem("scores_t_done")
        probs_ready = sem("probs_ready")
        pv_done = sem("pv_done")
        mixed_ready = sem("mixed_ready")
        recip_done = sem("recip_done")
        recip_copied = sem("recip_copied")
        den_picked = sem("den_picked")
        recip_spread = sem("recip_spread")
        heads_t_ready = sem("heads_t_ready")
        o_done = sem("o_done")
        x_updated = sem("x_updated")

        x_tiles = x_in.rearrange("b (c p) d -> b p c d", p=P)
        ctx_tiles = ctx_in.rearrange("b (c p) d -> b p c d", p=P)
        N_CONSTS = 3 if causal else 1
        N_READY = 5

        FIRST, LAST, HEAD, TAIL = -3, B, 5, 7

        def w_view(w, n):
            return w[:, n].rearrange("p c (o d h) -> p (c o) d h", o=KC, d=HD) if n < 2 else w[:, n].rearrange("p c d -> p (c d)")

        def stage_view(n):
            return stage[n % 2][:].rearrange("p (c h d) -> p c d h", c=KC * KC, d=HD) if n < 2 else stage[n % 2][:]

        block = ctx.enter_context(nc.Block())

        @block.sync
        def _(sp):
            for n, w in enumerate(weights):
                sp.dma_start(w_rows[:, n], w.rearrange("(c p) d -> p c d", p=P)).then_inc(w_loaded, 16)
            if causal:
                bv, bo = biases
                for c in range(TC):
                    sp.dma_start(bv_rows[:, c], bv.rearrange("(a d) -> a d", a=1).to_broadcast((P, D))).then_inc(consts_loaded, 16)
                sp.dma_start(bo_rows[:], bo.rearrange("(a d) -> a d", a=1).to_broadcast((P, D))).then_inc(consts_loaded, 16)
            else:
                sp.dma_start(lens_i[:], lens.rearrange("(a n) -> a n", a=1).to_broadcast((P, B))).then_inc(consts_loaded, 16)
            for b in range(2):
                sp.dma_start(keep.x[:, TC * b:TC * b + TC, :], x_tiles[b]).then_inc(x_loaded[b], 16)
            sp.dma_start(ctx_rows[0][:], ctx_tiles[0]).then_inc(ctx_loaded[0], 16)
            sp.wait_ge(consts_ready, N_READY)

            def step(i):
                if i.has(5):
                    need(sp, stats_done, i.at(3) + 1)
                    sp.dma_start(keep.x[:, bass.ds(i.at(5) * TC, TC), :], x_tiles[i.at(5)]).then_inc(x_loaded[i.par(5)], 16)
                if i.has(4):
                    need(sp, ctx_turned, i.at(2) + 1)
                    sp.dma_start(ctx_rows[i.par(4)][:], ctx_tiles[i.at(4)]).then_inc(ctx_loaded[i.par(4)], 16)
                if i.has(2):
                    p = i.par(2)
                    need(sp, parts_ready, i.at(2) + 1)
                    sp.dma_start(scratch[p].rearrange("n j p s -> p (n j) s"), parts[p][:].rearrange("p n j s -> p (n j) s")).then_inc(parts_stored[p], 16)
                    need(sp, parts_stored[p], (i.half(2) + 1) * 16)
                    for half in range(2):
                        need(sp, scores_t_done, i.at(0) * H + HH * (half + 1))
                        hs = slice(half * HH, half * HH + HH)
                        row = 0
                        for qs, k in RUNS:
                            rows = slice(row, row + HD * len(qs))
                            row = rows.stop
                            q_src = scratch[p][half, qs[0]:qs[-1] + 1].rearrange("j (d h) s -> (j d) (h s)", d=HD)
                            k_src = scratch[p][KC + half, k:k + 1].rearrange("a (d h) s -> a d (h s)", d=HD)
                            sp.dma_start(q_stack[p][rows, hs, :].rearrange("r h s -> r (h s)"), q_src).then_inc(stacked[half][p], 16)
                            sp.dma_start(k_stack[p][rows, hs, :].rearrange("r h s -> r (h s)"),
                                         k_src.to_broadcast((len(qs), HD, HH * S))).then_inc(stacked[half][p], 16)
                        if not causal:
                            row = mask_row[p][STACK:STACK + 2, :].unsqueeze(1).to_broadcast((2, HH, S))
                            sp.dma_start(k_stack[p][STACK:STACK + 2, hs, :], row).then_inc(stacked[half][p], 16)

            pipeline(sp, step, B, FIRST, LAST, HEAD, TAIL)

        STACK_DMAS = 2 * len(RUNS) + (0 if causal else 1)

        @block.gpsimd
        def _(pool):
            for n in range(2):
                nc.gpsimd.memset(q_stack[n][STACK:P, :, :], 1.0).then_inc(ones_filled, 1)
            pool.wait_ge(ones_filled, 2)
            nc.gpsimd.memset(eps[:], LN_EPS)
            nc.gpsimd.memset(wo_rows[:], 0.0).then_inc(wo_cleared, 1)
            nc.gpsimd.memset(den_rows[:], 0.0).then_inc(wo_cleared, 1)
            pool.wait_ge(wo_cleared, 2)
            nc.gpsimd.affine_select(out=den_rows[:], in_=den_rows[:], compare_op=ALU.not_equal, fill=1.0,
                                    base=-HD, pattern=[[-VW, GH]], channel_multiplier=1).then_inc(wo_cleared, 1)
            nc.gpsimd.memset(minus_half[:], -0.5).then_inc(consts_step, 1)
            if causal:
                nc.gpsimd.memset(mask_st[:], 0.0).then_inc(consts_step, 1)
                nc.gpsimd.memset(mask_ts[:], 0.0).then_inc(consts_step, 1)
                pool.wait_ge(consts_step, 3)
                nc.gpsimd.affine_select(out=mask_st[:], in_=mask_st[:], compare_op=ALU.is_gt, fill=CAUSAL_FILL,
                                        base=0, pattern=[[0, 2], [-1, P]], channel_multiplier=1).then_inc(consts_step, 1)
                nc.gpsimd.affine_select(out=mask_ts[:], in_=mask_ts[:], compare_op=ALU.is_gt, fill=CAUSAL_FILL,
                                        base=0, pattern=[[0, 2], [1, P]], channel_multiplier=-1).then_inc(consts_step, 1)
                pool.wait_ge(consts_step, 5)
                nc.gpsimd.memset(mask_st[0:1, 0, 0:1], 0.0).then_inc(consts_step, 1)
                nc.gpsimd.memset(mask_ts[0:1, 0, 0:1], 0.0).then_inc(consts_step, 1)
                pool.wait_ge(consts_step, 7)
            else:
                nc.gpsimd.iota(iota_t[:], pattern=[[1, S]], base=0, channel_multiplier=0,
                               allow_small_or_imprecise_dtypes=True).then_inc(consts_step, 1)
                nc.gpsimd.memset(neg_col[:], NEG_LO).then_inc(consts_step, 1)
                pool.wait_ge(consts_step, 3)
                nc.gpsimd.memset(neg_col[STACK:STACK + 1, :], NEG_HI).then_inc(consts_step, 1)
                pool.wait_ge(consts_step, 4)
            nc.gpsimd.memset(var_eps[:], 1.0).then_inc(consts_ready, 1)

            def rstd_of(b, base):
                pool.wait_ge(mean_done, b + 1)
                nc.gpsimd.tensor_tensor(var_eps[:], mean_var[:, :, 1], eps[:], ALU.add).then_inc(eps_added, 1)
                pool.wait_ge(eps_added, b + 1)
                nc.gpsimd.tensor_tensor(rstd[:], var_eps[:], minus_half[:], ALU.pow).then_inc(rstd_done, 1)
                if causal:
                    pool.wait_ge(xn_ready, b + 1)
                    if isinstance(b, int) and b == 0:
                        pool.wait_ge(bo_gated, 1)
                    rows = keep.x[:, bass.ds(b * TC, TC), :] if not isinstance(b, int) else keep.x[:, b * TC:b * TC + TC, :]
                    nc.gpsimd.tensor_tensor(rows, rows, bo_rows[:].unsqueeze(1).to_broadcast((P, TC, D)), ALU.add).then_inc(x_biased, 1)

            rstd_of(0, 0)

            def step(i):
                if i.has(2):
                    b, p = i.at(2), i.par(2)
                    pool.wait_ge(part_hi, b + 1)
                    nc.gpsimd.tensor_tensor(rest[:], qk[p][:], parts[p][:, :, 0, :], ALU.subtract).then_inc(part_rest, 1)
                    pool.wait_ge(part_mid, b + 1)
                    nc.gpsimd.tensor_tensor(parts[p][:, :, 2, :], rest[:], parts[p][:, :, 1, :], ALU.subtract).then_inc(parts_ready, 1)
                if i.has(4):
                    rstd_of(i.at(4), 0)

            pipeline(pool, step, B, FIRST, LAST, HEAD, TAIL)

        @block.vector
        def _(dve):
            for n in range(2):
                nc.vector.memset(v_ones[n][:], 1.0).then_inc(consts_ready, 1)
                nc.vector.memset(k_stack[n][STACK:P, :, :], 1.0).then_inc(consts_ready, 1)
            dve.wait_ge(consts_ready, N_READY)
            dve.wait_ge(consts_loaded, 16 * N_CONSTS)
            if causal:
                nc.vector.tensor_scalar(bo_rows[:], bo_rows[:], keep.tanh_gates[:, gate_col:gate_col + 1], None, ALU.mult).then_inc(bo_gated, 1)
            else:
                nc.vector.tensor_copy(lens_f[:], lens_i[:]).then_inc(bo_gated, 1)
                dve.wait_ge(bo_gated, 1)

            def ln_stats(b, n, x_par):
                dve.wait_ge(x_loaded[x_par], (n + 1) * 16)
                for c in range(TC):
                    last = nc.vector.bn_stats(stats[:, c, :], keep.x[:, b * TC + c, :])
                last.then_inc(stats_done, 1)

            def ln_mean(b):
                for c in range(TC):
                    last = nc.vector.bn_aggr(mean_var[:, c, :], stats[:, c, :])
                last.then_inc(mean_done, 1)

            def ln_apply(b, p):
                dve.wait_ge(rstd_done, b + 1)
                need(dve, xn_turned, b - 1)
                for c in range(TC):
                    last = nc.vector.tensor_scalar(xn[p][:, c, :], keep.x[:, b * TC + c, :], mean_var[:, c, 0:1],
                                                   rstd[:, c:c + 1], ALU.subtract, ALU.mult)
                last.then_inc(xn_ready, 1)

            dve.wait_ge(wo_cleared, 2)
            dve.wait_ge(w_loaded, 64)
            for c in range(KC):
                last = nc.vector.tensor_copy(wo_rows[:, c, :, 0:HD], w_rows[:, 3, c, :].rearrange("p (h w) -> p h w", w=HD))
            last.then_inc(wo_spread, 1)
            for n in range(3):
                dve.wait_ge(w_hi_done, n + 1)
                nc.vector.tensor_tensor(w_view(w_t[1], n), stage_view(n), w_view(w_t[0], n).bitcast(F32), ALU.subtract).then_inc(w_ready, 1)
            ln_stats(0, 0, 0)
            dve.wait_ge(stats_done, 1)
            ln_mean(0)
            ln_apply(0, 0)

            def evac_k(i):
                b, p = i.at(2), i.par(2)
                need(dve, part_rest, b - 1)
                if causal:
                    dve.wait_ge(k_done, b + 1)
                    nc.vector.tensor_copy(qk[p][:, KC:2 * KC, :].rearrange("p c s -> p (c s)"), stage[0][:]).then_inc(k_ready, 1)
                else:
                    n = bass.ds(b, 1)
                    nc.vector.tensor_scalar(valid[:], iota_t[:], lens_f[:, n], None, ALU.is_lt).then_inc(valid_done, 1)
                    if i.has(0):
                        dve.wait_ge(stacked[1][p], i.half(2) * 16 * STACK_DMAS)
                    nc.vector.tensor_scalar(mask_row[p][STACK:STACK + 2, :], iota_t[STACK:STACK + 2, :], lens_f[STACK:STACK + 2, n],
                                            neg_col[STACK:STACK + 2, :], ALU.is_ge, ALU.mult).then_inc(valid_done, 1)
                    dve.wait_ge(valid_done, 2 * b + 2)
                    dve.wait_ge(k_done, b + 1)
                    nc.vector.tensor_tensor(qk[p][:, KC:2 * KC, :], stage[0][:].rearrange("p (c s) -> p c s", c=KC),
                                            valid[:].unsqueeze(1).to_broadcast((P, KC, S)), ALU.mult).then_inc(k_ready, 1)

            def step(i):
                if i.has(-1):
                    b, p = i.at(-1), i.par(-1)
                    dve.wait_ge(den_picked, b + 1)
                    nc.vector.reciprocal(den_recip[:].rearrange("p c h -> p (c h)"), stage[1][:, 0:TC * H]).then_inc(recip_done, 1)
                if i.has(2):
                    evac_k(i)
                def divide():
                    b, p = i.at(-1), i.par(-1)
                    need(dve, o_done, b - 1)
                    for n in range(GROUPS // PER_BANK):
                        gs = slice(n * PER_BANK, (n + 1) * PER_BANK)
                        dve.wait_ge(recip_spread, b * (GROUPS // PER_BANK) + n + 1)
                        nc.vector.tensor_tensor(heads_t[p][:, gs, :].rearrange("p g s -> p (g s)"), mixed[:, gs, :].rearrange("p g s -> p (g s)"),
                                                pv[n][:], ALU.mult).then_inc(heads_t_ready, 1)

                def update_x():
                    b = i.at(-1)
                    dve.wait_ge(o_done, b + 1)
                    if causal:
                        dve.wait_ge(x_biased, b + 1)
                    rows = keep.x[:, bass.ds(b * TC, TC), :].rearrange("p c d -> p (c d)")
                    nc.vector.scalar_tensor_tensor(out=rows, in0=stage[1][:], scalar=keep.tanh_gates[:, gate_col:gate_col + 1],
                                                   in1=rows, op0=ALU.mult, op1=ALU.add).then_inc(x_updated, 1)

                def evac_v():
                    b, p = i.at(1), i.par(1)
                    dve.wait_ge(v_done, b + 1)
                    need(dve, pv_done, (b - 1) * GROUPS)
                    out = v_ones[p][:].rearrange("p c h w -> p (c h) w")[:, :, 0:HD]
                    src = stage[1][:].rearrange("p (n w) -> p n w", w=HD)
                    if causal:
                        nc.vector.tensor_tensor(out, src, bv_rows[:].rearrange("p c (h w) -> p (c h) w", w=HD), ALU.add).then_inc(v_ready, 1)
                    else:
                        nc.vector.tensor_copy(out, src).then_inc(v_ready, 1)

                def turned_lo(parts, bank, hi_done, ready):
                    hi, lo = (x[:].rearrange("p c s -> p (c s)") for x in parts[i.par(3)])
                    dve.wait_ge(hi_done, i.at(3) + 1)
                    nc.vector.tensor_tensor(lo, bank[:], hi.bitcast(F32), ALU.subtract).then_inc(ready, 1)

                between = {}
                if i.has(-1):
                    between |= {2: divide, 5: update_x}
                if i.has(1):
                    between |= {7: evac_v}
                if i.has(4):
                    b4 = i.at(4)
                    between |= {10: lambda: ln_stats(b4, i.half(4), i.par(4)), 11: lambda: ln_mean(b4), 13: lambda: ln_apply(b4, i.par(4))}
                if i.has(3):
                    between |= {9: lambda: turned_lo(xn_t, stage[0], xn_hi_done, xn_t_ready),
                                12: lambda: turned_lo(ctx_t, stage[1], ctx_hi_done, ctx_t_ready)}
                for h in range(H):
                    if h == 11 and i.has(4):
                        dve.wait_ge(stats_done, i.at(4) + 1)
                    if i.has(1):
                        dve.wait_ge(scores_done, i.at(1) * H + h + 1)
                        bank = scores[h % 2]
                        if causal:
                            nc.vector.reduce_max(row_max[:, 0, h:h + 1], bank[:, 0:P], AX_X)
                            nc.vector.reduce_max(row_max[:, 1, h:h + 1], bank[:, P:3 * P], AX_X).then_inc(maxed, 1)
                        else:
                            nc.vector.reduce_max(row_max[:, :, h], bank[:].rearrange("p (c t) -> p c t", c=TC), AX_X).then_inc(maxed, 1)
                    if h in between:
                        between[h]()
                if i.has(1):
                    b = i.at(1)
                    dve.wait_ge(maxed, (b + 1) * H)
                    need(dve, max_turned, b)
                    nc.vector.tensor_scalar(max_parts[:, :, 0, :], row_max[:], -1.0, None, ALU.mult).then_inc(max_hi, 1)
                    dve.wait_ge(max_hi, b + 1)
                    nc.vector.scalar_tensor_tensor(out=max_rest[:], in0=row_max[:], scalar=-1.0, in1=max_parts[:, :, 0, :],
                                                   op0=ALU.mult, op1=ALU.subtract).then_inc(max_r1, 1)
                    dve.wait_ge(max_r1, b + 1)
                    nc.vector.tensor_copy(max_parts[:, :, 1, :], max_rest[:]).then_inc(max_mid, 1)
                    dve.wait_ge(max_mid, b + 1)
                    nc.vector.tensor_tensor(max_parts[:, :, 2, :], max_rest[:], max_parts[:, :, 1, :], ALU.subtract).then_inc(max_ready, 1)

            pipeline(dve, step, B, FIRST, LAST, HEAD, TAIL)

        @block.scalar
        def _(act):
            for n in range(3):
                act.wait_ge(w_turned, n + 1)
                nc.scalar.activation(w_view(w_t[0], n), stage_view(n), ACT.Copy).then_inc(w_hi_done, 1)
            for n in range(GROUPS // 2):
                act.wait_ge(w_turned, 4 + n)
                nc.scalar.activation(wo_t[:, 2 * n:2 * n + 2].rearrange("p g d -> p (g d)"), stage[(3 + n) % 2][:], ACT.Copy).then_inc(wo_ready, 1)

            def cut_hi(i):
                b, p = i.at(2), i.par(2)
                act.wait_ge(q_ready, b + 1)
                act.wait_ge(k_ready, b + 1)
                need(act, parts_stored[p], i.half(2) * 16)
                nc.scalar.activation(parts[p][:, :, 0, :], qk[p][:], ACT.Copy).then_inc(part_hi, 1)

            def cut_mid(i):
                act.wait_ge(part_rest, i.at(2) + 1)
                nc.scalar.activation(parts[i.par(2)][:, :, 1, :], rest[:], ACT.Copy).then_inc(part_mid, 1)

            def evac_xn(i):
                b, p = i.at(3), i.par(3)
                act.wait_ge(xn_turned, b + 1)
                need(act, q_done, b - 1)
                nc.scalar.activation(xn_t[p][0][:].rearrange("p c s -> p (c s)"), stage[0][:], ACT.Copy).then_inc(xn_hi_done, 1)

            def evac_ctx(i):
                b, p = i.at(3), i.par(3)
                act.wait_ge(ctx_turned, b + 1)
                need(act, v_done, b - 1)
                nc.scalar.activation(ctx_t[p][0][:].rearrange("p c s -> p (c s)"), stage[1][:], ACT.Copy).then_inc(ctx_hi_done, 1)

            def copy_mixed(i, n):
                b = i.at(0)
                act.wait_ge(pv_done, b * GROUPS + (n + 1) * PER_BANK)
                need(act, heads_t_ready, (b - 1) * (GROUPS // PER_BANK) + n + 1)
                nc.scalar.activation(mixed[:, n * PER_BANK:(n + 1) * PER_BANK, :].rearrange("p g s -> p (g s)"),
                                     pv[n][:], ACT.Copy).then_inc(mixed_ready, 1)

            def step(i):
                if i.has(2):
                    b, p = i.at(2), i.par(2)
                    act.wait_ge(q_done, b + 1)
                    need(act, part_rest, b - 1)
                    nc.scalar.activation(qk[p][:, 0:KC, :].rearrange("p c s -> p (c s)"), stage[0][:], ACT.Copy, scale=scale).then_inc(q_ready, 1)
                if i.has(0):
                    b, p = i.at(0), i.par(0)
                    act.wait_ge(max_turned, b + 1)
                    need(act, max_stacked[p], i.half(0) * 48)
                    nc.scalar.activation(max_t[p][:], stage[1][0:3 * H, 0:S // 2].bitcast(BF16), ACT.Copy).then_inc(max_t_ready, 1)
                    act.wait_ge(max_t_ready, b + 1)
                    for j in range(3):
                        act.dma_start(q_stack[p][MAX_ROW + j:MAX_ROW + j + 1, :, :],
                                      max_t[p][j * H:(j + 1) * H, :]).then_inc(max_stacked[p], 16)
                if i.has(-1):
                    b = i.at(-1)
                    act.wait_ge(recip_done, b + 1)
                    need(act, recip_spread, b * (GROUPS // PER_BANK))
                    nc.scalar.activation(strip_recip[:].rearrange("p c h w -> p (c h) w"),
                                         den_recip[:].rearrange("p c h -> p (c h)").unsqueeze(2).to_broadcast((P, TC * H, VW)),
                                         ACT.Copy).then_inc(recip_copied, 1)
                between = {}
                if i.has(0):
                    between |= {12: lambda: copy_mixed(i, 0), 15: lambda: copy_mixed(i, 1)}
                if i.has(2):
                    between |= {1: lambda: cut_hi(i), 5: lambda: cut_mid(i)}
                if i.has(3):
                    between |= {8: lambda: evac_xn(i), 10: lambda: evac_ctx(i)}
                for h in range(H):
                    if i.has(0):
                        b = i.at(0)
                        width = 3 * P if causal else 4 * P
                        act.wait_ge(scores_t_done, b * H + h + 1)
                        if h % GH == 0:
                            need(act, pv_done, b * GROUPS + h // GH - 1)
                        nc.scalar.activation(probs[h % NP][:, 0:width], scores_t[h % 2][:, 0:width], ACT.Exp).then_inc(probs_ready, 1)
                    if h in between:
                        between[h]()

            pipeline(act, step, B, FIRST, LAST, HEAD, TAIL)

        @block.tensor
        def _(pe):
            pe.wait_ge(w_loaded, 64)
            for n in range(3):
                need(pe, w_ready, n - 1)
                for kc in range(KC):
                    for oc in range(KC):
                        last = nc.tensor.transpose(stage[n % 2][:, kc * D + oc * P:kc * D + oc * P + P],
                                                   w_rows[:, n, oc, kc * P:kc * P + P], keep.ident[:])
                last.then_inc(w_turned, 1)
            pe.wait_ge(wo_spread, 1)
            pe.wait_ge(wo_cleared, 3)
            for n in range(GROUPS // 2):
                pe.wait_ge(w_ready, n + 2)
                for k in range(2):
                    g = 2 * n + k
                    for oc in range(KC):
                        last = nc.tensor.transpose(stage[(3 + n) % 2][:, k * D + oc * P:k * D + oc * P + P],
                                                   wo_rows[:, oc, g * GH:(g + 1) * GH, :].rearrange("p h w -> p (h w)"), keep.ident[:])
                last.then_inc(w_turned, 1)
            pe.wait_ge(w_ready, 3)
            pe.wait_ge(wo_ready, GROUPS // 2)
            pe.wait_ge(consts_ready, N_READY)

            def turn(bank, rows, done):
                for kc in range(KC):
                    for c in range(TC):
                        last = nc.tensor.transpose(bank[:, kc * S + c * P:kc * S + c * P + P], rows[:, c, kc * P:kc * P + P], keep.ident[:])
                last.then_inc(done, 1)

            TERMS = ((0, 0), (0, 1), (1, 0))

            def project_t(bank, n, cols, done):
                for m in range(KC):
                    for kc in range(KC):
                        for w, x in TERMS:
                            last = nc.tensor.matmul(bank[:, m * S:(m + 1) * S], w_t[w][:, n, kc, m * P:(m + 1) * P], cols[x][:, kc, :],
                                                    start=(kc == 0 and (w, x) == TERMS[0]), stop=(kc == KC - 1 and (w, x) == TERMS[-1]))
                last.then_inc(done, 1)

            def project(bank, n, cols, done):
                for c in range(TC):
                    for kc in range(KC):
                        for w, x in TERMS:
                            last = nc.tensor.matmul(bank[:, c * D:(c + 1) * D], cols[x][:, kc, c * P:(c + 1) * P], w_t[w][:, n, kc, :],
                                                    start=(kc == 0 and (w, x) == TERMS[0]), stop=(kc == KC - 1 and (w, x) == TERMS[-1]))
                last.then_inc(done, 1)

            def pick_dens(i):
                pe.wait_ge(mixed_ready, i.at(-1) * 2 + 2)
                for c in range(TC):
                    for g in range(GROUPS):
                        at = c * H + g * GH
                        last = nc.tensor.matmul(stage[1][:, at:at + GH], mixed[:, g, c * P:(c + 1) * P], den_rows[:], start=True, stop=True)
                last.then_inc(den_picked, 1)

            def spread_recips(i):
                pe.wait_ge(recip_copied, i.at(-1) + 1)
                for g in range(GROUPS):
                    for c in range(TC):
                        at = g % PER_BANK * S + c * P
                        last = nc.tensor.matmul(pv[g // PER_BANK][:, at:at + P],
                                                strip_recip[:, c, g * GH:(g + 1) * GH, :].rearrange("p h w -> p (h w)"),
                                                keep.ident[:], start=True, stop=True)
                    if g % PER_BANK == PER_BANK - 1:
                        last.then_inc(recip_spread, 1)

            def front(i):
                if i.has(0):
                    need(pe, ctx_t_ready, i.upto(2))
                    need(pe, v_ready, i.upto(0))
                    need(pe, x_updated, i.at(-1))
                if i.has(2):
                    b, p = i.at(2), i.par(2)
                    pe.wait_ge(xn_t_ready, b + 1)
                    project_t(stage[0], 0, xn_t[p], q_done)
                if i.has(0):
                    wait_apart(pe, max_ready, i.at(0) + 1, consts_ready, N_READY)
                    turned = stage[1][0:3 * H, 0:S // 2].bitcast(BF16)
                    for c in range(TC):
                        last = nc.tensor.transpose(turned[:, c * P:(c + 1) * P], max_parts[:, c].rearrange("p j h -> p (j h)"), keep.ident16[:])
                    last.then_inc(max_turned, 1)
                if i.has(2):
                    b, p = i.at(2), i.par(2)
                    pe.wait_ge(ctx_t_ready, b + 1)
                    pe.wait_ge(q_ready, b + 1)
                    project_t(stage[0], 1, ctx_t[p], k_done)
                if i.has(-1):
                    need(pe, max_t_ready, i.upto(0))
                    need(pe, v_ready, i.upto(0))
                    need(pe, x_updated, i.at(-1))
                    pick_dens(i)

            def project_heads(i):
                pe.wait_ge(heads_t_ready, i.at(-1) * 2 + 2)
                for c in range(TC):
                    for g in range(GROUPS):
                        last = nc.tensor.matmul(stage[1][:, c * D:(c + 1) * D], heads_t[i.par(-1)][:, g, c * P:(c + 1) * P], wo_t[:, g, :],
                                                start=(g == 0), stop=(g == GROUPS - 1))
                last.then_inc(o_done, 1)

            def project_v(i):
                need(pe, ctx_t_ready, i.upto(2))
                need(pe, max_t_ready, i.upto(0))
                need(pe, x_updated, i.at(0))
                project(stage[1], 2, ctx_t[i.par(1)], v_done)

            def turn_xn(i):
                b, p = i.at(3), i.par(3)
                pe.wait_ge(xn_ready, b + 1)
                need(pe, k_ready, i.upto(2))
                turn(stage[0], xn[p], xn_turned)

            def turn_ctx(i):
                p = i.par(3)
                pe.wait_ge(ctx_loaded[p], (i.half(3) + 1) * 16)
                need(pe, v_ready, i.upto(1))
                need(pe, x_updated, i.at(0))
                turn(stage[1], ctx_rows[p], ctx_turned)

            def score_head(i, h):
                b, p = i.at(1), i.par(1)
                if h % HH == 0:
                    pe.wait_ge(stacked[h // HH][p], (i.half(1) + 1) * 16 * STACK_DMAS)
                need(pe, maxed, b * H + h - 1)
                bank, q, k = scores[h % 2], q_stack[p], k_stack[p]
                rows = slice(0, STACK + MASK_ROWS)
                if causal:
                    nc.tensor.matmul(bank[:, 0:P], keep.ident16[:], mask_st[:, 0, :], start=True, stop=False)
                    nc.tensor.matmul(bank[:, 0:P], q[rows, h, 0:P], k[rows, h, 0:P], start=False, stop=True)
                    nc.tensor.matmul(bank[:, P:2 * P], q[rows, h, P:S], k[rows, h, 0:P], start=True, stop=True)
                    nc.tensor.matmul(bank[:, 2 * P:3 * P], keep.ident16[:], mask_st[:, 1, :], start=True, stop=False)
                    last = nc.tensor.matmul(bank[:, 2 * P:3 * P], q[rows, h, P:S], k[rows, h, P:S], start=False, stop=True)
                else:
                    for c in range(TC):
                        last = nc.tensor.matmul(bank[:, c * S:(c + 1) * S], q[rows, h, c * P:(c + 1) * P], k[rows, h, :], start=True, stop=True)
                last.then_inc(scores_done, 1)

            def score_head_t(i, h):
                b, p = i.at(0), i.par(0)
                if h == 0:
                    pe.wait_ge(max_stacked[p], (i.half(0) + 1) * 48)
                need(pe, probs_ready, b * H + h - 1)
                bank, q, k = scores_t[h % 2], q_stack[p], k_stack[p]
                rows = slice(0, MAX_ROW + 3)
                if causal:
                    nc.tensor.matmul(bank[:, 0:P], keep.ident16[:], mask_ts[:, 0, :], start=True, stop=False)
                    nc.tensor.matmul(bank[:, 0:P], k[rows, h, 0:P], q[rows, h, 0:P], start=False, stop=True)
                    nc.tensor.matmul(bank[:, P:2 * P], k[rows, h, 0:P], q[rows, h, P:S], start=True, stop=True)
                    nc.tensor.matmul(bank[:, 2 * P:3 * P], keep.ident16[:], mask_ts[:, 1, :], start=True, stop=False)
                    last = nc.tensor.matmul(bank[:, 2 * P:3 * P], k[rows, h, P:S], q[rows, h, P:S], start=False, stop=True)
                else:
                    for c in range(TC):
                        last = nc.tensor.matmul(bank[:, c * S:(c + 1) * S], k[rows, h, c * P:(c + 1) * P], q[rows, h, :], start=True, stop=True)
                last.then_inc(scores_t_done, 1)

            def mix_group(i, g):
                b, p = i.at(0), i.par(0)
                pe.wait_ge(probs_ready, b * H + (g + 1) * GH)
                if g == 0:
                    pe.wait_ge(v_ready, b + 1)
                if g % PER_BANK == 0:
                    need(pe, heads_t_ready, (b - 1) * 2 + g // PER_BANK + 1)
                bank, at = pv[g // PER_BANK], g % PER_BANK * S
                for t in range(TC):
                    first, col = (t * P, t * S) if causal else (0, t * S)
                    for n in range(GH):
                        h = g * GH + n
                        last = nc.tensor.matmul(bank[n * VW:(n + 1) * VW, at + first:at + S], v_ones[p][:, t, h, :],
                                                probs[h % NP][:, col:col + S - first], start=(t == 0), stop=(t == TC - 1),
                                                tile_position=(0, n * VW))
                last.then_inc(pv_done, 1)

            def step(i):
                front(i)
                between = {}
                if i.has(-1):
                    between |= {1: spread_recips, 4: project_heads}
                if i.has(1):
                    between |= {6: project_v}
                if i.has(3):
                    between |= {8: turn_xn, 9: turn_ctx}
                for h in range(H):
                    if i.has(1):
                        score_head(i, h)
                    if i.has(0):
                        score_head_t(i, h)
                        if h % GH == 1 and h > GH:
                            mix_group(i, h // GH - 1)
                    if h in between:
                        between[h](i)
                if i.has(0):
                    mix_group(i, GROUPS - 1)

            pipeline(pe, step, B, FIRST, LAST, HEAD, TAIL)

    clear_semaphores(nc, all_sems)


TS = 256
TT = TS // P
ROW = 258
EXPERTS = 8


def region_rows(tokens):
    return tokens + TS


def tile_count(tokens):
    return 2 * tokens // TS + EXPERTS


SPARE_TILES = 3


def routed_rows(tokens):
    return EXPERTS * region_rows(tokens) + SPARE_TILES * TS


class Routed:

    def __init__(self, nc, ctx, layer, tokens, D, F):
        tag = f"t{layer}_"

        def sb(name, shape, dt=F32):
            return ctx.enter_context(nc.sbuf_tensor(tag + name, shape, dt))

        def sem(name):
            s = ctx.enter_context(nc.semaphore(tag + name))
            self.all_sems.append(s)
            return s

        tiles = tile_count(tokens) + 2
        self.all_sems = []
        self.used_tiles = sb("used_tiles", [P, 1], I32)
        self.tile_expert = sb("tile_expert", [P, 1 + tiles], I32)
        self.tile_group = sb("tile_group", [P, 2 + tiles], I32)
        self.tile_row = sb("tile_row", [P, tiles], I32)
        self.up_bias = sb("up_bias", [P, EXPERTS * F // P])
        self.pad_rows = sb("pad_rows", [P, TT, ROW])
        self.pad_slot = sb("pad_slot", [P, EXPERTS, TT], U32)
        self.up = [sb(f"up{n}", [P, D // P, F]) for n in range(2)]
        self.down = [sb(f"down{n}", [P, F // P, D]) for n in range(2)]
        self.down_bias = sb("down_bias", [P, EXPERTS, D])
        self.w_loaded = [sem(f"w_loaded{n}") for n in range(2)]
        self.bias_loaded = sem("bias_loaded")

    def load_weights(self, eng, up_w, down_w, e, n):
        eng.dma_start(self.up[n][:], up_w[e].rearrange("(c p) f -> p c f", p=P)).then_inc(self.w_loaded[n], 16)
        eng.dma_start(self.down[n][:], down_w[e].rearrange("(c p) d -> p c d", p=P)).then_inc(self.w_loaded[n], 16)


def route_phase(nc, keep, routed, layer, F, up_w, up_b, down_w, down_b, gate, shared, xs, x_acc):
    NT = keep.x.shape[1]
    D = keep.x.shape[2]
    C, KC = 2, D // P
    S = C * P
    NB = NT // C
    tokens = NT * P
    R = region_rows(tokens)
    E = EXPERTS
    FC = F // P
    tiles = tile_count(tokens) + 2
    soft = layer == 0
    gate_col = 2 + layer
    GW = E if soft else D + E
    tag = f"r{layer}_"
    J = tokens // TS

    all_sems = []
    with ExitStack() as ctx:
        def sb(name, shape, dt=F32):
            return ctx.enter_context(nc.sbuf_tensor(tag + name, shape, dt))

        def sem(name):
            s = ctx.enter_context(nc.semaphore(tag + name))
            all_sems.append(s)
            return s

        xn = [sb(f"xn{n}", [P, C, D]) for n in range(2)]
        rows = [sb(f"rows{n}", [P, 2, C, ROW]) for n in range(2)]
        stats = sb("stats", [P, C, 6])
        mean_var = sb("mean_var", [P, C, 2])
        var_eps = sb("var_eps", [P, C])
        eps = sb("eps", [P, C])
        minus_half = sb("minus_half", [P, C])
        rstd = sb("rstd", [P, C])
        xn_t = sb("xn_t", [P, KC, S])
        gate_w = sb("gate_w", [P, KC, GW])
        scores = sb("scores", [P, C, E])
        top = sb("top", [P, C, E])
        top_index = sb("top_index", [P, C, E], U32)
        top_index_f = sb("top_index_f", [P, 2, C])
        below_top = sb("below_top", [P, C, E])
        exps = sb("exps", [P, C, E])
        exp_sum = sb("exp_sum", [P, C])
        exp_recip = sb("exp_recip", [P, C])
        share = sb("share", [P, C, 2])
        share_sum = sb("share_sum", [P, C])
        share_recip = sb("share_recip", [P, C])
        one_hot = sb("one_hot", [P, 2, C, E])
        chosen = sb("chosen", [P, C, E], BF16)
        next_row = sb("next_row", [P, E])
        place = sb("place", [P, C, E])
        place_of = sb("place_of", [P, 2, C, E])
        slot_f = sb("slot_f", [P, 2, C])
        slot = [sb(f"slot{n}", [P, 2, C], U32) for n in range(2)]
        expert_iota = sb("expert_iota", [P, E])
        region_start = sb("region_start", [P, E])
        token_ids = sb("token_ids", [P, NT])
        ones16 = sb("ones16", [P, P], BF16)
        before16 = sb("before16", [P, P], BF16)
        pad_rows = routed.pad_rows
        pad_offset = sb("pad_offset", [P, TT])
        pad_slot_f = sb("pad_slot_f", [P, E, TT])
        pad_slot = routed.pad_slot
        count = sb("count", [P, E])
        full_steps = sb("full_steps", [P, J])
        beyond = sb("beyond", [P, E, J])
        n_tiles = sb("n_tiles", [P, E])
        ends = sb("ends", [P, E])
        tile_iota = sb("tile_iota", [P, tiles])
        past = sb("past", [P, tiles, E])
        past_tiles = sb("past_tiles", [P, tiles, E])
        region = sb("region", [P, tiles])
        first_tile = sb("first_tile", [P, tiles])
        in_region = sb("in_region", [P, tiles])
        row_f = sb("row_f", [P, tiles])
        group_f = sb("group_f", [P, tiles])
        up_b_rows = sb("up_b_rows", [E * FC, P])
        if soft:
            gate_rows = sb("gate_rows", [E, D])
            sh_up = sb("sh_up", [P, KC, D])
            sh_down = sb("sh_down", [P, KC, D])
            sh_up_bias = sb("sh_up_bias", [P, KC])
            sh_up_b_rows = sb("sh_up_b_rows", [KC, P])
            sh_down_bias = sb("sh_down_bias", [P, D])
            sh_hidden = sb("sh_hidden", [P, KC, S])
        else:
            wp_rows = sb("wp_rows", [P, KC, D])
            sim_rows = sb("sim_rows", [E, D])
            sim_sq = sb("sim_sq", [E, D])
            sim_ss = sb("sim_ss", [E, 1])
            sim_ss_min = sb("sim_ss_min", [E, 1])
            sim_rnorm = sb("sim_rnorm", [E, 1])
            sim_unit = sb("sim_unit", [E, D])
            sim_t = sb("sim_t", [P, KC, E])
            temp = sb("temp", [P, 1])
            temp_recip = sb("temp_recip", [P, 1])
            proj_sq = sb("proj_sq", [P, C, D])
            proj_ss = sb("proj_ss", [P, C])
            proj_ss_min = sb("proj_ss_min", [P, C])
            proj_rnorm = sb("proj_rnorm", [P, C])

        def bank(name):
            return ctx.enter_context(nc.psum_tensor(tag + name, [P, 512], F32))

        turned = bank("turned")
        gated = [[bank(f"gated{n}_{c}") for c in range(1 if soft else C)] for n in range(2)]
        ranked = bank("ranked")
        if soft:
            sh_h = bank("sh_h")
            sh_y = bank("sh_y")

        w_loaded = sem("w_loaded")
        consts_step = sem("consts_step")
        consts_ready = sem("consts_ready")
        prep_turned = sem("prep_turned")
        prep_copied = sem("prep_copied")
        sim_step = sem("sim_step")
        temp_done = sem("temp_done")
        stats_done = sem("stats_done")
        mean_done = sem("mean_done")
        eps_added = sem("eps_added")
        rstd_done = sem("rstd_done")
        xn_ready = sem("xn_ready")
        rows_copied = sem("rows_copied")
        xn_turned = sem("xn_turned")
        xn_t_ready = sem("xn_t_ready")
        gate_done = sem("gate_done")
        ss_done = sem("ss_done")
        ss_floored = sem("ss_floored")
        rnorm_done = sem("rnorm_done")
        scores_ready = sem("scores_ready")
        top_done = sem("top_done")
        index_done = sem("index_done")
        below_done = sem("below_done")
        exps_done = sem("exps_done")
        index_f_done = sem("index_f_done")
        one_hot_done = sem("one_hot_done")
        chosen_ready = sem("chosen_ready")
        share_step = sem("share_step")
        rank_done = sem("rank_done")
        placed = sem("placed")
        counted = sem("counted")
        place_picked = sem("place_picked")
        slot_summed = sem("slot_summed")
        rows_ready = sem("rows_ready")
        rows_sent = keep.rows_sent[layer]
        table_step = sem("table_step")
        x_stored = sem("x_stored")
        if soft:
            x_biased = sem("x_biased")
            sh_bias_gated = sem("sh_bias_gated")
            sh_up_done = sem("sh_up_done")
            sh_hidden_ready = sem("sh_hidden_ready")
            sh_down_done = sem("sh_down_done")
            x_updated = sem("x_updated")

        acc_tiles = x_acc[0:tokens, :].rearrange("(n c p) d -> n p c d", c=C, p=P)
        N_LOADS = 6 if soft else 4
        FIRST, LAST, HEAD, TAIL = -3, NB - 1, 5, 4
        SHARES = 5 if soft else 2

        block = ctx.enter_context(nc.Block())

        @block.sync
        def _(sp):
            sp.dma_start(up_b_rows[:], up_b.rearrange("e (c p) -> (e c) p", p=P)).then_inc(w_loaded, 16)
            if soft:
                sh_up_w, sh_up_b, sh_down_w, sh_down_b = shared
                sp.dma_start(gate_rows[:], gate[0]).then_inc(w_loaded, 16)
                sp.dma_start(sh_up[:], sh_up_w.rearrange("(c p) f -> p c f", p=P)).then_inc(w_loaded, 16)
                sp.dma_start(sh_down[:], sh_down_w.rearrange("(c p) d -> p c d", p=P)).then_inc(w_loaded, 16)
                sp.dma_start(sh_up_b_rows[:], sh_up_b.rearrange("(c p) -> c p", p=P)).then_inc(w_loaded, 16)
                sp.dma_start(sh_down_bias[:], sh_down_b.rearrange("(a d) -> a d", a=1).to_broadcast((P, D))).then_inc(w_loaded, 16)
            else:
                wp, sim, temperature = gate
                sp.dma_start(wp_rows[:], wp.rearrange("(c p) d -> p c d", p=P)).then_inc(w_loaded, 16)
                sp.dma_start(sim_rows[:], sim).then_inc(w_loaded, 16)
                sp.dma_start(temp[:], temperature.rearrange("(a d) -> a d", a=1).to_broadcast((P, 1))).then_inc(w_loaded, 16)
            for e in range(2):
                routed.load_weights(sp, up_w, down_w, e, e)
            sp.dma_start(routed.down_bias[:], down_b.rearrange("(a e) d -> a e d", a=1).to_broadcast((P, E, D))).then_inc(routed.bias_loaded, 16)
            sp.wait_ge(consts_ready, 1)
            for n in range(SPARE_TILES):
                at = E * R + n * TS
                sp.dma_start(xs[at:at + TS, :].rearrange("(c p) w -> p c w", p=P), pad_rows[:]).then_inc(x_stored, 16)
            sp.dma_start(x_acc[tokens:tokens + TS, :].rearrange("(c p) d -> p c d", p=P), pad_rows[:, :, 0:D]).then_inc(x_stored, 16)
            n_stores = SPARE_TILES + 1
            if soft:
                with sp.Fori(0, NB) as b:
                    sp.wait_ge(x_updated, b + 1)
                    sp.dma_start(acc_tiles[b], keep.x[:, bass.ds(b * C, C), :]).then_inc(x_stored, 16)
                n_stores += NB
            else:
                sp.dma_start(x_acc[0:tokens, :].rearrange("(n p) d -> p n d", p=P), keep.x[:]).then_inc(x_stored, 16)
                n_stores += 1
            sp.wait_ge(x_stored, n_stores * 16)

        @block.gpsimd
        def _(pool):
            nc.gpsimd.memset(pad_rows[:], 0.0).then_inc(consts_step, 1)
            nc.gpsimd.iota(token_ids[:], pattern=[[P, NT]], base=0, channel_multiplier=1,
                           allow_small_or_imprecise_dtypes=True)
            nc.gpsimd.iota(expert_iota[:], pattern=[[1, E]], base=0, channel_multiplier=0, allow_small_or_imprecise_dtypes=True)
            nc.gpsimd.iota(region_start[:], pattern=[[R, E]], base=0, channel_multiplier=0, allow_small_or_imprecise_dtypes=True)
            nc.gpsimd.iota(next_row[:], pattern=[[R, E]], base=0, channel_multiplier=0, allow_small_or_imprecise_dtypes=True)
            nc.gpsimd.iota(pad_offset[:], pattern=[[P, TT]], base=0, channel_multiplier=1, allow_small_or_imprecise_dtypes=True)
            nc.gpsimd.iota(tile_iota[:], pattern=[[1, tiles]], base=0, channel_multiplier=0, allow_small_or_imprecise_dtypes=True)
            nc.gpsimd.iota(full_steps[:], pattern=[[TS, J]], base=0, channel_multiplier=0,
                           allow_small_or_imprecise_dtypes=True).then_inc(consts_step, 1)
            nc.gpsimd.memset(minus_half[:], -0.5)
            nc.gpsimd.memset(eps[:], LN_EPS)
            nc.gpsimd.memset(ones16[:], 1.0)
            nc.gpsimd.memset(before16[:], 1.0).then_inc(consts_step, 1)
            pool.wait_ge(consts_step, 3)
            nc.gpsimd.memset(full_steps[:, 0:1], -1.0).then_inc(consts_step, 1)
            nc.gpsimd.affine_select(out=before16[:], in_=before16[:], compare_op=ALU.is_gt, fill=0.0, base=0,
                                    pattern=[[1, P]], channel_multiplier=-1).then_inc(consts_step, 1)
            nc.gpsimd.iota(pad_rows[:, :, D + 1], pattern=[[P, TT]], base=tokens, channel_multiplier=1,
                           allow_small_or_imprecise_dtypes=True).then_inc(consts_step, 1)
            pool.wait_ge(consts_step, 6)
            nc.gpsimd.memset(rstd[:], 1.0).then_inc(consts_ready, 1)
            if not soft:
                pool.wait_ge(sim_step, 1)
                nc.gpsimd.tensor_scalar(sim_ss_min[:], sim_ss[:], 1e-24, None, ALU.max).then_inc(sim_step, 1)
                pool.wait_ge(sim_step, 2)
                nc.gpsimd.tensor_tensor(sim_rnorm[:], sim_ss_min[:], minus_half[0:E, 0:1], ALU.pow).then_inc(sim_step, 1)

            def add_eps(b):
                pool.wait_ge(mean_done, b + 1)
                nc.gpsimd.tensor_tensor(var_eps[:], mean_var[:, :, 1], eps[:], ALU.add).then_inc(eps_added, 1)

            def rstd_of(b):
                pool.wait_ge(eps_added, b + 1)
                nc.gpsimd.tensor_tensor(rstd[:], var_eps[:], minus_half[:], ALU.pow).then_inc(rstd_done, 1)

            def bias_x(b):
                pool.wait_ge(xn_ready, b + 1)
                if isinstance(b, int) and b == 0:
                    pool.wait_ge(sh_bias_gated, 1)
                x_rows = keep.x[:, bass.ds(b * C, C), :]
                nc.gpsimd.tensor_tensor(x_rows, x_rows, sh_down_bias[:].unsqueeze(1).to_broadcast((P, C, D)), ALU.add).then_inc(x_biased, 1)

            def step(i):
                b, p = i.at(0), i.par(0)
                if i.has(3):
                    add_eps(i.at(3))
                    rstd_of(i.at(3))
                if i.has(0):
                    pool.wait_ge(rows_ready, b + 1)
                    pool.wait_ge(rows_copied, b + 1)
                if soft:
                    if i.has(2):
                        bias_x(i.at(2))
                elif i.has(1):
                    pool.wait_ge(ss_floored, i.at(1) + 1)
                    nc.gpsimd.tensor_tensor(proj_rnorm[:], proj_ss_min[:], minus_half[:], ALU.pow).then_inc(rnorm_done, 1)
                if i.has(0):
                    for k in range(2):
                        for c in range(C):
                            pool.indirect_dma_start(out=xs, out_offset=bass.IndirectOffsetOnAxis(ap=slot[p][:, k, c:c + 1], axis=0),
                                                    in_=rows[p][:, k, c, :], in_offset=None).then_inc(rows_sent[p], 16)

            pipeline(pool, step, NB, FIRST, LAST, HEAD, TAIL)
            for n in range(2):
                pool.wait_ge(rows_sent[n], 16 * 2 * C * NB // 2)

        @block.vector
        def _(dve):
            dve.wait_ge(consts_ready, 1)
            dve.wait_ge(w_loaded, 16 * N_LOADS)
            if soft:
                nc.vector.tensor_scalar(sh_down_bias[:], sh_down_bias[:], keep.tanh_gates[:, gate_col:gate_col + 1], None, ALU.mult).then_inc(sh_bias_gated, 1)
            else:
                nc.vector.reciprocal(temp_recip[:], temp[:]).then_inc(temp_done, 1)
                dve.wait_ge(sim_step, 3)
                nc.vector.tensor_scalar(sim_unit[:], sim_rows[:], sim_rnorm[:, 0:1], None, ALU.mult).then_inc(sim_step, 1)

            def ln(b):
                for c in range(C):
                    last = nc.vector.bn_stats(stats[:, c, :], keep.x[:, b * C + c, :])
                last.then_inc(stats_done, 1)

            def ln_mean(b):
                for c in range(C):
                    last = nc.vector.bn_aggr(mean_var[:, c, :], stats[:, c, :])
                last.then_inc(mean_done, 1)

            def ln_apply(i):
                b, p = i.at(2), i.par(2)
                dve.wait_ge(rstd_done, b + 1)
                need(dve, rows_copied, b - 1)
                need(dve, xn_turned, b - 1)
                for c in range(C):
                    last = nc.vector.tensor_scalar(xn[p][:, c, :], keep.x[:, b * C + c, :], mean_var[:, c, 0:1],
                                                   rstd[:, c:c + 1], ALU.subtract, ALU.mult)
                last.then_inc(xn_ready, 1)

            def floor_ss(b):
                dve.wait_ge(ss_done, b + 1)
                nc.vector.tensor_scalar(proj_ss_min[:], proj_ss[:], 1e-24, None, ALU.max).then_inc(ss_floored, 1)

            def step(i):
                b, p = i.at(0), i.par(0)
                if i.has(2):
                    ln_apply(i)
                if i.has(0):
                    dve.wait_ge(gate_done, b + 1)
                    if soft:
                        nc.vector.tensor_copy(scores[:], gated[p][0][:, 0:C * E].rearrange("p (c e) -> p c e", c=C)).then_inc(scores_ready, 1)
                    else:
                        dve.wait_ge(rnorm_done, b + 1)
                        for c in range(C):
                            last = nc.vector.tensor_scalar(scores[:, c, :], gated[p][c][:, D:D + E], proj_rnorm[:, c:c + 1], temp_recip[:, 0:1], ALU.mult, ALU.mult)
                        last.then_inc(scores_ready, 1)
                if i.has(3):
                    ln(i.at(3))
                if i.has(0):
                    choose(i)
                elif i.has(3):
                    dve.wait_ge(stats_done, i.at(3) + 1)
                    ln_mean(i.at(3))
                if not soft and i.has(1):
                    floor_ss(i.at(1))
                if i.has(0):
                    place_rows(i)

            def choose(i):
                b, p = i.at(0), i.par(0)
                wait_apart(dve, scores_ready, b + 1, consts_ready, 1)
                for c in range(C):
                    last = nc.vector.max(top[:, c, :], scores[:, c, :])
                last.then_inc(top_done, 1)
                wait_apart(dve, top_done, b + 1, consts_ready, 1)
                for c in range(C):
                    last = nc.vector.max_index(top_index[:, c, :], top[:, c, :], scores[:, c, :])
                last.then_inc(index_done, 1)
                if i.has(3):
                    dve.wait_ge(stats_done, i.at(3) + 1)
                nc.vector.tensor_tensor(below_top[:], top[:], top[:, :, 0:1].to_broadcast((P, C, E)), ALU.subtract).then_inc(below_done, 1)
                if i.has(3):
                    ln_mean(i.at(3))
                dve.wait_ge(index_done, b + 1)
                nc.vector.tensor_copy(top_index_f[:].rearrange("p k c -> p c k"), top_index[:, :, 0:2]).then_inc(index_f_done, 1)
                dve.wait_ge(index_f_done, b + 1)
                nc.vector.tensor_tensor(one_hot[:].rearrange("p k c e -> p (k c) e"),
                                        expert_iota[:].unsqueeze(1).to_broadcast((P, 2 * C, E)),
                                        top_index_f[:].rearrange("p k c -> p (k c)").unsqueeze(2).to_broadcast((P, 2 * C, E)),
                                        ALU.is_equal).then_inc(one_hot_done, 1)
                dve.wait_ge(one_hot_done, b + 1)
                nc.vector.tensor_tensor(chosen[:], one_hot[:, 0], one_hot[:, 1], ALU.add).then_inc(chosen_ready, 1)
                dve.wait_ge(exps_done, b + 1)
                steps = b * SHARES
                need(dve, rows_sent[p], i.half(0) * 16 * 2 * C)
                if soft:
                    nc.vector.reduce_sum(exp_sum[:], exps[:], AX_X).then_inc(share_step, 1)
                    dve.wait_ge(share_step, steps + 1)
                    nc.vector.reciprocal(exp_recip[:], exp_sum[:]).then_inc(share_step, 1)
                    dve.wait_ge(share_step, steps + 2)
                    nc.vector.tensor_tensor(share[:], exps[:, :, 0:2], exp_recip[:].unsqueeze(2).to_broadcast((P, C, 2)), ALU.mult).then_inc(share_step, 1)
                    dve.wait_ge(share_step, steps + 3)
                    nc.vector.scalar_tensor_tensor(out=share_sum[:], in0=share[:, :, 0], scalar=1e-20, in1=share[:, :, 1],
                                                   op0=ALU.add, op1=ALU.add).then_inc(share_step, 1)
                    dve.wait_ge(share_step, steps + 4)
                    parts2 = share
                else:
                    nc.vector.tensor_tensor(share_sum[:], exps[:, :, 0], exps[:, :, 1], ALU.add).then_inc(share_step, 1)
                    dve.wait_ge(share_step, steps + 1)
                    parts2 = exps
                nc.vector.reciprocal(share_recip[:], share_sum[:]).then_inc(share_step, 1)
                dve.wait_ge(share_step, steps + SHARES)
                nc.vector.scalar_tensor_tensor(out=rows[p][:, :, :, D].rearrange("p k c -> p c k"), in0=parts2[:, :, 0:2],
                                               scalar=keep.tanh_gates[:, gate_col:gate_col + 1],
                                               in1=share_recip[:].unsqueeze(2).to_broadcast((P, C, 2)), op0=ALU.mult, op1=ALU.mult)
                nc.vector.tensor_copy(rows[p][:, :, :, D + 1], token_ids[:, bass.ds(b * C, C)].unsqueeze(1).to_broadcast((P, 2, C)))

            def place_rows(i):
                b, p = i.at(0), i.par(0)
                dve.wait_ge(rank_done, b + 1)
                need(dve, counted, b)
                nc.vector.tensor_tensor(place[:], ranked[:, 0:C * E].rearrange("p (c e) -> p c e", c=C),
                                        next_row[:].unsqueeze(1).to_broadcast((P, C, E)), ALU.add).then_inc(placed, 1)
                dve.wait_ge(placed, b + 1)
                nc.vector.tensor_tensor(next_row[:], next_row[:], ranked[:, C * E:C * E + E], ALU.add).then_inc(counted, 1)
                nc.vector.tensor_tensor(place_of[:].rearrange("p k c e -> p k (c e)"), one_hot[:].rearrange("p k c e -> p k (c e)"),
                                        place[:].rearrange("p c e -> p (c e)").unsqueeze(1).to_broadcast((P, 2, C * E)), ALU.mult).then_inc(place_picked, 1)
                dve.wait_ge(place_picked, b + 1)
                nc.vector.reduce_sum(slot_f[:], place_of[:], AX_X).then_inc(slot_summed, 1)
                dve.wait_ge(slot_summed, b + 1)
                nc.vector.tensor_copy(slot[p][:], slot_f[:]).then_inc(rows_ready, 1)
                if soft:
                    dve.wait_ge(sh_down_done, b + 1)
                    dve.wait_ge(x_biased, b + 1)
                    x_rows = keep.x[:, bass.ds(b * C, C), :].rearrange("p c d -> p (c d)")
                    nc.vector.scalar_tensor_tensor(out=x_rows, in0=sh_y[:], scalar=keep.tanh_gates[:, gate_col:gate_col + 1],
                                                   in1=x_rows, op0=ALU.mult, op1=ALU.add).then_inc(x_updated, 1)

            pipeline(dve, step, NB, FIRST, LAST, HEAD, TAIL)

            steps = [0]

            def tail_step(ins):
                steps[0] += 1
                ins.then_inc(table_step, 1)
                dve.wait_ge(table_step, steps[0])

            dve.wait_ge(counted, NB)
            tail_step(nc.vector.tensor_tensor(pad_slot_f[:], next_row[:].unsqueeze(2).to_broadcast((P, E, TT)),
                                              pad_offset[:].unsqueeze(1).to_broadcast((P, E, TT)), ALU.add))
            nc.vector.tensor_copy(pad_slot[:], pad_slot_f[:])
            tail_step(nc.vector.tensor_tensor(count[:], next_row[:], region_start[:], ALU.subtract))
            tail_step(nc.vector.tensor_tensor(beyond[:], count[:].unsqueeze(2).to_broadcast((P, E, J)),
                                              full_steps[:].unsqueeze(1).to_broadcast((P, E, J)), ALU.is_gt))
            tail_step(nc.vector.reduce_sum(n_tiles[:], beyond[:], AX_X))
            tail_step(nc.vector.tensor_copy(ends[:, 0:1], n_tiles[:, 0:1]))
            for e in range(1, E):
                tail_step(nc.vector.tensor_tensor(ends[:, e:e + 1], ends[:, e - 1:e], n_tiles[:, e:e + 1], ALU.add))
            nc.vector.tensor_copy(routed.used_tiles[:], ends[:, E - 1:E])
            tail_step(nc.vector.tensor_tensor(past[:], tile_iota[:].unsqueeze(2).to_broadcast((P, tiles, E)),
                                              ends[:].unsqueeze(1).to_broadcast((P, tiles, E)), ALU.is_ge))
            tail_step(nc.vector.reduce_sum(region[:], past[:], AX_X))
            tail_step(nc.vector.tensor_tensor(past_tiles[:], past[:], n_tiles[:].unsqueeze(1).to_broadcast((P, tiles, E)), ALU.mult))
            tail_step(nc.vector.reduce_sum(first_tile[:], past_tiles[:], AX_X))
            tail_step(nc.vector.tensor_tensor(in_region[:], tile_iota[:], first_tile[:], ALU.subtract))
            tail_step(nc.vector.tensor_scalar(row_f[:], region[:], float(R), None, ALU.mult))
            tail_step(nc.vector.scalar_tensor_tensor(out=row_f[:], in0=in_region[:], scalar=float(TS), in1=row_f[:], op0=ALU.mult, op1=ALU.add))
            nc.vector.tensor_copy(routed.tile_row[:], row_f[:])
            tail_step(nc.vector.tensor_tensor(group_f[:], past[:, :, E - 1], in_region[:], ALU.mult))
            tail_step(nc.vector.tensor_tensor(group_f[:], group_f[:], region[:], ALU.add))
            nc.vector.tensor_copy(routed.tile_group[:, 0:1], group_f[:, 0:1])
            nc.vector.tensor_copy(routed.tile_group[:, 1:1 + tiles], group_f[:])
            nc.vector.tensor_scalar(routed.tile_group[:, 1 + tiles:2 + tiles], group_f[:, tiles - 1:tiles], 1.0, None, ALU.add)
            tail_step(nc.vector.tensor_scalar(region[:], region[:], float(E - 1), None, ALU.min))
            nc.vector.tensor_copy(routed.tile_expert[:, 0:1], region[:, 0:1])
            nc.vector.tensor_copy(routed.tile_expert[:, 1:1 + tiles], region[:])

        @block.scalar
        def _(act):
            act.wait_ge(prep_turned, 1)
            nc.scalar.activation(routed.up_bias[:], ranked[:, 0:E * FC], ACT.Copy).then_inc(prep_copied, 1)
            if soft:
                act.wait_ge(prep_turned, 2)
                nc.scalar.activation(gate_w[:], turned[:, 0:KC * E].rearrange("p (k e) -> p k e", k=KC), ACT.Copy).then_inc(prep_copied, 1)
                act.wait_ge(prep_turned, 3)
                nc.scalar.activation(sh_up_bias[:], ranked[:, 0:KC], ACT.Copy).then_inc(prep_copied, 1)
            else:
                act.wait_ge(w_loaded, 16 * N_LOADS)
                nc.scalar.activation(sim_sq[:], sim_rows[:], ACT.Square, accum_out=sim_ss[:, 0:1]).then_inc(sim_step, 1)
                act.wait_ge(prep_turned, 2)
                nc.scalar.activation(gate_w[:, :, 0:D], turned[:].rearrange("p (k d) -> p k d", k=KC), ACT.Copy).then_inc(prep_copied, 1)
                act.wait_ge(prep_turned, 3)
                nc.scalar.activation(sim_t[:], ranked[:, 0:KC * E].rearrange("p (k e) -> p k e", k=KC), ACT.Copy).then_inc(prep_copied, 1)
                act.wait_ge(prep_turned, 4)
                nc.scalar.activation(gate_w[:, :, D:D + E], turned[:, 0:KC * E].rearrange("p (k e) -> p k e", k=KC), ACT.Copy).then_inc(prep_copied, 1)

            def step(i):
                if i.has(0):
                    b, p = i.at(0), i.par(0)
                    act.wait_ge(xn_ready, b + 1)
                    need(act, rows_sent[p], i.half(0) * 16 * 2 * C)
                    nc.scalar.activation(rows[p][:, :, :, 0:D], xn[p][:].unsqueeze(1).to_broadcast((P, 2, C, D)), ACT.Copy).then_inc(rows_copied, 1)
                    act.wait_ge(below_done, b + 1)
                    nc.scalar.activation(exps[:], below_top[:], ACT.Exp).then_inc(exps_done, 1)
                if i.has(1):
                    b, p = i.at(1), i.par(1)
                    if soft:
                        act.wait_ge(sh_up_done, b + 1)
                        need(act, sh_down_done, b)
                        for fc in range(KC):
                            last = nc.scalar.activation(sh_hidden[:, fc, :], sh_h[:, fc * S:(fc + 1) * S], ACT.Silu, bias=sh_up_bias[:, fc:fc + 1])
                        last.then_inc(sh_hidden_ready, 1)
                    else:
                        act.wait_ge(gate_done, b + 1)
                        need(act, ss_floored, b)
                        for c in range(C):
                            last = nc.scalar.activation(proj_sq[:, c, :], gated[p][c][:, 0:D], ACT.Square, accum_out=proj_ss[:, c:c + 1])
                        last.then_inc(ss_done, 1)
                if i.has(2):
                    act.wait_ge(xn_turned, i.at(2) + 1)
                    nc.scalar.activation(xn_t[:].rearrange("p k s -> p (k s)"), turned[:], ACT.Copy).then_inc(xn_t_ready, 1)

            pipeline(act, step, NB, FIRST, LAST, HEAD, TAIL)

        @block.tensor
        def _(pe):
            pe.wait_ge(w_loaded, 16 * N_LOADS)
            nc.tensor.transpose(ranked[:, 0:E * FC], up_b_rows[:], keep.ident[0:E * FC, 0:E * FC]).then_inc(prep_turned, 1)
            if soft:
                for kc in range(KC):
                    last = nc.tensor.transpose(turned[:, kc * E:(kc + 1) * E], gate_rows[:, kc * P:(kc + 1) * P], keep.ident[0:E, 0:E])
                last.then_inc(prep_turned, 1)
                pe.wait_ge(prep_copied, 1)
                nc.tensor.transpose(ranked[:, 0:KC], sh_up_b_rows[:], keep.ident[0:KC, 0:KC]).then_inc(prep_turned, 1)
                pe.wait_ge(prep_copied, 3)
            else:
                for kc in range(KC):
                    for oc in range(KC):
                        last = nc.tensor.transpose(turned[:, kc * D + oc * P:kc * D + oc * P + P], wp_rows[:, oc, kc * P:kc * P + P], keep.ident[:])
                last.then_inc(prep_turned, 1)
                pe.wait_ge(prep_copied, 1)
                pe.wait_ge(sim_step, 4)
                for kc in range(KC):
                    last = nc.tensor.transpose(ranked[:, kc * E:(kc + 1) * E], sim_unit[:, kc * P:(kc + 1) * P], keep.ident[0:E, 0:E])
                last.then_inc(prep_turned, 1)
                pe.wait_ge(prep_copied, 3)
                for kc in range(KC):
                    for oc in range(KC):
                        last = nc.tensor.matmul(turned[:, kc * E:(kc + 1) * E], wp_rows[:, oc, kc * P:(kc + 1) * P], sim_t[:, oc, :],
                                                start=(oc == 0), stop=(oc == KC - 1))
                last.then_inc(prep_turned, 1)
                pe.wait_ge(prep_copied, 4)
            pe.wait_ge(consts_ready, 1)

            def turn(i):
                b, p = i.at(2), i.par(2)
                pe.wait_ge(xn_ready, b + 1)
                need(pe, xn_t_ready, b)
                for kc in range(KC):
                    for c in range(C):
                        last = nc.tensor.transpose(turned[:, kc * S + c * P:kc * S + c * P + P], xn[p][:, c, kc * P:(kc + 1) * P], keep.ident[:])
                last.then_inc(xn_turned, 1)

            def gate_block(i):
                b, p = i.at(1), i.par(1)
                pe.wait_ge(xn_t_ready, b + 1)
                need(pe, scores_ready, b - 1)
                for c in range(C):
                    out = gated[p][0][:, c * E:(c + 1) * E] if soft else gated[p][c][:, 0:GW]
                    for kc in range(KC):
                        last = nc.tensor.matmul(out, xn_t[:, kc, c * P:(c + 1) * P], gate_w[:, kc, :], start=(kc == 0), stop=(kc == KC - 1))
                last.then_inc(gate_done, 1)
                if soft:
                    need(pe, sh_hidden_ready, b)
                    for fc in range(KC):
                        for kc in range(KC):
                            last = nc.tensor.matmul(sh_h[:, fc * S:(fc + 1) * S], sh_up[:, kc, fc * P:(fc + 1) * P], xn_t[:, kc, :],
                                                    start=(kc == 0), stop=(kc == KC - 1))
                    last.then_inc(sh_up_done, 1)

            def shared_down(i):
                b = i.at(0)
                pe.wait_ge(sh_hidden_ready, b + 1)
                need(pe, x_updated, b)
                for c in range(C):
                    for fc in range(KC):
                        last = nc.tensor.matmul(sh_y[:, c * D:(c + 1) * D], sh_hidden[:, fc, c * P:(c + 1) * P], sh_down[:, fc, :],
                                                start=(fc == 0), stop=(fc == KC - 1))
                last.then_inc(sh_down_done, 1)

            def rank(i):
                b = i.at(0)
                pe.wait_ge(chosen_ready, b + 1)
                need(pe, counted, b)
                for c in range(C):
                    out = ranked[:, c * E:(c + 1) * E]
                    nc.tensor.matmul(out, before16[:], chosen[:, c, :], start=True, stop=(c == 0))
                    for q in range(c):
                        nc.tensor.matmul(out, ones16[:], chosen[:, q, :], start=False, stop=(q == c - 1))
                for c in range(C):
                    last = nc.tensor.matmul(ranked[:, C * E:C * E + E], ones16[:], chosen[:, c, :], start=(c == 0), stop=(c == C - 1))
                last.then_inc(rank_done, 1)

            def step(i):
                if soft and i.has(0):
                    shared_down(i)
                if i.has(1):
                    gate_block(i)
                if i.has(0):
                    rank(i)
                if i.has(2):
                    turn(i)

            pipeline(pe, step, NB, FIRST, LAST, HEAD, TAIL)

    clear_semaphores(nc, all_sems)


def expert_phase(nc, keep, routed, layer, F, act_func, up_w, down_w, xs, x_acc):
    D = keep.x.shape[2]
    tokens = keep.x.shape[1] * P
    E = EXPERTS
    KC, FC = D // P, F // P
    tiles = tile_count(tokens)
    tag = f"e{layer}_"
    PER_BANK = 512 // TS
    N_BANKS = max(1, FC // PER_BANK)
    split = F > D

    all_sems = []
    with ExitStack() as ctx:
        def sb(name, shape, dt=F32):
            return ctx.enter_context(nc.sbuf_tensor(tag + name, shape, dt))

        def sem(name):
            s = ctx.enter_context(nc.semaphore(tag + name))
            all_sems.append(s)
            return s

        up, down, down_bias = routed.up, routed.down, routed.down_bias
        xs_rows = [sb(f"xs_rows{n}", [P, TT, ROW]) for n in range(2)]
        xs_t = [sb(f"xs_t{n}", [P, KC, TS]) for n in range(2)]
        hidden = sb("hidden", [P, FC, TS])
        if split:
            xs_hi, xs_lo = ([sb(f"xs_{part}{n}", [P, KC, TS], F32R) for n in range(2)] for part in ("hi", "lo"))
            hidden_hi, hidden_lo = (sb(f"hidden_{part}", [P, FC, TS], F32R) for part in ("hi", "lo"))
            up_hi, up_lo = ([sb(f"up_{part}{n}", [P, KC, F], F32R) for n in range(2)] for part in ("hi", "lo"))
            down_hi, down_lo = ([sb(f"down_{part}{n}", [P, FC, D], F32R) for n in range(2)] for part in ("hi", "lo"))
        weight = [sb(f"weight{n}", [P, TT]) for n in range(2)]
        token = [sb(f"token{n}", [P, TT], U32) for n in range(2)]
        y_biased = [sb(f"y_biased{n}", [P, TT, D]) for n in range(2)]
        y = [sb(f"y{n}", [P, TT, D]) for n in range(2)]

        def bank(name):
            return ctx.enter_context(nc.psum_tensor(tag + name, [P, 512], F32))

        turned = bank("turned")
        h_bank = [bank(f"h{n}") for n in range(N_BANKS)]
        y_bank = bank("y_bank")

        bias_loaded, w_loaded = routed.bias_loaded, routed.w_loaded
        pads_sent = keep.pads_sent[layer]
        xs_loaded = [sem(f"xs_loaded{n}") for n in range(2)]
        xs_turned = sem("xs_turned")
        xs_t_ready = sem("xs_t_ready")
        up_done = sem("up_done")
        hidden_ready = sem("hidden_ready")
        y_done = sem("y_done")
        bias_added = sem("bias_added")
        y_ready = sem("y_ready")
        meta_ready = sem("meta_ready")
        if split:
            xs_hi_done = sem("xs_hi_done")
            hidden_hi_done = sem("hidden_hi_done")
            hidden_cut = sem("hidden_cut")
            w_hi_done = sem("w_hi_done")
            w_cut = [sem(f"w_cut{n}") for n in range(2)]
        y_sent = keep.y_sent[layer]
        SENT = 16 * TT

        FIRST, LAST, HEAD, TAIL = 0, tiles - 1, 2, 0
        AHEAD = tiles + 2
        block = ctx.enter_context(nc.Block())

        def expert_of(eng, t):
            return eng.value_load(routed.tile_expert[0:1, bass.ds(t + 1, 1)], min_val=0, max_val=E - 1)

        def group_of(eng, t):
            return eng.value_load(routed.tile_group[0:1, bass.ds(t + 1, 1)], min_val=0, max_val=E + AHEAD)

        def at_next_expert(eng, t, do):
            e, before = expert_of(eng, t), expert_of(eng, t - 1)
            with eng.If(e > before):
                with eng.If(e < E - 1):
                    nxt = nc.s_assert_within(e + 1, 1, E - 1, skip_runtime_bounds_check_because="e < E - 1 here")
                    with eng.If(nxt % 2 == 0):
                        do(nxt, 0)
                    with eng.Else():
                        do(nxt, 1)

        def cut_weights_hi(dve, e, n):
            dve.wait_ge(w_loaded[n], (e // 2 + 1) * 32)
            nc.vector.tensor_copy(up_hi[n][:], up[n][:])
            nc.vector.tensor_copy(down_hi[n][:], down[n][:]).then_inc(w_hi_done, 1)

        def cut_weights_lo(eng, ops, e, n):
            eng.wait_ge(w_hi_done, e + 1)
            ops.tensor_tensor(up_lo[n][:], up[n][:], up_hi[n][:].bitcast(F32), ALU.subtract).then_inc(w_cut[n], 1)
            ops.tensor_tensor(down_lo[n][:], down[n][:], down_hi[n][:].bitcast(F32), ALU.subtract).then_inc(w_cut[n], 1)

        def used_tiles(eng):
            return eng.value_load(routed.used_tiles[0:1, 0:1], min_val=2 * tokens // TS, max_val=tiles)

        def used_pairs(used):
            return (used + 1) // 2

        @block.sync
        def _(sp):
            def load_rows(t, n):
                if isinstance(t, int) and t < 4:
                    with sp.If(group_of(sp, t + 1) > group_of(sp, t)):
                        sp.wait_ge(pads_sent, 16 * E * TT)
                else:
                    sp.wait_ge(pads_sent, 16 * E * TT)
                row = sp.value_load(routed.tile_row[0:1, bass.ds(t, 1)], min_val=0, max_val=routed_rows(tokens) - TS)
                sp.dma_start(xs_rows[n][:], xs[bass.ds(row, TS), :].rearrange("(c p) w -> p c w", p=P)).then_inc(xs_loaded[n], 16)

            load_rows(0, 0)
            load_rows(1, 1)

            def step(i):
                t = i.at(0)
                if not (isinstance(t, int) and t == 0):
                    def load(e, n):
                        sp.wait_ge(y_done, t)
                        routed.load_weights(sp, up_w, down_w, e, n)

                    at_next_expert(sp, t, load)
                if i.has(2):
                    sp.wait_ge(meta_ready, t + 1)
                    sp.wait_ge(xs_turned, t + 1)
                    load_rows(i.at(2), i.par(0))

            used = used_tiles(sp)
            pipeline(sp, step, AHEAD, FIRST, LAST, HEAD, TAIL, while_below=used)

        @block.gpsimd
        def _(pool):
            for e in range(E):
                for c in range(TT):
                    pool.indirect_dma_start(out=xs, out_offset=bass.IndirectOffsetOnAxis(ap=routed.pad_slot[:, e, c:c + 1], axis=0),
                                            in_=routed.pad_rows[:, c, :], in_offset=None).then_inc(pads_sent, 16)

            if split:
                cut_weights_lo(pool, nc.gpsimd, 1, 1)

            def step(i):
                t, p = i.at(0), i.par(0)
                group, before = group_of(pool, t), group_of(pool, t - 1)
                with pool.If(group > before):
                    need(pool, y_sent[1 - p], i.half(1) * SENT)
                    pool.wait_ge(y_ready, t + 1)
                with pool.Else():
                    pool.wait_ge(y_ready, t + 1)
                for c in range(TT):
                    pool.indirect_dma_start(out=x_acc, out_offset=bass.IndirectOffsetOnAxis(ap=token[p][:, c:c + 1], axis=0),
                                            in_=y[p][:, c, :], in_offset=None, compute_op=ALU.add).then_inc(y_sent[p], 16)
                if split and not (isinstance(t, int) and t == 0):
                    at_next_expert(pool, t, lambda e, n: cut_weights_lo(pool, nc.gpsimd, e, n))

            used = used_tiles(pool)
            pipeline(pool, step, AHEAD, FIRST, LAST, HEAD, TAIL, while_below=used)
            for n in range(2):
                pool.wait_ge(xs_loaded[n], (used_pairs(used) + 1) * 16)
                pool.wait_ge(y_sent[n], used_pairs(used) * SENT)

        @block.vector
        def _(dve):
            def turn_out(t, n):
                dve.wait_ge(xs_turned, t + 1)
                src = turned[:, 0:KC * TS]
                if split:
                    hi, lo = (parts[n][:].rearrange("p k s -> p (k s)") for parts in (xs_hi, xs_lo))
                    nc.vector.tensor_copy(hi, src).then_inc(xs_hi_done, 1)
                    dve.wait_ge(xs_hi_done, t + 1)
                    nc.vector.tensor_tensor(lo, src, hi.bitcast(F32), ALU.subtract).then_inc(xs_t_ready, 1)
                else:
                    nc.vector.tensor_copy(xs_t[n][:].rearrange("p k s -> p (k s)"), src).then_inc(xs_t_ready, 1)

            def cut_hidden(t):
                for g in range(N_BANKS):
                    dve.wait_ge(hidden_ready, FC * t + (g + 1) * PER_BANK)
                    src, hi, lo = (x[:, g * PER_BANK:(g + 1) * PER_BANK, :] for x in (hidden, hidden_hi, hidden_lo))
                    nc.vector.tensor_copy(hi, src).then_inc(hidden_hi_done, 1)
                    dve.wait_ge(hidden_hi_done, N_BANKS * t + g + 1)
                    nc.vector.tensor_tensor(lo, src, hi.bitcast(F32), ALU.subtract).then_inc(hidden_cut, 1)

            if split:
                cut_weights_hi(dve, 0, 0)
                cut_weights_lo(dve, nc.vector, 0, 0)
            turn_out(0, 0)
            if split:
                cut_weights_hi(dve, 1, 1)
            dve.wait_ge(bias_loaded, 16)

            def step(i):
                t, p = i.at(0), i.par(0)
                e = expert_of(dve, t)
                if split:
                    cut_hidden(t)
                if i.has(1):
                    turn_out(i.at(1), i.par(1))
                dve.wait_ge(xs_loaded[p], 16 * (i.half(0) + 1))
                need(dve, y_sent[p], i.half(0) * SENT)
                nc.vector.tensor_copy(weight[p][:], xs_rows[p][:, :, D])
                nc.vector.tensor_copy(token[p][:], xs_rows[p][:, :, D + 1]).then_inc(meta_ready, 1)
                dve.wait_ge(y_done, t + 1)
                nc.vector.tensor_tensor(y_biased[p][:], y_bank[:].rearrange("p (c d) -> p c d", c=TT),
                                        down_bias[:, bass.ds(e, 1), :].to_broadcast((P, TT, D)), ALU.add).then_inc(bias_added, 1)
                dve.wait_ge(bias_added, t + 1)
                dve.wait_ge(meta_ready, t + 1)
                for c in range(TT):
                    last = nc.vector.tensor_scalar(y[p][:, c, :], y_biased[p][:, c, :], weight[p][:, c:c + 1], None, ALU.mult)
                last.then_inc(y_ready, 1)
                if split and not (isinstance(t, int) and t == 0):
                    at_next_expert(dve, t, lambda e, n: cut_weights_hi(dve, e, n))

            used = used_tiles(dve)
            pipeline(dve, step, AHEAD, FIRST, LAST, HEAD, TAIL, while_below=used)

        @block.scalar
        def _(act):
            def step(i):
                t = i.at(0)
                e = expert_of(act, t)
                for fc in range(FC):
                    if fc % PER_BANK == 0:
                        act.wait_ge(up_done, N_BANKS * t + fc // PER_BANK + 1)
                    g, at = fc // PER_BANK, fc % PER_BANK * TS
                    nc.scalar.activation(hidden[:, fc, :], h_bank[g][:, at:at + TS], act_func,
                                         bias=routed.up_bias[:, bass.ds(e * FC + fc, 1)]).then_inc(hidden_ready, 1)

            used = used_tiles(act)
            pipeline(act, step, AHEAD, FIRST, LAST, HEAD, TAIL, while_below=used)

        @block.tensor
        def _(pe):
            def turn(t, n, half):
                pe.wait_ge(xs_loaded[n], 16 * (half + 1))
                for kc in range(KC):
                    for c in range(TT):
                        last = nc.tensor.transpose(turned[:, kc * TS + c * P:kc * TS + c * P + P], xs_rows[n][:, c, kc * P:(kc + 1) * P], keep.ident[:])
                last.then_inc(xs_turned, 1)

            turn(0, 0, 0)

            def step(i):
                t, p = i.at(0), i.par(0)
                e = expert_of(pe, t)

                def through(n):
                    if split:
                        pe.wait_ge(w_cut[n], (e // 2 + 1) * 2)
                        up_terms = ((up_hi[n], xs_hi[p]), (up_hi[n], xs_lo[p]), (up_lo[n], xs_hi[p]))
                        down_terms = ((hidden_hi, down_hi[n]), (hidden_lo, down_hi[n]), (hidden_hi, down_lo[n]))
                    else:
                        pe.wait_ge(w_loaded[n], (e // 2 + 1) * 32)
                        up_terms, down_terms = ((up[n], xs_t[p]),), ((hidden, down[n]),)
                    pe.wait_ge(xs_t_ready, t + 1)
                    for fc in range(FC):
                        g, at = fc // PER_BANK, fc % PER_BANK * TS
                        for kc in range(KC):
                            for term, (w, x) in enumerate(up_terms):
                                last = nc.tensor.matmul(h_bank[g][:, at:at + TS], w[:, kc, fc * P:(fc + 1) * P], x[:, kc, :],
                                                        start=(kc == 0 and term == 0), stop=(kc == KC - 1 and term == len(up_terms) - 1))
                        if fc % PER_BANK == PER_BANK - 1:
                            last.then_inc(up_done, 1)
                    if i.has(1):
                        turn(i.at(1), i.par(1), i.half(1))
                    for c in range(TT):
                        for fc in range(FC):
                            if c == 0 and not split:
                                pe.wait_ge(hidden_ready, FC * t + fc + 1)
                            if c == 0 and split and fc % PER_BANK == 0:
                                pe.wait_ge(hidden_cut, N_BANKS * t + fc // PER_BANK + 1)
                            if c == 0 and fc == 0:
                                need(pe, bias_added, t)
                            for term, (x, w) in enumerate(down_terms):
                                last = nc.tensor.matmul(y_bank[:, c * D:(c + 1) * D], x[:, fc, c * P:(c + 1) * P], w[:, fc, :],
                                                        start=(fc == 0 and term == 0), stop=(fc == FC - 1 and term == len(down_terms) - 1))
                    last.then_inc(y_done, 1)

                with pe.If(e % 2 == 0):
                    through(0)
                with pe.Else():
                    through(1)

            used = used_tiles(pe)
            pipeline(pe, step, AHEAD, FIRST, LAST, HEAD, TAIL, while_below=used)

    clear_semaphores(nc, all_sems + routed.all_sems)


def gated_flamingo(nc, p, out):
    x, ctx_in, lens = p["x"], p["ctx_1024"], p["mask_B_ik0"]
    B, S, D = x.shape
    tokens = B * S
    F0 = p["L0_ffn_up_w"].shape[2]
    F1 = p["L1_ffn_W1"].shape[2]
    scratch = [nc.dram_tensor(f"parts_dram{n}", (2 * D // P, 3, P, S), BF16, kind="Internal").ap() for n in range(2)]
    xs = nc.dram_tensor("routed_rows_dram", (routed_rows(tokens), ROW), F32, kind="Internal").ap()
    x_mid = nc.dram_tensor("x_mid_dram", (tokens + TS, D), F32, kind="Internal").ap()

    with ExitStack() as ctx:
        keep = Resident(nc, ctx, tokens, D)
        setup_phase(nc, keep, p["g_xattn"], p["g_ffn"])

        attention_phase(nc, keep, 0, x, ctx_in, None, [p[f"L0_xattn_{w}"] for w in ("Wq", "Wk", "Wv", "Wo")],
                        [p["L0_xattn_bv"], p["L0_xattn_bo"]], scratch)
        with ExitStack() as tables:
            up_w, up_b, down_w, down_b = (p[f"L0_ffn_{w}"] for w in ("up_w", "up_b", "down_w", "down_b"))
            routed = Routed(nc, tables, 0, tokens, D, F0)
            route_phase(nc, keep, routed, 0, F0, up_w, up_b, down_w, down_b, [p["L0_ffn_gate_w"]],
                        [p[f"L0_ffn_sh_{w}"] for w in ("up_w", "up_b", "down_w", "down_b")], xs, x_mid)
            expert_phase(nc, keep, routed, 0, F0, ACT.Silu, up_w, down_w, xs, x_mid)

        attention_phase(nc, keep, 1, x_mid[0:tokens, :].rearrange("(b s) d -> b s d", s=S), ctx_in, lens,
                        [p[f"L1_xattn_{w}"] for w in ("W_q", "W_k", "W_v", "W_o")], None, scratch)
        with ExitStack() as tables:
            up_w, up_b, down_w, down_b = (p[f"L1_ffn_{w}"] for w in ("W1", "b1", "W2", "b2"))
            routed = Routed(nc, tables, 1, tokens, D, F1)
            route_phase(nc, keep, routed, 1, F1, up_w, up_b, down_w, down_b,
                        [p["L1_ffn_Wp"], p["L1_ffn_sim_matrix"], p["L1_ffn_temperature"]], None, xs, out)
            expert_phase(nc, keep, routed, 1, F1, ACT.Gelu, up_w, down_w, xs, out)


INPUTS = (["x", "ctx_1024", "mask_B_ik0", "g_xattn", "g_ffn"]
          + [f"L0_xattn_{n}" for n in ("Wq", "Wk", "Wv", "bv", "Wo", "bo")]
          + [f"L0_ffn_{n}" for n in ("gate_w", "up_w", "up_b", "down_w", "down_b", "sh_up_w", "sh_up_b", "sh_down_w", "sh_down_b")]
          + [f"L1_xattn_{n}" for n in ("W_q", "W_k", "W_v", "W_o")]
          + [f"L1_ffn_{n}" for n in ("Wp", "sim_matrix", "temperature", "W1", "b1", "W2", "b2")])


def kernel(**inputs):
    import numpy as _np
    import concourse.bacc as _bacc
    from concourse.bass_utils import run_bass_kernel_spmd as _run

    nc = _bacc.Bacc("TRN2", target_bir_lowering=False, num_devices=1)
    arrays, params = {}, {}
    for name in INPUTS:
        a = _np.ascontiguousarray(inputs[name])
        a = a.reshape(a.shape or (1,))
        arrays[f"in_{name}"] = a
        params[name] = nc.dram_tensor(f"in_{name}", a.shape, mybir.dt.from_np(a.dtype), kind="ExternalInput").ap()
    B, S, D = inputs["x"].shape
    out = nc.dram_tensor("out_rows", (B * S + TS, D), F32, kind="ExternalOutput").ap()
    gated_flamingo(nc, params, out)
    r = _run(nc, [arrays], core_ids=[0])
    return _np.asarray(r.results[0]["out_rows"])[:B * S].reshape(B, S, D)
```
